# Optimizing a Trainium2 kernel written in Bass

```python
import numpy as np
import jax
import jax.numpy as jnp

def _softmax(x, axis=-1):
    return jax.nn.softmax(x, axis=axis)

def _gelu(x):
    return jax.nn.gelu(x, approximate=True)

def _silu(x):
    return jax.nn.silu(x)

def _sigmoid(x):
    return jax.nn.sigmoid(x)

def _layernorm(x, axis=-1, eps=1e-05):
    m = jnp.mean(x, axis=axis, keepdims=True)
    v = jnp.var(x, axis=axis, keepdims=True)
    return (x - m) / jnp.sqrt(v + eps)

def _scatter_add(tgt, idx, src, axis=0):
    return tgt.at[idx].add(src)

def _segment_sum(src, seg, n):
    return jax.ops.segment_sum(src, seg, n)
kernel_name = 'mk_gps_d1_gnn_r32_bf8bf8'

def setup_inputs(seed: int=0):
    np.random.seed(seed)
    _w = jnp.asarray

    def _rec_inputs():
        import jax
        import jax.numpy as jnp
        _gk = jax.random.key(seed)
        x = -0.0001126 + 1 * jax.random.normal(jax.random.fold_in(_gk, 1), (3125, 256), jnp.float32)
        src = jax.random.randint(jax.random.fold_in(_gk, 2), (50000,), 0, 3125, jnp.int32)
        dst = jax.random.randint(jax.random.fold_in(_gk, 3), (50000,), 0, 3125, jnp.int32)
        _o = jnp.argsort(dst, stable=True)
        src = src[_o]
        dst = dst[_o]
        edge_type_8 = jax.random.randint(jax.random.fold_in(_gk, 12), (50000,), 0, 8, jnp.int32)
        return (x, src, dst, edge_type_8)
    x, src, dst, edge_type_8 = _rec_inputs()

    def _L0_gnn_setup():
        import jax, jax.numpy as jnp
        import numpy as np
        N, E, R, H, D = (30000, 9375, 8, 8, 32)
        IN_F = 256
        NEG_SLOPE = 0.2
        key = jax.random.key(seed)
        k = jax.random.split(key, 6)
        x = jax.random.normal(k[0], (N, IN_F), dtype=jnp.float32)
        W = jax.random.normal(k[1], (R, H * D, IN_F), dtype=jnp.float32) * 0.05
        attn_src = jax.random.normal(k[2], (H, D), dtype=jnp.float32) * 0.1
        attn_dst = jax.random.normal(k[3], (H, D), dtype=jnp.float32) * 0.1
        edge_index = jax.random.randint(k[4], (2, E), 0, N, dtype=jnp.int64) if jax.config.read('jax_enable_x64') else jax.random.randint(k[4], (2, E), 0, N, dtype=jnp.int32)
        edge_type = jax.random.randint(k[5], (E,), 0, R, dtype=edge_index.dtype)
        return dict(x=x, W=W, attn_src=attn_src, attn_dst=attn_dst, edge_index=edge_index, edge_type=edge_type)
    _L0_gnn_all = _L0_gnn_setup()
    _L0_gnn_in = {k: v for k, v in _L0_gnn_all.items() if k in ('W', 'attn_src', 'attn_dst')}
    del _L0_gnn_all

    def _L0_mix_setup():
        import jax, jax.numpy as jnp
        import numpy as np
        NUM_HEADS = 8
        key = jax.random.key(seed)
        ks = jax.random.split(key, 5)
        B, N, C = (8, 512, 256)
        x = jax.random.normal(ks[0], (B, N, C), dtype=jnp.float32)
        Wq = jax.random.normal(ks[1], (C, C), dtype=jnp.float32) * 0.02
        Wkv = jax.random.normal(ks[2], (2 * C, C), dtype=jnp.float32) * 0.02
        Wproj = jax.random.normal(ks[3], (C, C), dtype=jnp.float32) * 0.02
        bproj = jnp.zeros((C,), dtype=jnp.float32)
        return {'x': x, 'Wq': Wq, 'Wkv': Wkv, 'Wproj': Wproj, 'bproj': bproj}
    _L0_mix_all = _L0_mix_setup()
    _L0_mix_in = {k: v for k, v in _L0_mix_all.items() if k in ('Wq', 'Wkv', 'Wproj', 'bproj')}
    del _L0_mix_all

    def _L0_ffn_setup():
        import jax, jax.numpy as jnp
        import numpy as np
        TOP_K = 2
        LN_EPS = 1e-05
        key = jax.random.key(seed)
        ks = jax.random.split(key, 8)
        B, S, D, E, H = (16, 1024, 256, 8, 1024)
        x = jax.random.normal(ks[0], (B, S, D), dtype=jnp.float32)
        Wr = jax.random.normal(ks[1], (D, E), dtype=jnp.float32) * 0.1
        br = jnp.zeros((E,), dtype=jnp.float32)
        ln_g = jnp.ones((E, D), dtype=jnp.float32)
        ln_b = jnp.zeros((E, D), dtype=jnp.float32)
        W1 = jax.random.normal(ks[2], (E, D, H), dtype=jnp.float32) * (1.0 / np.sqrt(D))
        b1 = jnp.zeros((E, H), dtype=jnp.float32)
        W2 = jax.random.normal(ks[3], (E, H, D), dtype=jnp.float32) * (1.0 / np.sqrt(H))
        b2 = jnp.zeros((E, D), dtype=jnp.float32)
        return {'x': x, 'Wr': Wr, 'br': br, 'ln_g': ln_g, 'ln_b': ln_b, 'W1': W1, 'b1': b1, 'W2': W2, 'b2': b2}
    _L0_ffn_all = _L0_ffn_setup()
    _L0_ffn_in = {k: v for k, v in _L0_ffn_all.items() if k in ('Wr', 'br', 'ln_g', 'ln_b', 'W1', 'b1', 'W2', 'b2')}
    del _L0_ffn_all
    return {'x': x, 'src': src, 'dst': dst, 'edge_type_8': edge_type_8, 'L0_gnn_W': _L0_gnn_in['W'], 'L0_gnn_attn_src': _L0_gnn_in['attn_src'], 'L0_gnn_attn_dst': _L0_gnn_in['attn_dst'], 'L0_mix_Wq': _L0_mix_in['Wq'], 'L0_mix_Wkv': _L0_mix_in['Wkv'], 'L0_mix_Wproj': _L0_mix_in['Wproj'], 'L0_mix_bproj': _L0_mix_in['bproj'], 'L0_ffn_Wr': _L0_ffn_in['Wr'], 'L0_ffn_br': _L0_ffn_in['br'], 'L0_ffn_ln_g': _L0_ffn_in['ln_g'], 'L0_ffn_ln_b': _L0_ffn_in['ln_b'], 'L0_ffn_W1': _L0_ffn_in['W1'], 'L0_ffn_b1': _L0_ffn_in['b1'], 'L0_ffn_W2': _L0_ffn_in['W2'], 'L0_ffn_b2': _L0_ffn_in['b2']}

def reference(x, src, dst, edge_type_8, L0_gnn_W, L0_gnn_attn_src, L0_gnn_attn_dst, L0_mix_Wq, L0_mix_Wkv, L0_mix_Wproj, L0_mix_bproj, L0_ffn_Wr, L0_ffn_br, L0_ffn_ln_g, L0_ffn_ln_b, L0_ffn_W1, L0_ffn_b1, L0_ffn_W2, L0_ffn_b2):
    import jax
    import jax.numpy as jnp

    def _L0_gnn_ref(x, W, attn_src, attn_dst, edge_index, edge_type):
        import jax, jax.numpy as jnp
        import numpy as np
        N, E, R, H, D = (30000, 9375, 8, 8, 32)
        IN_F = 256
        NEG_SLOPE = 0.2
        n = x.shape[0]
        r = W.shape[0]
        h, d = attn_src.shape
        h_all = jnp.einsum('nf,rof->rno', x, W).reshape(r, n, h, d)
        src, dst = (edge_index[0], edge_index[1])
        h_src = h_all[edge_type, src]
        h_dst = h_all[edge_type, dst]
        scores = jnp.einsum('ehd,hd->eh', h_src, attn_src) + jnp.einsum('ehd,hd->eh', h_dst, attn_dst)
        scores = jnp.where(scores > 0, scores, NEG_SLOPE * scores)
        amax = jnp.maximum(jax.ops.segment_max(scores, dst, num_segments=n), 0.0)
        w = jnp.exp(scores - amax[dst])
        denom = jax.ops.segment_sum(w, dst, num_segments=n) + 1e-12
        w = w / denom[dst]
        msg = h_src * w[..., None]
        out = jax.ops.segment_sum(msg, dst, num_segments=n)
        return out.reshape(n, h * d)

    def _L0_mix_ref(x, Wq, Wkv, Wproj, bproj):
        import jax, jax.numpy as jnp
        import numpy as np
        NUM_HEADS = 8
        B, N, C = x.shape
        h = NUM_HEADS
        d = C // h
        q = jnp.einsum('bnc,oc->bno', x, Wq).reshape(B, N, h, d).transpose(0, 2, 1, 3)
        kv = jnp.einsum('bnc,oc->bno', x, Wkv).reshape(B, N, 2, h, d)
        k = kv[:, :, 0].transpose(0, 2, 1, 3)
        v = kv[:, :, 1].transpose(0, 2, 1, 3)
        q = jax.nn.elu(q) + 1.0
        k = jax.nn.elu(k) + 1.0
        k_sum = k.sum(axis=2)
        D_inv = 1.0 / jnp.maximum(jnp.einsum('bhnd,bhd->bhn', q, k_sum), 1e-06)
        context = jnp.einsum('bhnd,bhne->bhde', k, v)
        attn = jnp.einsum('bhnd,bhde->bhne', q, context) * D_inv[..., None]
        out = attn.transpose(0, 2, 1, 3).reshape(B, N, C)
        out = jnp.einsum('bnc,oc->bno', out, Wproj) + bproj
        return out

    def _L0_ffn_ref(x, Wr, br, ln_g, ln_b, W1, b1, W2, b2):
        import jax, jax.numpy as jnp
        import numpy as np
        TOP_K = 2
        LN_EPS = 1e-05
        B, S, D = x.shape
        N = B * S
        xt = x.reshape(N, D)
        logits = xt @ Wr + br
        probs = jax.nn.softmax(logits, axis=-1)
        top_p, top_idx = jax.lax.top_k(probs, TOP_K)
        weights = top_p / top_p.sum(axis=-1, keepdims=True)
        mu = xt.mean(axis=-1, keepdims=True)
        var = ((xt - mu) ** 2).mean(axis=-1, keepdims=True)
        xn = (xt - mu) * jax.lax.rsqrt(var + LN_EPS)
        xe = xn[None, :, :] * ln_g[:, None, :] + ln_b[:, None, :]
        h = jax.nn.gelu(jnp.einsum('end,edh->enh', xe, W1) + b1[:, None, :], approximate=False)
        y = jnp.einsum('enh,ehd->end', h, W2) + b2[:, None, :]
        y_tok = jnp.transpose(y, (1, 0, 2))
        sel = jnp.take_along_axis(y_tok, top_idx[:, :, None], axis=1)
        out = (weights[:, :, None] * sel).sum(axis=1)
        return out.reshape(B, S, D)
    edge_index = jnp.stack([src, dst])
    xn = _layernorm(x, axis=-1)
    x = x + _L0_gnn_ref(xn, L0_gnn_W, L0_gnn_attn_src, L0_gnn_attn_dst, edge_index, edge_type_8) + _L0_mix_ref(xn[None], L0_mix_Wq, L0_mix_Wkv, L0_mix_Wproj, L0_mix_bproj)[0]
    x = x + _L0_ffn_ref(_layernorm(x, axis=-1)[None], L0_ffn_Wr, L0_ffn_br, L0_ffn_ln_g, L0_ffn_ln_b, L0_ffn_W1, L0_ffn_b1, L0_ffn_W2, L0_ffn_b2)[0]
    return x

_drawn_inputs = setup_inputs


def setup_inputs(seed=0):
    import zlib

    import numpy as np

    out = dict(_drawn_inputs(seed))
    spreads = {'L0_mix_bproj': (0.0, 0.1),
     'L0_ffn_br': (0.0, 0.1),
     'L0_ffn_ln_g': (1.0, 0.2),
     'L0_ffn_ln_b': (0.0, 0.1),
     'L0_ffn_b1': (0.0, 0.1),
     'L0_ffn_b2': (0.0, 0.1)}
    factors = {'L0_mix_Wq': 8.0, 'L0_mix_Wkv': 4.472, 'L0_mix_Wproj': 4.202}
    for name, (base, spread) in spreads.items():
        noise = np.random.default_rng([zlib.crc32(name.encode()), seed]).standard_normal(out[name].shape)
        drawn = base * np.exp(spread * noise) if base else spread * noise
        out[name] = jnp.asarray(drawn.astype(out[name].dtype))
    for name, factor in factors.items():
        out[name] = (out[name] * factor).astype(out[name].dtype)
    return out
```

```python
from contextlib import ExitStack

import numpy as np

import concourse.bass as bass
from concourse import mybir

F32 = mybir.dt.float32
BF16 = mybir.dt.bfloat16
I32 = mybir.dt.int32
U32 = mybir.dt.uint32
ALU = mybir.AluOpType
ACT = mybir.ActivationFunctionType
AX = mybir.AxisListType.X
ENG = mybir.EngineType

P = 128
N, E, D = 3125, 50000, 256
R, H, DH = 8, 8, 32
X, F, TOPK = 8, 1024, 2
KC = D // P
NT = -(-N // P)
NP = NT * P
LASTN = N - (NT - 1) * P
TE = -(-E // P)
LASTE = E - (TE - 1) * P
TC = -(-TE // P)
CH = P // H
G = 16
IT = -(-(TE - 1 + NT) // G) * G
NG = IT // G
J = IT // CH
L = J * P
XR = NP + P
FT = (N * TOPK - X) // P + X
FT += FT % 2
XW = D + 4
FC = F // P
LN_EPS = 1e-5
assert IT % CH == 0 and NG % 2 == 0 and NT % 2 == 1 and FT % 2 == 0

WORDS = 51200


class Chain:

    def __init__(self, eng, sem):
        self.eng, self.sem, self.base, self.k, self.per = eng, sem, 0, 0, 0

    def __call__(self, ins):
        self.k += 1
        ins.then_inc(self.sem, 1)
        return ins

    def settle(self, back=0):
        self.eng.wait_ge(self.sem, self.base + self.k - back)

    def enter(self, turn, per):
        if self.k and isinstance(self.base, int) and not self.per:
            self.base, self.k = self.base + self.k, 0
        self.start, self.per = self.base, per
        self.base, self.k = self.start + turn * per, 0

    def leave(self, turns):
        assert self.k == self.per, (self.k, self.per)
        self.base, self.k, self.per = self.start + turns * self.per, 0, 0


def gps_layer(nc, x, src, dst, etype, w_rel, w_rel_t, attn, wmix_t, wp_t, bproj,
              wr, br, ln_g, ln_b, w1, b1, w2, b2, out):
    s_tab = nc.dram_tensor("source_scores", [NP * R, H], F32, kind="Internal").ap()
    h_tab = nc.dram_tensor("node_rows", [NP * R, D], F32, kind="Internal").ap()
    w1_g = nc.dram_tensor("w1_scaled", [X, P, KC * F], F32, kind="Internal").ap()
    bias_d = nc.dram_tensor("expert_bias", [X, F], F32, kind="Internal").ap()
    x_rows = nc.dram_tensor("expert_rows", [X * XR + P, XW], F32, kind="Internal").ap()

    ctx = ExitStack()
    with ctx:
        def sb(name, shape, dt=F32):
            return ctx.enter_context(nc.sbuf_tensor(name, shape, dt))

        def sem(name):
            return ctx.enter_context(nc.semaphore(name))

        arena = sb("arena", [P, WORDS])

        def at(lo, *shape, dt=F32):
            n = int(np.prod(shape))
            view = arena[:, lo:lo + (n // 2 if dt == BF16 else n)]
            if dt != F32:
                view = view.bitcast(dt)
            names = "abcd"[:len(shape)]
            if len(shape) > 1:
                view = view.rearrange(f"p ({' '.join(names)}) -> p {' '.join(names)}",
                                      **dict(zip(names[1:], shape[1:])))
            return view

        A0 = NT * D
        ACC = A0 + X * KC * F
        QT = ACC + NT * D
        B0 = QT + KC * NP
        Z0 = ACC + X * FC * D
        x_sb = at(0, NT, D)
        acc = at(ACC, NT, D)
        qT = at(QT, KC, NP)
        xnT = at(A0, KC, NP)
        wrt_sb = at(A0 + 6400, KC, R * D)
        wmix_sb = at(A0 + 10496, KC, 3 * D)
        wp_sb = at(A0 + 12032, KC, D)
        ctxT = at(A0 + 12544, KC, P)
        xs_ring = at(A0 + 12800, 2, KC, P)
        b1_row = at(A0 + 13312, F)
        s_dtab = at(A0 + 14592, NT, R * H)
        wrel_sb = at(QT, R, KC, D)
        h_out = at(ACC, 2, R * D)
        kv_sb = at(ACC + 4096, 2, 2 * D)
        k_low = at(ACC + 5120, D)
        q_low = at(ACC + 5376, KC, P)
        q_high = at(ACC + 5632, KC, P)
        s_out = at(B0, NT, R * H)
        e_raw = at(B0 + 1600, 3, TC, P, dt=I32)
        e_f = at(B0 + 3136, 3, TC, P)
        spread = at(B0 + 4672, TC, IT)
        w1e = at(B0 + 1600, 2, KC, F)
        xn_ring = at(B0 + 6400, 2, D)
        lt = at(B0 + 6912, IT)
        cnt = at(B0 + 7328, NT)
        t_it = at(B0 + 7392, IT)
        stats = at(B0 + 7808, NT, 6)
        oh_a = at(A0, 2, G, P, dt=BF16)
        ohT = at(A0 + 2048, 2, G, P)
        tmp_s = at(A0 + 6144, G, R * H)
        rmask = at(A0 + 7168, IT, R)
        s_dst = at(A0 + 10496, IT, H)
        s_src = at(B0 + 10240, IT, H)
        sg = at(B0 + 13568, 2, G, H)
        typ = at(B0 + 13824, IT)
        m_sb = at(B0 + 14784, KC, D)
        kb_sb = at(B0 + 15296, KC, P)
        s_all = at(A0, H, CH, J)
        score = at(A0 + 3328, L)
        keep = at(A0 + 6656, L + 1)
        sc2 = at(A0 + 9992, L)
        sc1 = at(ACC, L)
        ring = at(B0, 2, G, D)
        oh_b = at(B0 + 8192, G, P)
        w_i = at(B0 + 10240, CH, J, H)
        xs = at(Z0, NT, XW)
        xs_pad = at(Z0 + NT * XW, XW)
        y_ring = at(Z0 + 26 * XW, 2, D)
        yT = at(Z0 + 26 * XW + 512, 2, KC, P)
        qr = at(Z0 + 26 * XW + 1280, 2, KC, P)
        q_inv = at(Z0 + 26 * XW + 1024, KC, P)
        Z1 = Z0 + 26 * XW + 1792
        rt = [at(Z1 + n * NT * X, NT * X) for n in range(9)]
        small = [at(Z1 + 9 * NT * X + n * NT, NT) for n in range(14)]
        w1_sb = at(A0, X, KC, F)
        w2_sb = at(ACC, X, FC, D)
        xg = at(Z0, 2, XW)
        xgT = at(Z0 + 520, 2, KC, P)
        bias_r = at(Z0 + 1032, 2, F + D)
        h_sb = at(Z0 + 3592, 2, F)
        hT = at(Z0 + 5640, 2, FC, P)
        y_out = at(Z0 + 7688, 2, D)
        assert Z1 + 9 * NT * X + 14 * NT <= B0 + 14784

        eye = sb("eye", [P, P + 2])
        ident, shift_up, shift_down = eye[:, 1:P + 1], eye[:, 0:P], eye[:, 2:P + 2]
        eye_b = sb("eye_b", [P, P], BF16)
        iota_r = sb("iota_r", [P, P])
        pcol = sb("pcol", [P, TC])
        ones = sb("ones", [P, P])
        idx_i = sb("idx_i", [P, IT], U32)
        idx_r = sb("idx_r", [P, 2, G], U32)
        dl = sb("dl", [P, IT])
        blk = sb("blk", [1, IT], I32)
        hmask = sb("hmask", [P, KC, H])
        wa_sb = at(B0 + 8192, KC, 2 * R * H)
        att_sb = at(B0 + 8448, KC, 2)
        ablock = at(B0 + 8464, KC, 2 * H)
        misc = at(B0 + 8512, 1024)
        ln_cols = at(B0 + 9536, 2, X, KC)
        bdm = at(B0 + 9600, P)
        zrow = at(B0 + 9728, 512)
        wr_sb = at(B0 + 15552, KC, X)
        br_sb = at(B0 + 15568, X)
        stx = sb("stx", [P, 4, NT])
        carry = sb("carry", [P, 4])
        ftab = sb("ftab", [1, 2 * FT + 8], I32)
        rows = at(B0 + 8192, 4, P + 1)
        psum = ctx.enter_context(nc.psum_tensor("psum", [P, 8, 512], F32))

        d_all = at(B0 + 10240, H, CH, J)
        tok_u = at(Z0 + 8200, 2).bitcast(U32)
        y_b2 = at(Z0 + 8204, D)
        slot_u = [m.bitcast(U32) for m in (small[11], small[12], small[13])]

        upper = at(Z0 + 26 * XW + 512, P)
        gt = at(Z0 + 26 * XW, FT, X - 1)
        stats_z = at(Z1 + 8 * NT * X, NT, 6)

        fill_done = sem("fill_done")
        in_edges, in_x, in_wrel, in_wt, in_misc = map(sem, ("in_edges", "in_x", "in_wrel", "in_wt", "in_misc"))
        pool_const = sem("pool_const")
        dve_step, act_step, pool_step = map(sem, ("dve_step", "act_step", "pool_step"))
        pool_turn = sem("pool_turn")
        dve_to_pe, pe_to_dve = sem("dve_to_pe"), sem("pe_to_dve")
        dve_to_act, act_to_dve = sem("dve_to_act"), sem("act_to_dve")
        pe_to_act, act_to_pe = sem("pe_to_act"), sem("act_to_pe")
        items_ready = sem("items_ready")
        xn_made = sem("xn_made")
        xt_made, xt_copied = sem("xt_made"), sem("xt_copied")
        stab_made, stab_copied = sem("stab_made"), sem("stab_copied")
        stab_stored = sem("stab_stored")
        xs_made = sem("xs_made")
        kv_made, kv_read, kv_ready, ctx_added = map(sem, ("kv_made", "kv_read", "kv_ready", "ctx_added"))
        q_made, q_read = sem("q_made"), sem("q_read")
        low_ready, exp_ready = sem("low_ready"), sem("exp_ready")
        h_made, h_copied = sem("h_made"), sem("h_copied")
        h_stored = [sem("h_stored0"), sem("h_stored1")]
        w1_in, w1_out = [sem("w1_in0"), sem("w1_in1")], [sem("w1_out0"), sem("w1_out1")]
        b1_in, b1_out, w1_scaled = sem("b1_in"), sem("b1_out"), sem("w1_scaled")
        w1_used, b1_added = sem("w1_used"), sem("b1_added")
        tr_made, tr_copied = sem("tr_made"), sem("tr_copied")
        sg_in = [sem("sg_in0"), sem("sg_in1")]
        s_src_ready = sem("s_src_ready")
        oha_made, oha_used, ohT_made, spread_made, spread_used = map(
            sem, ("oha_made", "oha_used", "ohT_made", "spread_made", "spread_used"))
        rows_in = [sem("rows_in0"), sem("rows_in1")]
        ohb_made, msg_made, sum_made, sum_added = map(sem, ("ohb_made", "msg_made", "sum_made", "sum_added"))
        w1_loaded, w2_loaded = sem("w1_loaded"), sem("w2_loaded")
        qr_made, mix_made, x1_made, yr_made, yr_used, yT_made, yT_copied, xs_copied = map(
            sem, ("qr_made", "mix_made", "x1_made", "yr_made", "yr_used", "yT_made", "yT_copied", "xs_copied"))
        den_made, q_copied = sem("den_made"), sem("q_copied")
        out_init = sem("out_init")
        send_ready, sent = sem("send_ready"), sem("sent")
        acc_free = sem("acc_free")
        xg_in = [sem("xg_in0"), sem("xg_in1")]
        tile_done = sem("tile_done")
        xgT_made, xgT_copied, f1_made, h_pre, h_act, hT_made, hT_copied, f2_made = map(
            sem, ("xgT_made", "xgT_copied", "f1_made", "h_pre", "h_act", "hT_made", "hT_copied", "f2_made"))
        y_free = sem("y_free")
        y_added = [sem("y_added0"), sem("y_added1")]

        def load_values(eng, row, hi):
            return nc.values_load_multi_w_load_instructions(
                row, engines=[eng], min_val=0, max_val=hi,
                skip_runtime_bounds_check_because="the program works these out itself, in range for any input",
            )[1]

        def pairs(eng, n, body):
            with eng.Fori(0, n // 2) as turn:
                body(2 * turn, 0)
                body(2 * turn + 1, 1)
            if n % 2:
                body(n - 1, 0)

        block = ctx.enter_context(nc.Block())

        @block.sync
        def _(sp):
            sp.wait_ge(fill_done, 1)
            full = (TE - 1) // P
            for n, a in enumerate((dst, src, etype)):
                sp.dma_start(e_raw[:, n, 0:full, :], a[0:full * P * P].rearrange("(c t e) -> t c e", t=P, e=P)).then_inc(in_edges, 16)
                rest = TE - 1 - full * P
                sp.dma_start(e_raw[0:rest, n, full, :], a[full * P * P:(TE - 1) * P].rearrange("(t e) -> t e", e=P)).then_inc(in_edges, 16)
                sp.dma_start(e_raw[rest:rest + 1, n, full, 0:LASTE], a[(TE - 1) * P:E].rearrange("(t e) -> t e", t=1)).then_inc(in_edges, 16)
            sp.dma_start(x_sb[:, 0:NT - 1, :], x[0:(NT - 1) * P, :].rearrange("(j p) d -> p j d", p=P)).then_inc(in_x, 16)
            sp.dma_start(x_sb[0:LASTN, NT - 1, :], x[(NT - 1) * P:N, :]).then_inc(in_x, 16)
            sp.dma_start(wrel_sb, w_rel).then_inc(in_wrel, 16)
            sp.dma_start(att_sb, attn).then_inc(in_wrel, 16)
            sp.dma_start(wrt_sb, w_rel_t).then_inc(in_wt, 16)
            sp.dma_start(wmix_sb, wmix_t).then_inc(in_wt, 16)
            sp.dma_start(wp_sb, wp_t).then_inc(in_wt, 16)
            sp.dma_start(ln_cols[:, 0], ln_g).then_inc(in_misc, 16)
            sp.dma_start(ln_cols[:, 1], ln_b).then_inc(in_misc, 16)
            sp.dma_start(wr_sb, wr).then_inc(in_misc, 16)
            sp.dma_start(br_sb, br.broadcast_to([P, X])).then_inc(in_misc, 16)
            sp.dma_start(misc[:, 0:D], bproj.broadcast_to([P, D])).then_inc(in_misc, 16)
            sp.wait_ge(stab_copied, NT + 2)
            sp.dma_start(s_tab.rearrange("(j p r) h -> p j (r h)", p=P, r=R), s_out).then_inc(stab_stored, 16)

            def load_w1(e):
                sp.dma_start(w1e[:, e % 2], w1[e].rearrange("p (c f) -> p c f", c=KC)).then_inc(w1_in[e % 2], 16)
            sp.wait_ge(items_ready, 1)
            load_w1(0)
            load_w1(1)
            h_view = h_tab.rearrange("(j p r) d -> j p (r d)", p=P, r=R)

            def store_rows(j, par):
                sp.wait_ge(h_copied, 4 * j + 8)
                sp.dma_start(h_view[bass.ds(j, 1)].rearrange("a p w -> (a p) w"), h_out[:, par]).then_inc(h_stored[par], 16)
            pairs(sp, NT, store_rows)
            for e in range(X):
                if e >= 1:
                    sp.wait_ge(b1_out, 16 * e)
                sp.dma_start(b1_row[0:1, :], b1[e:e + 1, :]).then_inc(b1_in, 16)
                sp.wait_ge(w1_scaled, 2 * e + 2)
                sp.dma_start(w1_g[e].rearrange("p (c f) -> p c f", c=KC), w1e[:, e % 2]).then_inc(w1_out[e % 2], 16)
                sp.wait_ge(b1_added, e + 1)
                sp.dma_start(bias_d[e:e + 1, :], b1_row[0:1, :]).then_inc(b1_out, 16)
                if e + 2 < X:
                    sp.wait_ge(w1_out[e % 2], 16 * (e // 2 + 1))
                    load_w1(e + 2)
            for par in range(2):
                sp.wait_ge(w1_out[par], 16 * X // 2)
            sp.wait_ge(b1_out, 16 * X)
            sp.wait_ge(acc_free, 1)
            for e in range(X):
                sp.dma_start(w1_sb[:, e], w1_g[e].rearrange("p (c f) -> p c f", c=KC)).then_inc(w1_loaded, 16)
            sp.wait_ge(x1_made, NT + 2)
            sp.dma_start(out[0:(NT - 1) * P, :].rearrange("(j p) d -> p j d", p=P), x_sb[:, 0:NT - 1, :]).then_inc(out_init, 16)
            sp.dma_start(out[(NT - 1) * P:N, :], x_sb[0:LASTN, NT - 1, :]).then_inc(out_init, 16)
            sp.dma_start(w2_sb, w2).then_inc(w2_loaded, 16)
            sp.wait_ge(send_ready, 1)
            sp.dma_start(out[N:N + P, :], xs_pad[:, 0:D]).then_inc(out_init, 16)
            sp.dma_start(x_rows[X * XR:X * XR + P, :], xs_pad).then_inc(out_init, 16)
            sp.wait_ge(sent, 16 * (2 * NT + X))
            sp.wait_ge(out_init, 64)

            def load_tile(i, par):
                sp.wait_ge(tile_done, i + 1)
                e_reg, = load_values(ENG.SP, ftab[0:1, bass.ds(i, 1)], X - 1)
                r_reg, = load_values(ENG.SP, ftab[0:1, bass.ds(i + FT, 1)], X * XR)
                sp.dma_start(xg[:, par], x_rows[bass.ds(r_reg, P), :]).then_inc(xg_in[par], 16)
                sp.dma_start(bias_r[:, par, 0:F], bias_d[bass.ds(e_reg, 1), :].broadcast_to([P, F])).then_inc(xg_in[par], 16)
                sp.dma_start(bias_r[:, par, F:F + D], b2[bass.ds(e_reg, 1), :].broadcast_to([P, D])).then_inc(xg_in[par], 16)
            pairs(sp, FT, load_tile)

        @block.gpsimd
        def _(pool):
            step = Chain(pool, pool_step)
            g = nc.gpsimd
            step(g.memset(eye[:], 0.0))
            step(g.memset(hmask[:], 1.0))
            step(g.iota(iota_r[:], pattern=[[1, P]], base=0, channel_multiplier=0, allow_small_or_imprecise_dtypes=True))
            step(g.iota(pcol[:], pattern=[[P, TC]], base=0, channel_multiplier=1, allow_small_or_imprecise_dtypes=True))
            step(g.iota(t_it, pattern=[[1, IT]], base=0, channel_multiplier=0, allow_small_or_imprecise_dtypes=True))
            step.settle()
            step(g.affine_select(out=eye[:], in_=eye[:], compare_op=ALU.not_equal, fill=1.0, base=1,
                                 pattern=[[-1, P + 2]], channel_multiplier=1))
            step(g.affine_select(out=hmask[:], in_=hmask[:], compare_op=ALU.is_ge, fill=0.0, base=0,
                                 pattern=[[P, KC], [-DH, H]], channel_multiplier=1))
            step.settle()
            g.affine_select(out=hmask[:], in_=hmask[:], compare_op=ALU.is_ge, fill=0.0, base=DH - 1,
                            pattern=[[-P, KC], [DH, H]], channel_multiplier=-1).then_inc(pool_const, 1)

            pool.wait_ge(items_ready, 1)
            pool.wait_ge(stab_stored, 16)

            def take_indices(i, par):
                step(g.tensor_copy(idx_r[:, par], idx_i[:, bass.ds(i * G, G)]))
                step.settle()
                pool.sem_inc(pool_turn, 1)

            def gather_scores(i, par):
                take_indices(i, par)
                for k in range(G):
                    g.indirect_dma_start(out=sg[:, par, k, :], out_offset=None, in_=s_tab,
                                         in_offset=bass.IndirectOffsetOnAxis(ap=idx_r[:, par, k:k + 1], axis=0)
                                         ).then_inc(sg_in[par], 16)

            def keep_scores(i, turn, par):
                pool.wait_ge(sg_in[par], 16 * G * (turn + 1))
                step(g.tensor_copy(s_src[:, bass.ds(i * G, G), :], sg[:, par]))

            gather_scores(0, 0)
            with pool.Fori(0, NG // 2 - 1) as turn:
                step.enter(turn, 4)
                gather_scores(2 * turn + 1, 1)
                keep_scores(2 * turn, turn, 0)
                step.settle()
                gather_scores(2 * turn + 2, 0)
                keep_scores(2 * turn + 1, turn, 1)
                step.settle()
                step.leave(NG // 2 - 1)
            gather_scores(NG - 1, 1)
            keep_scores(NG - 2, NG // 2 - 1, 0)
            keep_scores(NG - 1, NG // 2 - 1, 1)
            step.settle()
            pool.sem_inc(s_src_ready, 1)

            pool.wait_ge(h_stored[0], 16 * ((NT + 1) // 2 + 1))
            pool.wait_ge(h_stored[1], 16 * (NT // 2 + 1))
            for par in range(2):
                pool.wait_ge(w1_out[par], 16 * X // 2)

            def gather_rows(i, par):
                pool.wait_ge(sum_made, 4 * i + 4)
                take_indices(i, par)
                for k in range(G):
                    g.indirect_dma_start(out=ring[:, par, k, :], out_offset=None, in_=h_tab,
                                         in_offset=bass.IndirectOffsetOnAxis(ap=idx_r[:, par, k:k + 1], axis=0)
                                         ).then_inc(rows_in[par], 16)

            with pool.Fori(0, NG // 2) as turn:
                step.enter(turn, 2)
                gather_rows(2 * turn, 0)
                gather_rows(2 * turn + 1, 1)
                step.leave(NG // 2)

            s1_u, s2_u, pad_u = slot_u[0], slot_u[1], slot_u[2]
            pool.wait_ge(send_ready, 1)
            for j in range(NT):
                n = P if j < NT - 1 else LASTN
                g.indirect_dma_start(out=x_rows, out_offset=bass.IndirectOffsetOnAxis(ap=s1_u[0:n, j:j + 1], axis=0),
                                     in_=xs[0:n, j, :], in_offset=None).then_inc(sent, 16)
            for e in range(X):
                g.indirect_dma_start(out=x_rows, out_offset=bass.IndirectOffsetOnAxis(ap=pad_u[:, e:e + 1], axis=0),
                                     in_=xs_pad, in_offset=None).then_inc(sent, 16)
            pool.wait_ge(send_ready, 2)
            for j in range(NT):
                n = P if j < NT - 1 else LASTN
                g.indirect_dma_start(out=x_rows, out_offset=bass.IndirectOffsetOnAxis(ap=s2_u[0:n, j:j + 1], axis=0),
                                     in_=xs[0:n, j, :], in_offset=None).then_inc(sent, 16)
            pool.wait_ge(out_init, 64)

            with pool.Fori(0, FT // 2) as turn:
                for par in range(2):
                    pool.wait_ge(tile_done, 2 * turn + par + 3)
                    pool.sem_inc(pool_turn, 1)
                    g.indirect_dma_start(out=out, out_offset=bass.IndirectOffsetOnAxis(ap=tok_u[:, par:par + 1], axis=0),
                                         in_=y_out[:, par], in_offset=None, compute_op=ALU.add).then_inc(y_added[par], 16)
                    pool.wait_ge(y_added[par], 16 * (turn + 1))
                    pool.sem_inc(y_free, 1)


        @block.vector
        def _(dve):
            step = Chain(dve, dve_step)
            v = nc.vector
            dve.sem_inc(stab_copied, 2)
            dve.sem_inc(kv_ready, 1)
            dve.sem_inc(q_read, 1)
            dve.sem_inc(y_free, 2)
            dve.sem_inc(spread_used, 2)
            dve.sem_inc(sum_added, 4)
            dve.sem_inc(x1_made, 2)
            dve.sem_inc(tile_done, 2)

            step(v.memset(e_raw[:, 0, TC - 1, :], NP))
            step(v.memset(e_raw[:, 1, TC - 1, :], 0))
            step(v.memset(e_raw[:, 2, TC - 1, :], 0))
            step(v.memset(x_sb[:, NT - 1, :], 0.0))
            step.settle()
            dve.sem_inc(fill_done, 1)
            step(v.memset(ones[:], 1.0))
            step(v.memset(zrow, 0.0))

            dve.wait_ge(in_edges, 16 * 9)
            step(v.tensor_copy(e_f, e_raw))
            step.settle()
            for b in range(1, NT):
                step(v.tensor_scalar(spread[:, 0:2].rearrange("p c i -> p (c i)")[:, 0:TC * P], e_f[:, 0].rearrange("p c e -> p (c e)"),
                                     float(b * P), 0.0, ALU.is_lt, ALU.add, accum_out=cnt[:, b - 1:b]))
                step.settle()
            dve.sem_inc(dve_to_pe, 1)
            step(v.scalar_tensor_tensor(out=e_f[:, 1], in0=e_f[:, 1], scalar=float(R), in1=e_f[:, 2], op0=ALU.mult, op1=ALU.add))
            dve.wait_ge(pool_const, 1)
            step(v.tensor_copy(eye_b[:], ident))
            dve.wait_ge(pe_to_dve, 1)
            fcol, fint = carry[0:NT - 1, 0:1], carry[0:NT - 1, 1:2].bitcast(I32)
            step(v.tensor_copy(fint, psum[0:NT - 1, 0, 0:1]))
            step.settle()
            step(v.tensor_scalar(fint, fint, 7, None, ALU.arith_shift_right))
            step.settle()
            step(v.tensor_copy(fcol, fint))
            step.settle()
            step(v.scalar_tensor_tensor(out=fcol, in0=fcol, scalar=1.0, in1=pcol[0:NT - 1, 0:1], op0=ALU.add, op1=ALU.add))
            step.settle()
            v.tensor_scalar(lt[0:NT - 1, :], t_it[0:NT - 1, :], fcol, None, ALU.is_ge).then_inc(dve_to_pe, 1)
            dve.wait_ge(pe_to_dve, 2)
            step(v.tensor_copy(blk[:], psum[0:1, 1, 0:IT]))
            step(v.tensor_copy(lt, psum[:, 1, 0:IT]))
            step.settle()
            step(v.tensor_tensor(t_it, t_it, lt, ALU.subtract))
            step.settle()
            for c in range(TC):
                step(v.tensor_scalar(spread[:, c], t_it, pcol[:, c:c + 1], None, ALU.is_equal))
            step.settle()
            dve.sem_inc(dve_to_pe, 1)
            dve.wait_ge(pe_to_dve, 3)
            step(v.scalar_tensor_tensor(out=dl[:], in0=lt, scalar=float(-P), in1=psum[:, 2, 0:IT], op0=ALU.mult, op1=ALU.add))
            step(v.tensor_copy(typ, psum[:, 4, 0:IT]))
            step(v.tensor_copy(idx_i[:], psum[:, 3, 0:IT]))
            step.settle()
            dve.sem_inc(items_ready, 1)

            dve.wait_ge(in_wrel, 32)
            for c in range(KC):
                for w in range(2):
                    step(v.tensor_scalar(ablock[:, c, w * H:(w + 1) * H], hmask[:, c, :], att_sb[:, c, w:w + 1], None, ALU.mult))
            step.settle()
            dve.sem_inc(dve_to_pe, 1)
            dve.wait_ge(pe_to_dve, 4)
            for m in range(KC):
                step(v.tensor_copy(wa_sb[:, m].rearrange("p (w r h) -> p w r h", w=2, r=R),
                                   psum[:, 5, m * 2 * R * H:(m + 1) * 2 * R * H].rearrange("p (r w h) -> p w r h", w=2, r=R)))
            step.settle()
            dve.sem_inc(dve_to_pe, 1)

            def spread_of(mean, dev, out_stats):
                m0, m1, s0, s1 = (out_stats[:, :, c] for c in (1, 4, 2, 5))
                step(v.tensor_tensor(mean, m0, m1, ALU.add))
                step(v.tensor_tensor(stx[:, 3], m0, m1, ALU.subtract))
                step(v.tensor_tensor(dev, s0, s1, ALU.add))
                step.settle()
                step(v.tensor_scalar(mean, mean, 0.5, None, ALU.mult))
                step(v.tensor_tensor(stx[:, 3], stx[:, 3], stx[:, 3], ALU.mult))
                step(v.tensor_scalar(dev, dev, 1.0 / D, LN_EPS, ALU.mult, ALU.add))
                step.settle()
                step(v.scalar_tensor_tensor(out=dev, in0=stx[:, 3], scalar=0.25, in1=dev, op0=ALU.mult, op1=ALU.add))
                step.settle()

            dve.wait_ge(in_x, 32)
            with dve.Fori(0, NT) as j:
                step.enter(j, 1)
                step(v.bn_stats(stats[:, bass.ds(j, 1), :].rearrange("p a s -> p (a s)"), x_sb[:, bass.ds(j, 1), :].rearrange("p a d -> p (a d)")))
                step.leave(NT)
            step.settle()
            spread_of(stx[:, 0], stx[:, 1], stats)
            dve.sem_inc(dve_to_act, 1)
            dve.wait_ge(act_to_dve, 1)
            step(v.reciprocal(stx[:, 2], stx[:, 1]))
            step.settle()

            def normalise(j, par):
                dve.wait_ge(xt_made, j + 1)
                v.tensor_scalar(xn_ring[:, par], x_sb[:, bass.ds(j, 1), :].rearrange("p a d -> p (a d)"),
                                stx[:, 0, bass.ds(j, 1)], stx[:, 2, bass.ds(j, 1)],
                                ALU.subtract, ALU.mult).then_inc(xn_made, 1)

            def copy_stab(j, par):
                dve.wait_ge(stab_made, j + 3)
                step(v.tensor_copy(s_out[:, bass.ds(j, 1), :].rearrange("p a s -> p (a s)"), psum[:, par, 0:R * H]))
                v.tensor_copy(s_dtab[:, bass.ds(j, 1), :].rearrange("p a s -> p (a s)"),
                              psum[:, par, R * H:2 * R * H]).then_inc(stab_copied, 1)

            normalise(0, 0)
            with dve.Fori(0, NT // 2) as turn:
                step.enter(turn, 2)
                normalise(2 * turn + 1, 1)
                copy_stab(2 * turn, 0)
                normalise(2 * turn + 2, 0)
                copy_stab(2 * turn + 1, 1)
                step.leave(NT // 2)
            copy_stab(NT - 1, 0)
            step.settle()

            dve.wait_ge(in_misc, 16 * 5)
            dve.wait_ge(xt_made, NT + 2)
            step(v.tensor_tensor(x_sb, x_sb, misc[:, 0:D].unsqueeze(1).broadcast_to([P, NT, D]), ALU.add))
            step(v.tensor_copy(bdm.rearrange("p (h d) -> p h d", d=DH), hmask[:, 0, 0:P // DH].unsqueeze(2).broadcast_to([P, P // DH, DH])))
            step.settle()

            def kv_q(j, par):
                dve.wait_ge(kv_made, j + 1)
                step.settle()
                step(v.tensor_scalar(k_low, psum[:, 4, 0:D], 0.0, None, ALU.min))
                dve.wait_ge(q_made, j + 1)
                v.tensor_scalar(q_low, psum[:, 5, 0:D].rearrange("p (a n) -> p a n", a=KC), 0.0, None, ALU.min).then_inc(low_ready, 1)
                dve.wait_ge(ctx_added, j + 1)
                step(v.tensor_copy(kv_sb[:, par, D:2 * D], psum[:, 4, D:2 * D]))
                dve.wait_ge(exp_ready, j + 1)
                step.settle()
                v.scalar_tensor_tensor(out=kv_sb[:, par, 0:D], in0=psum[:, 4, 0:D], scalar=0.0, in1=k_low,
                                       op0=ALU.max, op1=ALU.add).then_inc(kv_ready, 1)
                step(v.scalar_tensor_tensor(out=qT[:, :, bass.ds(j * P, P)], in0=psum[:, 5, 0:D].rearrange("p (a n) -> p a n", a=KC),
                                            scalar=0.0, in1=q_low, op0=ALU.max, op1=ALU.add))
                step.settle()
                dve.sem_inc(q_read, 1)

            with dve.Fori(0, NT // 2) as turn:
                step.enter(turn, 6)
                kv_q(2 * turn, 0)
                kv_q(2 * turn + 1, 1)
                step.leave(NT // 2)
            kv_q(NT - 1, 0)

            dve.wait_ge(ctx_added, NT + 2)
            for a in range(KC):
                step(v.tensor_tensor(ctxT[:, a], psum[:, 6, a * P:(a + 1) * P], bdm, ALU.mult))
                step(v.tensor_scalar(kb_sb[:, a], bdm, psum[:, 6, D + a:D + a + 1], None, ALU.mult))
            step.settle()
            dve.sem_inc(dve_to_pe, 1)
            dve.wait_ge(pe_to_dve, 5)
            step(v.tensor_copy(m_sb, psum[:, 7].rearrange("p (a o) -> p a o", a=KC)))
            step.settle()
            dve.sem_inc(dve_to_pe, 1)

            for e in range(X):
                dve.wait_ge(w1_used, e + 1)
                dve.wait_ge(b1_in, 16 * (e + 1))
                v.tensor_tensor(b1_row[0:1, :], b1_row[0:1, :], psum[0:1, 0:2, :].rearrange("p n f -> p (n f)"),
                                ALU.add).then_inc(b1_added, 1)

            step(v.tensor_tensor(rmask, typ.unsqueeze(2).broadcast_to([P, IT, R]),
                                 iota_r[:, 0:R].unsqueeze(1).broadcast_to([P, IT, R]), ALU.is_equal))
            dve.wait_ge(b1_out, 16 * X)

            def one_hot(i, par):
                dve.wait_ge(oha_used, i + 1)
                v.tensor_tensor(oh_a[:, par], dl[:, bass.ds(i * G, G)].unsqueeze(2).broadcast_to([P, G, P]),
                                iota_r[:].unsqueeze(1).broadcast_to([P, G, P]), ALU.is_equal).then_inc(oha_made, 1)

            def pick_relation(i, par):
                dve.wait_ge(spread_made, i + 3)
                step.settle()
                step(v.tensor_tensor(tmp_s.rearrange("p k (r h) -> p k r h", r=R),
                                     psum[:, 4 + 2 * par:6 + 2 * par, :].rearrange("p b (k r h) -> p (b k) r h", r=R, h=H),
                                     rmask[:, bass.ds(i * G, G), :].unsqueeze(3).broadcast_to([P, G, R, H]), ALU.mult))
                step.settle()
                step(v.tensor_reduce(s_dst[:, bass.ds(i * G, G), :], tmp_s.rearrange("p k (r h) -> p k h r", r=R), AX, ALU.add))
                step.settle()
                dve.sem_inc(spread_used, 1)

            one_hot(0, 0)
            with dve.Fori(0, NG // 2 - 1) as turn:
                step.enter(turn, 4)
                one_hot(2 * turn + 1, 1)
                pick_relation(2 * turn, 0)
                one_hot(2 * turn + 2, 0)
                pick_relation(2 * turn + 1, 1)
                step.leave(NG // 2 - 1)
            one_hot(NG - 1, 1)
            pick_relation(NG - 2, 0)
            pick_relation(NG - 1, 1)

            dve.wait_ge(s_src_ready, 1)
            step(v.tensor_tensor(s_all.rearrange("p h c j -> p h (c j)"), s_src.rearrange("p i h -> p h i"),
                                 s_dst.rearrange("p i h -> p h i"), ALU.add))
            step.settle()
            step(v.tensor_copy(d_all.rearrange("p h c j -> p h (c j)"), dl[:].unsqueeze(1).broadcast_to([P, H, IT])))
            step.settle()
            dve.sem_inc(dve_to_pe, 1)

            def ask_pe(n):
                step.settle()
                dve.sem_inc(dve_to_pe, 1)
                dve.wait_ge(pe_to_dve, n)

            NB = -(-J // 4)
            dve.wait_ge(tr_copied, NB)
            step(v.scalar_tensor_tensor(out=score, in0=score, scalar=0.2, in1=score, op0=ALU.mult, op1=ALU.max))
            dve.wait_ge(tr_copied, 2 * NB)
            step(v.tensor_tensor(keep[:, 1:L], sc2[:, 1:L], sc2[:, 0:L - 1], ALU.is_equal))
            ask_pe(6)
            step(v.tensor_reduce(carry[:, 0:1], ident.rearrange("p (h c) -> p c h", h=H)[:, 0, :], AX, ALU.add))
            step(v.tensor_tensor(keep[:, 0:1], sc2[:, 0:1], psum[:, 0, 0:1], ALU.is_equal))
            step.settle()
            step(v.tensor_scalar(carry[:, 0:1], carry[:, 0:1], -1.0, 1.0, ALU.mult, ALU.add))
            step.settle()
            step(v.tensor_tensor(keep[:, 0:1], keep[:, 0:1], carry[:, 0:1], ALU.mult))
            ask_pe(7)
            step(v.tensor_copy(keep[:, L:L + 1], psum[:, 1, 0:1]))
            step.settle()
            step(v.tensor_reduce(carry[:, 1:2], keep[:, 0:L], AX, ALU.min))
            step(v.tensor_reduce(carry[:, 2:3], keep[:, 1:L + 1], AX, ALU.min))
            step(v.memset(rows[0:1, 3, :], 0.0))
            ask_pe(8)
            step(v.tensor_copy(rows[0:1, 0:2, 0:P], psum[0:1, 2, 0:2 * P].rearrange("p (a n) -> p a n", a=2)))
            step.settle()

            def scan(out_, data, op, back, answer):
                flip = slice(None, None, -1) if back else slice(None)
                kp = keep[:, 1:L + 1] if back else keep[:, 0:L]
                args = kp[:, flip], data[:, flip]
                step(v.tensor_tensor_scan(out_[:, flip], *args, 0.0, ALU.mult, op))
                step.settle()
                end = 0 if back else L - 1
                step(v.tensor_copy(carry[:, 0:1], out_[:, end:end + 1]))
                ask_pe(answer)
                step(v.tensor_copy(rows[0:1, 2, 0:P], psum[0:1, 3, 0:P]))
                step.settle()
                to = rows[0:1, 3, 0:P] if back else rows[0:1, 3, 1:P + 1]
                edge = rows[0:1, 3, P:P + 1] if back else rows[0:1, 3, 0:1]
                step(v.memset(edge, 0.0))
                step(v.tensor_tensor_scan(to[:, flip], rows[0:1, 1 if back else 0, 0:P][:, flip],
                                          rows[0:1, 2, 0:P][:, flip], 0.0, ALU.mult, op))
                ask_pe(answer + 1)
                step(v.tensor_copy(carry[:, 3:4], psum[:, 4, 0:1]))
                step.settle()
                step(v.tensor_tensor_scan(out_[:, flip], *args, carry[:, 3:4], ALU.mult, op))
                step.settle()

            scan(sc1, score, ALU.max, False, 9)
            scan(sc2, sc1, ALU.max, True, 11)
            step(v.tensor_tensor(score, score, sc2, ALU.subtract))
            step.settle()
            dve.sem_inc(dve_to_act, 1)
            dve.wait_ge(act_to_dve, 2)
            scan(sc1, score, ALU.add, False, 13)
            scan(sc2, sc1, ALU.max, True, 15)
            step(v.tensor_scalar(sc2, sc2, 1e-12, None, ALU.add))
            step.settle()
            step(v.reciprocal(sc2, sc2))
            step.settle()
            step(v.tensor_tensor(score, score, sc2, ALU.mult))
            step.settle()
            dve.sem_inc(dve_to_pe, 1)
            step(v.memset(acc, 0.0))
            dve.wait_ge(tr_copied, 3 * NB)
            step.settle()
            dve.sem_inc(acc_free, 1)

            def weigh(i, par, turn, q):
                dve.wait_ge(sum_made, 4 * i + q + 5)
                step(v.tensor_tensor(oh_b[:, 4 * q:4 * q + 4], dl[:, bass.ds(i * G + 4 * q, 4)].unsqueeze(2).broadcast_to([P, 4, P]),
                                     iota_r[:].unsqueeze(1).broadcast_to([P, 4, P]), ALU.is_equal))
                if q == 0:
                    dve.wait_ge(rows_in[par], 16 * G * (turn + 1))
                part = ring[:, par, 4 * q:4 * q + 4].rearrange("p k (h d) -> p (k h) d", d=DH)
                wts = w_i.rearrange("p c j h -> p (c j h)")[:, bass.ds(i * G * H + 4 * q * H, 4 * H)]
                v.tensor_tensor(part, part, wts.unsqueeze(2).broadcast_to([P, 4 * H, DH]), ALU.mult).then_inc(msg_made, 1)

            def add_up(i, q, blocks):
                dve.wait_ge(sum_made, 4 * i + q + 9)
                for k in range(4 * q, 4 * q + 4):
                    a = acc[:, bass.ds(blocks[k], 1), :].rearrange("p a d -> p (a d)")
                    step(v.tensor_tensor(a, a, psum[:, k // 2, (k % 2) * D:(k % 2 + 1) * D], ALU.add))
                    step.settle()
                dve.sem_inc(sum_added, 1)

            def group(i, par, turn):
                blocks = load_values(ENG.DVE, blk[0:1, bass.ds((i - 1) * G, G)], NT - 1)
                for q in range(4):
                    weigh(i, par, turn, q)
                    add_up(i - 1, q, blocks)

            for q in range(4):
                weigh(0, 0, 0, q)
            with dve.Fori(0, NG // 2 - 1) as turn:
                step.enter(turn, 40)
                group(2 * turn + 1, 1, turn)
                group(2 * turn + 2, 0, turn + 1)
                step.leave(NG // 2 - 1)
            group(NG - 1, 1, NG // 2 - 1)
            blocks = load_values(ENG.DVE, blk[0:1, (NG - 1) * G:NG * G], NT - 1)
            for q in range(4):
                add_up(NG - 1, q, blocks)
            dve.sem_inc(dve_to_pe, 1)

            def divide_q(j, par):
                dve.wait_ge(den_made, j + 1)
                dve.wait_ge(mix_made, j + 1)
                step(v.tensor_scalar(q_inv, psum[:, 0, 0:D].rearrange("p (a n) -> p a n", a=KC), 1e-6, None, ALU.max))
                step.settle()
                step(v.reciprocal(q_inv, q_inv))
                step.settle()
                v.tensor_tensor(qr[:, par], qT[:, :, bass.ds(j * P, P)], q_inv, ALU.mult).then_inc(qr_made, 1)

            def tile_of(t, j):
                return t[:, bass.ds(j, 1), :].rearrange("p a d -> p (a d)")

            def add_x1(j, par):
                xj = tile_of(x_sb, j)
                step(v.tensor_tensor(xj, xj, tile_of(acc, j), ALU.add))
                dve.wait_ge(mix_made, j + 3)
                step.settle()
                v.tensor_tensor(xj, xj, psum[:, 1 + par, 0:D], ALU.add).then_inc(x1_made, 1)
                dve.wait_ge(x1_made, j + 3)
                step(v.bn_stats(tile_of(stats_z, j), xj))

            divide_q(0, 0)
            with dve.Fori(0, NT // 2) as turn:
                step.enter(turn, 8)
                divide_q(2 * turn + 1, 1)
                add_x1(2 * turn, 0)
                divide_q(2 * turn + 2, 0)
                add_x1(2 * turn + 1, 1)
                step.leave(NT // 2)
            add_x1(NT - 1, 0)
            step.settle()

            spread_of(stx[:, 0], stx[:, 1], stats_z)
            dve.sem_inc(dve_to_act, 1)
            dve.wait_ge(act_to_dve, 3)
            step(v.reciprocal(stx[:, 2], stx[:, 1]))
            step.settle()

            def norm_y(j, par):
                dve.wait_ge(yT_made, j + 1)
                dve.wait_ge(xs_copied, j + 1)
                v.tensor_scalar(y_ring[:, par], tile_of(x_sb, j), stx[:, 0, bass.ds(j, 1)], stx[:, 2, bass.ds(j, 1)],
                                ALU.subtract, ALU.mult).then_inc(yr_made, 1)
                dve.wait_ge(yr_made, j + 1)
                step(v.bn_stats(tile_of(stats_z, j), y_ring[:, par]))

            with dve.Fori(0, NT // 2) as turn:
                step.enter(turn, 2)
                norm_y(2 * turn, 0)
                norm_y(2 * turn + 1, 1)
                step.leave(NT // 2)
            norm_y(NT - 1, 0)
            step.settle()
            spread_of(stx[:, 0], stx[:, 1], stats_z)
            dve.sem_inc(dve_to_act, 1)
            dve.wait_ge(act_to_dve, 4)
            step(v.reciprocal(stx[:, 2], stx[:, 1]))
            step.settle()
            dve.wait_ge(xs_copied, NT + 2)
            with dve.Fori(0, NT) as j:
                step.enter(j, 1)
                step(v.tensor_scalar(xs[:, bass.ds(j, 1), 0:D].rearrange("p a d -> p (a d)"),
                                     xs[:, bass.ds(j, 1), 0:D].rearrange("p a d -> p (a d)"),
                                     stx[:, 0, bass.ds(j, 1)], stx[:, 2, bass.ds(j, 1)], ALU.subtract, ALU.mult))
                step.leave(NT)

            def by_x(t):
                return t.rearrange("p (t x) -> p t x", x=X)

            def over_x(t):
                return t.unsqueeze(2).broadcast_to([P, NT, X])

            def x_row(t):
                return t.unsqueeze(1).broadcast_to([P, NT, X])

            pr, o1, o2, tmp, osum, tot, incl, rank, msk = rt
            mx, sm, p1, p2, w1c, w2c, f1, f2, cx, ntx, cumx = small[:11]
            dve.wait_ge(pe_to_dve, 17)
            step(v.tensor_tensor(by_x(pr), by_x(psum[:, 3, 0:NT * X]), x_row(br_sb), ALU.add))
            step.settle()
            step(v.tensor_reduce(mx, by_x(pr), AX, ALU.max))
            step.settle()
            step(v.tensor_tensor(by_x(pr), by_x(pr), over_x(mx), ALU.subtract))
            step.settle()
            dve.sem_inc(dve_to_act, 1)
            dve.wait_ge(act_to_dve, 5)
            step(v.tensor_reduce(sm, by_x(pr), AX, ALU.add))
            step.settle()
            step(v.reciprocal(sm, sm))
            step(v.tensor_scalar(mx[:, 0:X], iota_r[:, 0:X], -1.0, float(X), ALU.mult, ALU.add))
            step.settle()
            step(v.tensor_tensor(by_x(pr), by_x(pr), over_x(sm), ALU.mult))
            step.settle()

            def top(one_hot_, best):
                step(v.tensor_reduce(best, by_x(pr), AX, ALU.max))
                step.settle()
                step(v.tensor_tensor(by_x(tmp), by_x(pr), over_x(best), ALU.is_equal))
                step.settle()
                step(v.tensor_tensor(by_x(tmp), by_x(tmp), x_row(mx[:, 0:X]), ALU.mult))
                step.settle()
                step(v.tensor_reduce(f1, by_x(tmp), AX, ALU.max))
                step.settle()
                step(v.tensor_tensor(by_x(one_hot_), by_x(tmp), over_x(f1), ALU.is_equal))
                step.settle()

            top(o1, p1)
            step(v.scalar_tensor_tensor(out=pr, in0=o1, scalar=-4.0, in1=pr, op0=ALU.mult, op1=ALU.add))
            step.settle()
            top(o2, p2)
            step(v.tensor_tensor(f1, p1, p2, ALU.add))
            step.settle()
            step(v.reciprocal(f1, f1))
            step.settle()
            step(v.tensor_tensor(w1c, p1, f1, ALU.mult))
            step(v.tensor_tensor(w2c, p2, f1, ALU.mult))
            step(v.tensor_scalar(f2[:, 0:1], pcol[:, 0:1], float(LASTN), None, ALU.is_lt))
            step.settle()
            for o in (o1, o2):
                step(v.tensor_scalar(o[:, (NT - 1) * X:], o[:, (NT - 1) * X:], f2[:, 0:1], None, ALU.mult))
            step.settle()
            by_t = "p (x t) -> p t x"
            step(v.tensor_tensor(osum.rearrange(by_t, x=X), by_x(o1), by_x(o2), ALU.add))
            step(v.tensor_scalar(upper, iota_r[:], pcol[:, 0:1], None, ALU.is_gt))
            step(v.memset(msk, 1.0))
            step.settle()
            step(v.memset(msk.rearrange("p (x t) -> p x t", x=X)[:, :, 0], 0.0))
            ask_pe(18)
            step(v.tensor_copy(tot, psum[:, 5, 0:NT * X]))
            step.settle()
            step(v.tensor_tensor_scan(incl, msk, tot, 0.0, ALU.mult, ALU.add))
            step.settle()
            step(v.tensor_copy(cx[:, 0:X], incl.rearrange("p (x t) -> p x t", x=X)[:, :, NT - 1]))
            step(v.tensor_tensor(rank, incl, tot, ALU.subtract))
            step.settle()
            step(v.tensor_tensor(rank, rank, psum[:, 4, 0:NT * X], ALU.add))
            step.settle()
            step(v.scalar_tensor_tensor(out=rank.rearrange("p (x t) -> p x t", x=X),
                                        in0=iota_r[:, 0:X].unsqueeze(2).broadcast_to([P, X, NT]), scalar=float(XR),
                                        in1=rank.rearrange("p (x t) -> p x t", x=X), op0=ALU.mult, op1=ALU.add))
            step.settle()
            for o, slot in ((o1, slot_u[0]), (o2, slot_u[1])):
                step(v.tensor_tensor(by_x(tmp), by_x(o), rank.rearrange(by_t, x=X), ALU.mult))
                step.settle()
                step(v.tensor_reduce(f1, by_x(tmp), AX, ALU.add))
                step.settle()
                step(v.tensor_copy(slot, f1))
                step.settle()
            step(v.scalar_tensor_tensor(out=f1[:, 0:X], in0=iota_r[:, 0:X], scalar=float(XR), in1=cx[:, 0:X], op0=ALU.mult, op1=ALU.add))
            step.settle()
            step(v.tensor_scalar(f1[:, 0:X], f1[:, 0:X], pcol[:, 0:1], None, ALU.add))
            step.settle()
            step(v.tensor_copy(slot_u[2][:, 0:X], f1[:, 0:X]))
            step(v.memset(xs_pad, 0.0))
            step(v.memset(xs[:, :, D + 2:XW], 0.0))
            step(v.tensor_copy(xs[:, :, D], w1c))
            step(v.tensor_scalar(xs[:, :, D + 1], iota_r[:, 0:NT], float(P), pcol[:, 0:1], ALU.mult, ALU.add))
            step.settle()
            step(v.tensor_scalar(xs_pad[:, D + 1:D + 2], pcol[:, 0:1], float(N), None, ALU.add))
            nti = f2[0:1, 0:X].bitcast(I32)
            step(v.tensor_scalar(ntx[0:1, 0:X], cx[0:1, 0:X], float(P - 1), None, ALU.add))
            step.settle()
            step(v.tensor_copy(nti, ntx[0:1, 0:X]))
            step.settle()
            step(v.tensor_scalar(nti, nti, 7, None, ALU.arith_shift_right))
            step.settle()
            step(v.tensor_copy(ntx[0:1, 0:X], nti))
            step.settle()
            step(v.tensor_tensor_scan(cumx[0:1, 0:X], ones[0:1, 0:X], ntx[0:1, 0:X], 0.0, ALU.mult, ALU.add))
            step.settle()
            step(v.tensor_tensor(ntx[0:1, 0:X], cumx[0:1, 0:X], ntx[0:1, 0:X], ALU.subtract))
            step.settle()
            step(v.tensor_scalar(ntx[0:1, 0:X], ntx[0:1, 0:X], float(-P), None, ALU.mult))
            step.settle()
            step(v.scalar_tensor_tensor(out=ntx[0:1, 0:X], in0=iota_r[0:1, 0:X], scalar=float(XR), in1=ntx[0:1, 0:X], op0=ALU.mult, op1=ALU.add))
            step.settle()
            step(v.tensor_tensor(sm[0:1, 0:X - 1], ntx[0:1, 1:X], ntx[0:1, 0:X - 1], ALU.subtract))
            ge = at(Z1 + 5 * NT * X, FT, X)[0:1]
            step(v.tensor_tensor(ge, iota_r[0:1, 0:FT].unsqueeze(2).broadcast_to([1, FT, X]),
                                 cumx[0:1, 0:X].unsqueeze(1).broadcast_to([1, FT, X]), ALU.is_ge))
            step.settle()
            et, rw = tmp[0:1, 0:FT], tmp[0:1, FT:2 * FT]
            step(v.tensor_reduce(et, ge[:, :, 0:X - 1], AX, ALU.add))
            step(v.tensor_tensor(gt[0:1], ge[:, :, 0:X - 1],
                                 sm[0:1, 0:X - 1].unsqueeze(1).broadcast_to([1, FT, X - 1]), ALU.mult))
            step.settle()
            step(v.tensor_reduce(rw, gt[0:1], AX, ALU.add))
            step.settle()
            step(v.scalar_tensor_tensor(out=rw, in0=iota_r[0:1, 0:FT], scalar=float(P), in1=rw, op0=ALU.mult, op1=ALU.add))
            step.settle()
            step(v.tensor_scalar(rw, rw, ntx[0:1, 0:1], None, ALU.add))
            step.settle()
            step(v.tensor_scalar(gt[0:1, :, 0], rw, -1.0, float(X * XR), ALU.mult, ALU.add))
            step.settle()
            step(v.tensor_tensor(gt[0:1, :, 0], gt[0:1, :, 0], ge[:, :, X - 1], ALU.mult))
            step.settle()
            step(v.tensor_tensor(rw, rw, gt[0:1, :, 0], ALU.add))
            step.settle()
            step(v.tensor_copy(ftab[:, 0:FT], et))
            step(v.tensor_copy(ftab[:, FT:2 * FT], rw))
            step.settle()
            dve.sem_inc(send_ready, 1)
            dve.wait_ge(sent, 16 * (NT + X))
            dve.wait_ge(out_init, 64)
            step(v.tensor_copy(xs[:, :, D], w2c))
            step.settle()
            dve.sem_inc(send_ready, 1)

            def copy_xT(i, par):
                dve.wait_ge(xgT_made, i + 1)
                v.tensor_copy(xgT[:, par], psum[:, 0, 0:D].rearrange("p (a n) -> p a n", a=KC)).then_inc(xgT_copied, 1)

            def add_b1(i, par, turn):
                dve.wait_ge(xg_in[par], 48 * (turn + 1))
                for n in range(2):
                    dve.wait_ge(f1_made, 2 * i + n + 1)
                    v.tensor_tensor(h_sb[:, par, n * 512:(n + 1) * 512], psum[:, 1 + n, :],
                                    bias_r[:, par, n * 512:(n + 1) * 512], ALU.add).then_inc(h_pre, 1)

            def finish(i, par, turn):
                dve.wait_ge(hT_made, 2 * i + 1)
                v.tensor_copy(hT[:, par, 0:4], psum[:, 3].rearrange("p (c n) -> p c n", c=4)).then_inc(hT_copied, 1)
                dve.wait_ge(f2_made, i + 1)
                dve.wait_ge(y_free, i + 1)
                step(v.tensor_tensor(y_b2, psum[:, 5, 0:D], bias_r[:, par, F:F + D], ALU.add))
                step(v.tensor_copy(tok_u[:, par:par + 1], xg[:, par, D + 1:D + 2]))
                step.settle()
                v.tensor_scalar(y_out[:, par], y_b2, xg[:, par, D:D + 1], None, ALU.mult).then_inc(tile_done, 1)
                dve.wait_ge(tile_done, i + 3)

            copy_xT(0, 0)
            add_b1(0, 0, 0)
            with dve.Fori(0, FT // 2 - 1) as turn:
                step.enter(turn, 4)
                copy_xT(2 * turn + 1, 1)
                add_b1(2 * turn + 1, 1, turn)
                finish(2 * turn, 0, turn)
                copy_xT(2 * turn + 2, 0)
                add_b1(2 * turn + 2, 0, turn + 1)
                finish(2 * turn + 1, 1, turn)
                step.leave(FT // 2 - 1)
            copy_xT(FT - 1, 1)
            add_b1(FT - 1, 1, FT // 2 - 1)
            finish(FT - 2, 0, FT // 2 - 1)
            finish(FT - 1, 1, FT // 2 - 1)

        @block.scalar
        def _(act):
            a_ = nc.scalar
            act.sem_inc(xt_copied, 2)
            act.sem_inc(h_copied, 4)
            for par in range(2):
                act.sem_inc(h_stored[par], 16)
            act.sem_inc(ohT_made, 2)
            act.sem_inc(yT_copied, 2)
            act.sem_inc(xs_copied, 2)

            def root(n):
                act.wait_ge(dve_to_act, n)
                a_.activation(stx[:, 1], stx[:, 1], ACT.Sqrt).then_inc(act_to_dve, 1)

            root(1)

            def copy_xt(j, par):
                act.wait_ge(xt_made, j + 3)
                act.wait_ge(stab_made, j + 1)
                src_ = psum[:, 6 + par, 0:D].rearrange("p (a n) -> p a n", a=KC)
                a_.copy(xs_ring[:, par], src_)
                a_.copy(xnT[:, :, bass.ds(j * P, P)], src_).then_inc(xt_copied, 1)
            pairs(act, NT, copy_xt)

            def copy_xs(j, par):
                act.wait_ge(ctx_added, j + 1)
                a_.copy(xs_ring[:, par], xnT[:, :, bass.ds(j * P, P)]).then_inc(xs_made, 1)

            act.wait_ge(stab_made, NT + 2)
            act.wait_ge(xt_copied, NT + 2)

            def evacuate(j, par, turn, more):
                if more:
                    copy_xs(j + 1, 1 - par)
                act.wait_ge(low_ready, j + 1)
                a_.activation(k_low, k_low, ACT.Exp)
                a_.activation(q_low, q_low, ACT.Exp).then_inc(exp_ready, 1)
                for n in range(4):
                    act.wait_ge(h_made, 4 * j + n + 1)
                    if n == 0:
                        act.wait_ge(h_stored[par], 16 * (turn + 1))
                    a_.copy(h_out[:, par, n * 512:(n + 1) * 512], psum[:, n, :]).then_inc(h_copied, 1)

            copy_xs(0, 0)
            with act.Fori(0, NT // 2) as turn:
                evacuate(2 * turn, 0, turn, True)
                evacuate(2 * turn + 1, 1, turn, True)
            evacuate(NT - 1, 0, NT // 2, False)

            act.wait_ge(in_misc, 16 * 5)
            for e in range(X):
                act.wait_ge(w1_used, e + 1)
                for c in range(KC):
                    a_.mul(w1e[:, e % 2, c], w1e[:, e % 2, c], ln_cols[:, 0, e, c:c + 1]).then_inc(w1_scaled, 1)

            def copy_ohT(i, par):
                act.wait_ge(oha_used, i + 3)
                act.wait_ge(spread_made, i + 1)
                a_.copy(ohT[:, par].rearrange("p k n -> p (k n)"),
                        psum[:, 2 * par:2 * par + 2, :].rearrange("p b n -> p (b n)").bitcast(BF16)).then_inc(ohT_made, 1)
            pairs(act, NG, copy_ohT)

            NB = -(-J // 4)
            n = 0
            for to in (score, sc2):
                for b in range(NB):
                    width = min(4, J - 4 * b) * P
                    act.wait_ge(tr_made, n + 1)
                    a_.copy(to[:, 4 * b * P:4 * b * P + width], psum[:, n % 8, 0:width]).then_inc(tr_copied, 1)
                    n += 1
            act.wait_ge(dve_to_act, 2)
            a_.activation(score, score, ACT.Exp).then_inc(act_to_dve, 1)
            for b in range(NB):
                w = min(4, J - 4 * b)
                act.wait_ge(tr_made, n + 1)
                for k in range(w):
                    ins = a_.copy(w_i[:, :, 4 * b + k, :].rearrange("p c h -> p h c"),
                                  psum[:, b % 8, k * P:(k + 1) * P].rearrange("p (h c) -> p h c", h=H))
                ins.then_inc(tr_copied, 1)
                n += 1

            root(3)

            def copy_y(j, par):
                act.wait_ge(yr_made, j + 1)
                a_.copy(xs[:, bass.ds(j, 1), 0:D].rearrange("p a d -> p (a d)"), y_ring[:, par]).then_inc(xs_copied, 1)
                act.wait_ge(yT_made, j + 3)
                a_.copy(yT[:, par], psum[:, 4 + par, 0:D].rearrange("p (a n) -> p a n", a=KC)).then_inc(yT_copied, 1)
            pairs(act, NT, copy_y)
            root(4)
            act.wait_ge(dve_to_act, 5)
            a_.activation(rt[0], rt[0], ACT.Exp).then_inc(act_to_dve, 1)

            def gelu(i, par):
                for n in range(2):
                    act.wait_ge(h_pre, 2 * i + n + 1)
                    half = h_sb[:, par, n * 512:(n + 1) * 512]
                    a_.activation(half, half, ACT.Gelu).then_inc(h_act, 1)

            def copy_hT(i, par):
                act.wait_ge(hT_made, 2 * i + 2)
                a_.copy(hT[:, par, 4:8], psum[:, 4].rearrange("p (c n) -> p c n", c=4)).then_inc(hT_copied, 1)

            gelu(0, 0)
            with act.Fori(0, FT // 2 - 1) as turn:
                gelu(2 * turn + 1, 1)
                copy_hT(2 * turn, 0)
                gelu(2 * turn + 2, 0)
                copy_hT(2 * turn + 1, 1)
            gelu(FT - 1, 1)
            copy_hT(FT - 2, 0)
            copy_hT(FT - 1, 1)

        @block.tensor
        def _(pe):
            t_ = nc.tensor
            for s_, n in ((xt_made, 2), (stab_made, 2), (ctx_added, 2), (oha_used, 2), (spread_made, 2),
                          (sum_made, 8), (mix_made, 2), (yT_made, 2)):
                pe.sem_inc(s_, n)

            def mm(o, lhsT, rhs, first=True, last=True, **kw):
                return t_.matmul(o, lhsT, rhs, start=first, stop=last, **kw)

            pe.wait_ge(dve_to_pe, 1)
            mm(psum[0:NT - 1, 0, 0:1], cnt[:, 0:NT - 1], ones[:, 0:1]).then_inc(pe_to_dve, 1)
            pe.wait_ge(dve_to_pe, 2)
            mm(psum[:, 1, 0:IT], ones[0:NT - 1, :], lt[0:NT - 1, :]).then_inc(pe_to_dve, 1)
            pe.wait_ge(dve_to_pe, 3)
            for n, bank in ((0, 2), (1, 3), (2, 4)):
                for c in range(TC):
                    last = mm(psum[:, bank, 0:IT], e_f[:, n, c, :], spread[:, c], c == 0, c == TC - 1)
            last.then_inc(pe_to_dve, 1)

            pe.wait_ge(dve_to_pe, 4)
            for m in range(KC):
                for r in range(R):
                    for c in range(KC):
                        lo = m * 2 * R * H + r * 2 * H
                        last = mm(psum[:, 5, lo:lo + 2 * H], wrel_sb[:, r, c, m * P:(m + 1) * P], ablock[:, c], c == 0, c == KC - 1)
            last.then_inc(pe_to_dve, 1)
            pe.wait_ge(dve_to_pe, 5)

            pe.wait_ge(pool_const, 1)

            def turn_x(j, par):
                pe.wait_ge(xn_made, j + 1)
                pe.wait_ge(xt_copied, j + 1)
                for a in range(KC):
                    last = t_.transpose(psum[:, 6 + par, a * P:(a + 1) * P], xn_ring[:, par, a * P:(a + 1) * P], ident)
                last.then_inc(xt_made, 1)

            def scores(j, par):
                pe.wait_ge(xt_copied, j + 3)
                pe.wait_ge(stab_copied, j + 1)
                for c in range(KC):
                    last = mm(psum[:, par, 0:2 * R * H], xs_ring[:, par, c], wa_sb[:, c], c == 0, c == KC - 1)
                last.then_inc(stab_made, 1)

            turn_x(0, 0)
            with pe.Fori(0, NT // 2) as turn:
                turn_x(2 * turn + 1, 1)
                scores(2 * turn, 0)
                turn_x(2 * turn + 2, 0)
                scores(2 * turn + 1, 1)
            scores(NT - 1, 0)

            pe.wait_ge(stab_copied, NT + 2)
            pe.wait_ge(in_wt, 48)
            mm(psum[:, 6, :], zrow[0:1, 0:P], zrow[0:1, :], skip_group_check=True)

            def node_tile(j, par, rows_=P):
                pe.wait_ge(xs_made, j + 1)
                xt = xs_ring[:, par]
                pe.wait_ge(kv_ready, j + 1)
                pe.wait_ge(q_read, j + 1)
                for c in range(KC):
                    last = mm(psum[:, 4, :], xt[:, c], wmix_sb[:, c, 0:2 * D], c == 0, c == KC - 1)
                last.then_inc(kv_made, 1)
                for a in range(KC):
                    for c in range(KC):
                        last = mm(psum[:, 5, a * P:(a + 1) * P], wmix_sb[:, c, 2 * D + a * P:2 * D + (a + 1) * P], xt[:, c], c == 0, c == KC - 1)
                last.then_inc(q_made, 1)
                for n in range(4):
                    pe.wait_ge(h_copied, 4 * j + n + 1)
                    for c in range(KC):
                        last = mm(psum[:, n, :], xt[:, c], wrt_sb[:, c, n * 512:(n + 1) * 512], c == 0, c == KC - 1)
                    last.then_inc(h_made, 1)
                pe.wait_ge(kv_ready, j + 2)
                for a in range(KC):
                    k_a, v_a = kv_sb[0:rows_, par, a * P:(a + 1) * P], kv_sb[0:rows_, par, D + a * P:D + (a + 1) * P]
                    mm(psum[:, 6, a * P:(a + 1) * P], v_a, k_a, False, False, skip_group_check=True)
                    last = mm(psum[:, 6, D + a:D + a + 1], k_a, ones[0:rows_, 0:1], False, False, skip_group_check=True)
                last.then_inc(ctx_added, 1)

            with pe.Fori(0, NT // 2) as turn:
                node_tile(2 * turn, 0)
                node_tile(2 * turn + 1, 1)
            node_tile(NT - 1, 0, LASTN)

            pe.wait_ge(dve_to_pe, 6)
            for a in range(KC):
                last = mm(psum[:, 7, a * D:(a + 1) * D], ctxT[:, a], wp_sb[:, a])
            last.then_inc(pe_to_dve, 1)

            pe.wait_ge(in_misc, 16 * 5)
            pe.wait_ge(h_copied, 4 * NT + 4)
            for e in range(X):
                pe.wait_ge(w1_in[e % 2], 16 * (e // 2 + 1))
                if e:
                    pe.wait_ge(b1_added, e)
                for n in range(2):
                    for c in range(KC):
                        last = mm(psum[0:1, n, :], ln_cols[:, 1, e, c:c + 1], w1e[:, e % 2, c, n * 512:(n + 1) * 512], c == 0, c == KC - 1)
                last.then_inc(w1_used, 1)
            pe.wait_ge(dve_to_pe, 7)
            pe.wait_ge(b1_added, X)

            def turn_one_hot(i, par):
                pe.wait_ge(oha_made, i + 1)
                pe.wait_ge(ohT_made, i + 1)
                for k in range(G):
                    to = psum[:, 2 * par + k // 8, (k % 8) * 64:(k % 8 + 1) * 64].bitcast(BF16)
                    last = t_.transpose(to, oh_a[:, par, k], eye_b[:])
                last.then_inc(oha_used, 1)

            def spread_scores(i, par):
                blocks = load_values(ENG.PE, blk[0:1, bass.ds(i * G, G)], NT - 1)
                pe.wait_ge(ohT_made, i + 3)
                pe.wait_ge(spread_used, i + 1)
                for k in range(G):
                    last = mm(psum[:, 4 + 2 * par + k // 8, (k % 8) * 64:(k % 8 + 1) * 64], ohT[:, par, k],
                              s_dtab[:, bass.ds(blocks[k], 1), :].rearrange("p a s -> p (a s)"))
                last.then_inc(spread_made, 1)

            turn_one_hot(0, 0)
            with pe.Fori(0, NG // 2 - 1) as turn:
                turn_one_hot(2 * turn + 1, 1)
                spread_scores(2 * turn, 0)
                turn_one_hot(2 * turn + 2, 0)
                spread_scores(2 * turn + 1, 1)
            turn_one_hot(NG - 1, 1)
            spread_scores(NG - 2, 0)
            spread_scores(NG - 1, 1)

            NB = -(-J // 4)
            pe.wait_ge(dve_to_pe, 8)
            n = 0
            for table in (s_all, d_all):
                for b in range(NB):
                    if n >= 8:
                        pe.wait_ge(tr_copied, n - 7)
                    for k in range(min(4, J - 4 * b)):
                        last = t_.transpose(psum[:, n % 8, k * P:(k + 1) * P], table[:, :, :, 4 * b + k].rearrange("p h c -> p (h c)"), ident)
                    last.then_inc(tr_made, 1)
                    n += 1
            pe.wait_ge(dve_to_pe, 9)
            mm(psum[:, 0, 0:1], shift_up, sc2[:, L - 1:L]).then_inc(pe_to_dve, 1)
            pe.wait_ge(dve_to_pe, 10)
            mm(psum[:, 1, 0:1], shift_down, keep[:, 0:1]).then_inc(pe_to_dve, 1)
            pe.wait_ge(dve_to_pe, 11)
            mm(psum[0:1, 2, 0:P], carry[:, 1:2], ident)
            mm(psum[0:1, 2, P:2 * P], carry[:, 2:3], ident).then_inc(pe_to_dve, 1)
            asked = 11
            for back in (0, 1, 0, 1):
                pe.wait_ge(dve_to_pe, asked + 1)
                mm(psum[0:1, 3, 0:P], carry[:, 0:1], ident).then_inc(pe_to_dve, 1)
                pe.wait_ge(dve_to_pe, asked + 2)
                mm(psum[:, 4, 0:1], rows[0:1, 3, back:back + P], ones[0:1, 0:1]).then_inc(pe_to_dve, 1)
                asked += 2
            pe.wait_ge(dve_to_pe, 20)
            for b in range(NB):
                for k in range(min(4, J - 4 * b)):
                    last = t_.transpose(psum[:, b % 8, k * P:(k + 1) * P], score[:, (4 * b + k) * P:(4 * b + k + 1) * P], ident)
                last.then_inc(tr_made, 1)
            pe.wait_ge(tr_copied, 3 * NB)

            def sum_rows(i, par):
                for q in range(4):
                    pe.wait_ge(msg_made, 4 * i + q + 1)
                    pe.wait_ge(sum_added, 4 * i + q + 1)
                    for k in range(4 * q, 4 * q + 4):
                        last = mm(psum[:, k // 2, (k % 2) * D:(k % 2 + 1) * D], oh_b[:, k], ring[:, par, k])
                    last.then_inc(sum_made, 1)
            pairs(pe, NG, sum_rows)

            pe.wait_ge(dve_to_pe, 21)

            def denominators(j, par):
                if not isinstance(j, int):
                    pe.wait_ge(qr_made, j)
                for a in range(KC):
                    last = mm(psum[:, 0, a * P:(a + 1) * P], kb_sb[:, a], qT[:, a, bass.ds(j * P, P)])
                last.then_inc(den_made, 1)

            def mix(j, par):
                pe.wait_ge(qr_made, j + 1)
                pe.wait_ge(x1_made, j + 1)
                for a in range(KC):
                    last = mm(psum[:, 1 + par, 0:D], qr[:, par, a], m_sb[:, a], a == 0, a == KC - 1)
                last.then_inc(mix_made, 1)

            denominators(0, 0)
            with pe.Fori(0, NT // 2) as turn:
                denominators(2 * turn + 1, 1)
                mix(2 * turn, 0)
                denominators(2 * turn + 2, 0)
                mix(2 * turn + 1, 1)
            mix(NT - 1, 0)

            def turn_y(j, par):
                pe.wait_ge(yr_made, j + 1)
                pe.wait_ge(yT_copied, j + 1)
                for a in range(KC):
                    last = t_.transpose(psum[:, 4 + par, a * P:(a + 1) * P], y_ring[:, par, a * P:(a + 1) * P], ident)
                last.then_inc(yT_made, 1)

            def logits(j, par):
                pe.wait_ge(yT_copied, j + 3)
                for c in range(KC):
                    last = mm(psum[:, 3, bass.ds(j * X, X)], yT[:, par, c], wr_sb[:, c], c == 0, c == KC - 1)
                return last

            turn_y(0, 0)
            with pe.Fori(0, NT // 2) as turn:
                turn_y(2 * turn + 1, 1)
                logits(2 * turn, 0)
                turn_y(2 * turn + 2, 0)
                logits(2 * turn + 1, 1)
            logits(NT - 1, 0).then_inc(pe_to_dve, 1)
            pe.wait_ge(dve_to_pe, 22)
            mm(psum[:, 4, 0:NT * X], upper, rt[4])
            mm(psum[:, 5, 0:NT * X], ones[:], rt[4]).then_inc(pe_to_dve, 1)

            pe.wait_ge(w1_loaded, 16 * X)
            pe.wait_ge(w2_loaded, 16)

            def turn_rows(i, par, turn):
                pe.wait_ge(xg_in[par], 48 * (turn + 1))
                if not isinstance(i, int) or i:
                    pe.wait_ge(xgT_copied, i)
                for a in range(KC):
                    last = t_.transpose(psum[:, 0, a * P:(a + 1) * P], xg[:, par, a * P:(a + 1) * P], ident)
                last.then_inc(xgT_made, 1)

            def hidden(i, par, e_reg):
                pe.wait_ge(xgT_copied, i + 1)
                if not isinstance(i, int) or i:
                    pe.wait_ge(h_pre, 2 * i)
                for n in range(2):
                    for c in range(KC):
                        last = mm(psum[:, 1 + n, :], xgT[:, par, c],
                                  w1_sb[:, bass.ds(e_reg, 1), c, n * 512:(n + 1) * 512].rearrange("p a f -> p (a f)"), c == 0, c == KC - 1)
                    last.then_inc(f1_made, 1)

            def turn_hidden(i, par):
                for n in range(2):
                    pe.wait_ge(h_act, 2 * i + n + 1)
                    for c in range(4):
                        last = t_.transpose(psum[:, 3 + n, c * P:(c + 1) * P], h_sb[:, par, (4 * n + c) * P:(4 * n + c + 1) * P], ident)
                    last.then_inc(hT_made, 1)

            def project(i, par, e_reg):
                pe.wait_ge(hT_copied, 2 * i + 2)
                pe.wait_ge(tile_done, i + 2)
                for c in range(FC):
                    last = mm(psum[:, 5, 0:D], hT[:, par, c], w2_sb[:, bass.ds(e_reg, 1), c, :].rearrange("p a d -> p (a d)"), c == 0, c == FC - 1)
                last.then_inc(f2_made, 1)

            pe.wait_ge(xg_in[0], 48)
            turn_rows(0, 0, 0)
            first = load_values(ENG.PE, ftab[0:1, 0:1], X - 1)
            hidden(0, 0, first[0])
            with pe.Fori(0, FT // 2 - 1) as turn:
                e3 = load_values(ENG.PE, ftab[0:1, bass.ds(2 * turn, 3)], X - 1)
                turn_rows(2 * turn + 1, 1, turn)
                hidden(2 * turn + 1, 1, e3[1])
                turn_hidden(2 * turn, 0)
                project(2 * turn, 0, e3[0])
                turn_rows(2 * turn + 2, 0, turn + 1)
                hidden(2 * turn + 2, 0, e3[2])
                turn_hidden(2 * turn + 1, 1)
                project(2 * turn + 1, 1, e3[1])
            e2 = load_values(ENG.PE, ftab[0:1, FT - 2:FT], X - 1)
            turn_rows(FT - 1, 1, FT // 2 - 1)
            hidden(FT - 1, 1, e2[1])
            turn_hidden(FT - 2, 0)
            project(FT - 2, 0, e2[0])
            turn_hidden(FT - 1, 1)
            project(FT - 1, 1, e2[1])


def kernel(x, src, dst, edge_type_8, L0_gnn_W, L0_gnn_attn_src, L0_gnn_attn_dst, L0_mix_Wq, L0_mix_Wkv,
           L0_mix_Wproj, L0_mix_bproj, L0_ffn_Wr, L0_ffn_br, L0_ffn_ln_g, L0_ffn_ln_b, L0_ffn_W1,
           L0_ffn_b1, L0_ffn_W2, L0_ffn_b2):
    import concourse.bacc as bacc
    from concourse.bass_utils import run_bass_kernel_spmd

    def chunks(a):
        return a.reshape(-1, P, a.shape[-1]).transpose(1, 0, 2)

    w = np.asarray(L0_gnn_W)
    att = np.stack([np.asarray(L0_gnn_attn_src).reshape(-1), np.asarray(L0_gnn_attn_dst).reshape(-1)], 1)
    wkv, wq = np.asarray(L0_mix_Wkv), np.asarray(L0_mix_Wq)
    arrays = {
        "x": np.asarray(x), "src": np.asarray(src), "dst": np.asarray(dst), "etype": np.asarray(edge_type_8),
        "w_rel": w.reshape(R, KC, P, D).transpose(2, 0, 1, 3),
        "w_rel_t": chunks(w.transpose(2, 0, 1).reshape(D, R * D)),
        "attn": chunks(att),
        "wmix_t": chunks(np.concatenate([wkv, wq], 0).T),
        "wp_t": chunks(np.asarray(L0_mix_Wproj).T),
        "bproj": np.asarray(L0_mix_bproj).reshape(1, D),
        "wr": chunks(np.asarray(L0_ffn_Wr)),
        "br": np.asarray(L0_ffn_br).reshape(1, X),
        "ln_g": np.asarray(L0_ffn_ln_g).reshape(X, KC, P).transpose(2, 0, 1),
        "ln_b": np.asarray(L0_ffn_ln_b).reshape(X, KC, P).transpose(2, 0, 1),
        "w1": np.asarray(L0_ffn_W1).reshape(X, KC, P, F).transpose(0, 2, 1, 3).reshape(X, P, KC * F),
        "b1": np.asarray(L0_ffn_b1),
        "w2": np.asarray(L0_ffn_W2).reshape(X, FC, P, D).transpose(2, 0, 1, 3),
        "b2": np.asarray(L0_ffn_b2),
    }
    arrays = {f"in_{k}": np.ascontiguousarray(a) for k, a in arrays.items()}
    nc = bacc.Bacc("TRN2", target_bir_lowering=False, num_devices=1)
    args = [nc.dram_tensor(k, a.shape, mybir.dt.from_np(a.dtype), kind="ExternalInput").ap() for k, a in arrays.items()]
    args.append(nc.dram_tensor("out", [N + P, D], F32, kind="ExternalOutput").ap())
    gps_layer(nc, *args)
    r = run_bass_kernel_spmd(nc, [arrays], core_ids=[0])
    return r.results[0]["out"][0:N]
```

```python
from contextlib import ExitStack

import numpy as np

import concourse.bass as bass
from concourse import mybir

F32 = mybir.dt.float32
BF16 = mybir.dt.bfloat16
I32 = mybir.dt.int32
U32 = mybir.dt.uint32
ALU = mybir.AluOpType
ACT = mybir.ActivationFunctionType
AX = mybir.AxisListType.X
ENG = mybir.EngineType

P = 128
N, E, D = 3125, 50000, 256
R, H, DH = 8, 8, 32
X, F, TOPK = 8, 1024, 2
KC = D // P
NT = -(-N // P)
NP = NT * P
LASTN = N - (NT - 1) * P
TE = -(-E // P)
LASTE = E - (TE - 1) * P
TC = -(-TE // P)
CH = P // H
G = 16
IT = -(-(TE - 1 + NT) // G) * G
NG = IT // G
RING = 5
J = IT // CH
L = J * P
XR = NP + P
FT = (N * TOPK - X) // P + X
FT += -FT % 4
XW = D + 4
FC = F // P
LN_EPS = 1e-5
assert IT % CH == 0 and NG % 2 == 0 and NT % 2 == 1 and FT % 4 == 0

WORDS = 51200


class Chain:

    def __init__(self, eng, sem):
        self.eng, self.sem, self.base, self.k, self.per = eng, sem, 0, 0, 0

    def __call__(self, ins):
        self.k += 1
        ins.then_inc(self.sem, 1)
        return ins

    def settle(self, back=0):
        self.eng.wait_ge(self.sem, self.base + self.k - back)

    def enter(self, turn, per):
        if self.k and isinstance(self.base, int) and not self.per:
            self.base, self.k = self.base + self.k, 0
        self.start, self.per = self.base, per
        self.base, self.k = self.start + turn * per, 0

    def leave(self, turns):
        assert self.k == self.per, (self.k, self.per)
        self.base, self.k, self.per = self.start + turns * self.per, 0, 0


def gps_layer(nc, x, src, dst, etype, w_rel, w_rel_t, attn, wmix_t, wp_t, bproj,
              wr, br, ln_g, ln_b, w1, b1, w2, b2, out):
    s_tab = nc.dram_tensor("source_scores", [NP * R, H], F32, kind="Internal").ap()
    h_tab = nc.dram_tensor("node_rows", [NP * R, D], F32, kind="Internal").ap()
    bias_d = nc.dram_tensor("expert_bias", [X, F], F32, kind="Internal").ap()
    x_rows = nc.dram_tensor("expert_rows", [X * XR + P, XW], F32, kind="Internal").ap()

    ctx = ExitStack()
    with ctx:
        def sb(name, shape, dt=F32):
            return ctx.enter_context(nc.sbuf_tensor(name, shape, dt))

        def sem(name):
            return ctx.enter_context(nc.semaphore(name))

        arena = sb("arena", [P, WORDS])

        def at(lo, *shape, dt=F32):
            n = int(np.prod(shape))
            view = arena[:, lo:lo + (n // 2 if dt == BF16 else n)]
            if dt != F32:
                view = view.bitcast(dt)
            names = "abcd"[:len(shape)]
            if len(shape) > 1:
                view = view.rearrange(f"p ({' '.join(names)}) -> p {' '.join(names)}",
                                      **dict(zip(names[1:], shape[1:])))
            return view

        A0 = NT * D
        ACC = A0 + X * KC * F
        QT = ACC + NT * D
        B0 = QT + KC * NP
        Z0 = ACC + X * FC * D
        x_sb = at(0, NT, D)
        qT = at(QT, KC, NP)
        xnT = at(A0, KC, NP)
        wrt_sb = at(A0 + 6400, KC, R * D)
        wmix_sb = at(A0 + 10496, KC, 3 * D)
        wp_sb = at(A0 + 12032, KC, D)
        ctxT = at(A0 + 12544, KC, P)
        xs_ring = at(A0 + 12800, 2, KC, P)
        s_dtab = at(A0 + 14592, NT, R * H)
        wrel_sb = at(QT, R, KC, D)
        h_out = at(ACC, 2, R * D)
        kv_sb = at(ACC + 4096, 2, 2 * D)
        k_low = at(ACC + 5120, D)
        q_low = at(ACC + 5376, KC, P)
        q_high = at(ACC + 5632, KC, P)
        s_out = at(B0, NT, R * H)
        e_raw = at(B0 + 1600, 3, TC, P, dt=I32)
        e_f = at(B0 + 3136, 3, TC, P)
        spread = at(B0 + 4672, TC, IT)
        qr = at(B0 + 1600, 2, KC, P)
        q_inv = at(B0 + 2112, 2, KC, P)
        xn_ring = at(B0 + 6400, 2, D)
        lt = at(B0 + 6912, IT)
        cnt = at(B0 + 7328, NT)
        t_it = at(B0 + 7392, IT)
        cnt_i = lt.bitcast(U32)
        stats = at(B0 + 7808, NT, 6)
        oh_a = at(A0, 2, G, P, dt=BF16)
        ohT = at(A0 + 2048, 2, G, P, dt=BF16)
        s_parts = at(A0 + 4096, NT, 3, R * H, dt=BF16)
        s_rest = at(A0 + 7168, NT, R * H)
        tmp_s = at(A0 + 14592, G, R * H)
        rmask = at(A0 + 7168, IT, R)
        s_dst = at(A0 + 10496, IT, H)
        s_src = at(B0 + 10240, IT, H)
        sg = at(B0 + 13568, 2, G, H)
        typ = at(B0 + 13824, IT)
        m_sb = at(B0 + 14784, KC, D)
        kb_sb = at(B0 + 15296, KC, P)
        s_all = at(A0, H, CH, J)
        score = at(A0 + 3328, L)
        keep = at(A0 + 6656, L + 1)
        sc2 = at(A0 + 9992, L)
        sc1 = at(A0, L)
        ring = at(ACC + 384, RING, G, D)
        oh_b = at(B0 + 8192, G, P)
        w_i = at(B0 + 10240, CH, J, H)
        xs = at(Z0, NT, XW)
        xs_pad = at(Z0 + NT * XW, XW)
        y_ring = at(Z0 + 26 * XW, 2, D)
        yT = at(Z0 + 26 * XW + 512, 2, KC, P)
        b1_row = at(Z0 + 26 * XW + 704, F)
        Z1 = Z0 + 26 * XW + 1792
        rt = [at(Z1 + n * NT * X, NT * X) for n in range(9)]
        small = [at(Z1 + 9 * NT * X + n * NT, NT) for n in range(14)]
        w1_sb = at(A0, X, KC, F)
        w2_sb = at(ACC, X, FC, D)
        xg = at(Z0, 4, XW)
        xgT = at(Z0 + 1040, 2, KC, P)
        bias_r = at(Z0 + 1552, 4, F + D)
        h_sb = at(Z0 + 6672, 2, F)
        hT = at(Z0 + 8720, 2, FC, P)
        y_out = at(Z0 + 10768, 2, D)
        y_b2 = at(Z0 + 11280, D)
        tok_u = at(Z0 + 11536, 2).bitcast(U32)
        assert Z1 + 9 * NT * X + 14 * NT <= B0 + 14784

        eye = sb("eye", [P, P + 2])
        ident, shift_up, shift_down = eye[:, 1:P + 1], eye[:, 0:P], eye[:, 2:P + 2]
        eye_b = sb("eye_b", [P, P], BF16)
        iota_r = sb("iota_r", [P, P])
        pcol = sb("pcol", [P, TC])
        ones = sb("ones", [P, P])
        idx_i = sb("idx_i", [P, IT], U32)
        idx_r = sb("idx_r", [P, RING, G], U32)
        dl = sb("dl", [P, IT])
        blk = sb("blk", [1, IT], I32)
        hmask = sb("hmask", [P, KC, H])
        wa_sb = at(B0 + 8192, KC, 2 * R * H)
        att_sb = at(B0 + 8448, KC, 2)
        ablock = at(B0 + 8464, KC, 2 * H)
        misc = at(B0 + 8512, 1024)
        ln_cols = at(B0 + 15296, 2, X, KC)
        bdm = at(B0 + 9600, P)
        zrow = at(B0 + 9728, 512)
        wr_sb = at(B0 + 15552, KC, X)
        br_sb = at(B0 + 15568, X)
        stx = sb("stx", [P, 4, NT])
        carry = sb("carry", [P, 4])
        ftab = at(B0 + 15124, 2 * FT + 8, dt=I32)[0:1]
        rows = at(B0 + 8192, 4, P + 1)
        psum = ctx.enter_context(nc.psum_tensor("psum", [P, 8, 512], F32))

        d_all = at(B0 + 10240, H, CH, J)
        slot_u = [m.bitcast(U32) for m in (small[11], small[12])]

        upper = at(Z0 + 26 * XW + 512, P)
        gt = at(Z0 + 26 * XW, FT, X - 1)
        stats_z = at(Z1 + 8 * NT * X, NT, 6)

        fill_done = sem("fill_done")
        in_edges, in_att, in_x, in_wrel, in_wt, in_misc = map(
            sem, ("in_edges", "in_att", "in_x", "in_wrel", "in_wt", "in_misc"))
        pool_const = sem("pool_const")
        dve_step, act_step, pool_step = map(sem, ("dve_step", "act_step", "pool_step"))
        pool_turn = sem("pool_turn")
        dve_to_pe, pe_to_dve = sem("dve_to_pe"), sem("pe_to_dve")
        dve_to_act, act_to_dve = sem("dve_to_act"), sem("act_to_dve")
        pe_to_act, act_to_pe = sem("pe_to_act"), sem("act_to_pe")
        items_ready = sem("items_ready")
        xn_made = sem("xn_made")
        xt_made, xt_copied = sem("xt_made"), sem("xt_copied")
        stab_made, stab_copied = sem("stab_made"), sem("stab_copied")
        stab_stored = sem("stab_stored")
        xs_made = sem("xs_made")
        kv_made, kv_read, kv_ready, ctx_added = map(sem, ("kv_made", "kv_read", "kv_ready", "ctx_added"))
        q_made, q_read = sem("q_made"), sem("q_read")
        low_ready, exp_ready = sem("low_ready"), sem("exp_ready")
        h_made, h_copied = sem("h_made"), sem("h_copied")
        h_stored = [sem("h_stored0"), sem("h_stored1")]
        b1_in, b1_out, w1_scaled = sem("b1_in"), sem("b1_out"), sem("w1_scaled")
        w1_used, b1_added = sem("w1_used"), sem("b1_added")
        tr_made, tr_copied = sem("tr_made"), sem("tr_copied")
        sg_in = [sem("sg_in0"), sem("sg_in1")]
        s_src_ready = sem("s_src_ready")
        oha_made, oha_used, ohT_made, spread_made, spread_used = map(
            sem, ("oha_made", "oha_used", "ohT_made", "spread_made", "spread_used"))
        rows_in = [sem(f"rows_in{n}") for n in range(RING)]
        ohb_made, msg_made, sum_made, sum_added = map(sem, ("ohb_made", "msg_made", "sum_made", "sum_added"))
        w1_loaded, w2_loaded = sem("w1_loaded"), sem("w2_loaded")
        qr_made, mix_made, mix_added, x1_ready, yr_made, yr_used, yT_made, yT_copied, xs_copied = map(
            sem, ("qr_made", "mix_made", "mix_added", "x1_ready", "yr_made", "yr_used", "yT_made", "yT_copied", "xs_copied"))
        den_made, ln_loaded, xs_normed = sem("den_made"), sem("ln_loaded"), sem("xs_normed")
        out_init = sem("out_init")
        send_ready, sent = sem("send_ready"), sem("sent")
        acc_free = sem("acc_free")
        xg_in = [sem(f"xg_in{n}") for n in range(4)]
        tile_done = sem("tile_done")
        xgT_made, xgT_copied, f1_made, h_pre, h_act, hT_made, hT_copied, f2_made = map(
            sem, ("xgT_made", "xgT_copied", "f1_made", "h_pre", "h_act", "hT_made", "hT_copied", "f2_made"))
        y_free = sem("y_free")
        y_added = [sem("y_added0"), sem("y_added1")]

        def load_values(eng, row, hi):
            return nc.values_load_multi_w_load_instructions(
                row, engines=[eng], min_val=0, max_val=hi,
                skip_runtime_bounds_check_because="the program works these out itself, in range for any input",
            )[1]

        def pairs(eng, n, body):
            with eng.Fori(0, n // 2) as turn:
                body(2 * turn, 0)
                body(2 * turn + 1, 1)
            if n % 2:
                body(n - 1, 0)

        block = ctx.enter_context(nc.Block())

        @block.sync
        def _(sp):
            sp.wait_ge(fill_done, 1)
            full = (TE - 1) // P
            sp.dma_start(att_sb, attn).then_inc(in_att, 16)
            for n, a in enumerate((dst, src, etype)):
                sp.dma_start(e_raw[:, n, 0:full, :], a[0:full * P * P].rearrange("(c t e) -> t c e", t=P, e=P)).then_inc(in_edges, 16)
                rest = TE - 1 - full * P
                sp.dma_start(e_raw[0:rest, n, full, :], a[full * P * P:(TE - 1) * P].rearrange("(t e) -> t e", e=P)).then_inc(in_edges, 16)
                sp.dma_start(e_raw[rest:rest + 1, n, full, 0:LASTE], a[(TE - 1) * P:E].rearrange("(t e) -> t e", t=1)).then_inc(in_edges, 16)
            sp.dma_start(wrel_sb, w_rel).then_inc(in_wrel, 16)
            sp.dma_start(x_sb[:, 0:NT - 1, :], x[0:(NT - 1) * P, :].rearrange("(j p) d -> p j d", p=P)).then_inc(in_x, 16)
            sp.dma_start(x_sb[0:LASTN, NT - 1, :], x[(NT - 1) * P:N, :]).then_inc(in_x, 16)
            sp.dma_start(wrt_sb, w_rel_t).then_inc(in_wt, 16)
            sp.dma_start(wmix_sb, wmix_t).then_inc(in_wt, 16)
            sp.dma_start(wp_sb, wp_t).then_inc(in_wt, 16)
            sp.dma_start(wr_sb, wr).then_inc(in_misc, 16)
            sp.dma_start(br_sb, br.broadcast_to([P, X])).then_inc(in_misc, 16)
            sp.dma_start(misc[:, 0:D], bproj.broadcast_to([P, D])).then_inc(in_misc, 16)
            sp.wait_ge(stab_copied, NT + 2)
            sp.dma_start(s_tab.rearrange("(j p r) h -> p j (r h)", p=P, r=R), s_out).then_inc(stab_stored, 16)

            h_view = h_tab.rearrange("(j p r) d -> j p (r d)", p=P, r=R)

            def store_rows(j, par):
                sp.wait_ge(h_copied, 4 * j + 8)
                sp.dma_start(h_view[bass.ds(j, 1)].rearrange("a p w -> (a p) w"), h_out[:, par]).then_inc(h_stored[par], 16)
            pairs(sp, NT, store_rows)
            sp.wait_ge(mix_added, NT + 2)
            sp.dma_start(ln_cols[:, 0], ln_g).then_inc(ln_loaded, 16)
            sp.dma_start(ln_cols[:, 1], ln_b).then_inc(ln_loaded, 16)
            sp.wait_ge(acc_free, 1)
            for e in range(X):
                sp.dma_start(w1_sb[:, e], w1[e].rearrange("p (c f) -> p c f", c=KC)).then_inc(w1_loaded, 16)
            sp.wait_ge(x1_ready, 1)
            sp.dma_start(out[0:(NT - 1) * P, :].rearrange("(j p) d -> p j d", p=P), x_sb[:, 0:NT - 1, :]).then_inc(out_init, 16)
            sp.dma_start(out[(NT - 1) * P:N, :], x_sb[0:LASTN, NT - 1, :]).then_inc(out_init, 16)
            sp.dma_start(w2_sb, w2).then_inc(w2_loaded, 16)
            sp.wait_ge(send_ready, 1)
            sp.dma_start(out[N:N + P, :], xs_pad[:, 0:D]).then_inc(out_init, 16)
            sp.dma_start(x_rows[X * XR:X * XR + P, :], xs_pad).then_inc(out_init, 16)
            ends = load_values(ENG.SP, ftab[0:1, 2 * FT:2 * FT + X], X * XR)
            for e in range(X):
                sp.dma_start(x_rows[bass.ds(ends[e], P), :], xs_pad).then_inc(out_init, 16)
            for e in range(X):
                if e >= 1:
                    sp.wait_ge(b1_out, 16 * e)
                sp.dma_start(b1_row[0:1, :], b1[e:e + 1, :]).then_inc(b1_in, 16)
                sp.wait_ge(b1_added, e + 1)
                sp.dma_start(bias_d[e:e + 1, :], b1_row[0:1, :]).then_inc(b1_out, 16)
            sp.wait_ge(b1_out, 16 * X)
            sp.wait_ge(sent, 16 * 2 * NT)
            sp.wait_ge(out_init, 16 * (4 + X))

            with sp.Fori(0, FT // 4) as turn:
                e_regs = load_values(ENG.SP, ftab[0:1, bass.ds(4 * turn, 4)], X - 1)
                r_regs = load_values(ENG.SP, ftab[0:1, bass.ds(4 * turn + FT, 4)], X * XR)
                for n in range(4):
                    sp.wait_ge(tile_done, 4 * turn + n + 1)
                    sp.dma_start(xg[:, n], x_rows[bass.ds(r_regs[n], P), :]).then_inc(xg_in[n], 16)
                    sp.dma_start(bias_r[:, n, 0:F], bias_d[bass.ds(e_regs[n], 1), :].broadcast_to([P, F])).then_inc(xg_in[n], 16)
                    sp.dma_start(bias_r[:, n, F:F + D], b2[bass.ds(e_regs[n], 1), :].broadcast_to([P, D])).then_inc(xg_in[n], 16)

        @block.gpsimd
        def _(pool):
            step = Chain(pool, pool_step)
            g = nc.gpsimd
            step(g.memset(eye[:], 0.0))
            step(g.memset(hmask[:], 1.0))
            step(g.iota(iota_r[:], pattern=[[1, P]], base=0, channel_multiplier=0, allow_small_or_imprecise_dtypes=True))
            step(g.iota(pcol[:], pattern=[[P, TC]], base=0, channel_multiplier=1, allow_small_or_imprecise_dtypes=True))
            step(g.iota(t_it, pattern=[[1, IT]], base=0, channel_multiplier=0, allow_small_or_imprecise_dtypes=True))
            step.settle()
            step(g.affine_select(out=eye[:], in_=eye[:], compare_op=ALU.not_equal, fill=1.0, base=1,
                                 pattern=[[-1, P + 2]], channel_multiplier=1))
            step(g.affine_select(out=hmask[:], in_=hmask[:], compare_op=ALU.is_ge, fill=0.0, base=0,
                                 pattern=[[P, KC], [-DH, H]], channel_multiplier=1))
            step.settle()
            g.affine_select(out=hmask[:], in_=hmask[:], compare_op=ALU.is_ge, fill=0.0, base=DH - 1,
                            pattern=[[-P, KC], [DH, H]], channel_multiplier=-1).then_inc(pool_const, 1)

            pool.wait_ge(items_ready, 1)
            pool.wait_ge(stab_stored, 16)

            def take_indices(i, par):
                step(g.tensor_copy(idx_r[:, par], idx_i[:, bass.ds(i * G, G)]))
                step.settle()
                pool.sem_inc(pool_turn, 1)

            def gather_scores(i, par):
                take_indices(i, par)
                for k in range(G):
                    g.indirect_dma_start(out=sg[:, par, k, :], out_offset=None, in_=s_tab,
                                         in_offset=bass.IndirectOffsetOnAxis(ap=idx_r[:, par, k:k + 1], axis=0)
                                         ).then_inc(sg_in[par], 16)

            def keep_scores(i, turn, par):
                pool.wait_ge(sg_in[par], 16 * G * (turn + 1))
                step(g.tensor_copy(s_src[:, bass.ds(i * G, G), :], sg[:, par]))

            gather_scores(0, 0)
            with pool.Fori(0, NG // 2 - 1) as turn:
                step.enter(turn, 4)
                gather_scores(2 * turn + 1, 1)
                keep_scores(2 * turn, turn, 0)
                step.settle()
                gather_scores(2 * turn + 2, 0)
                keep_scores(2 * turn + 1, turn, 1)
                step.settle()
                step.leave(NG // 2 - 1)
            gather_scores(NG - 1, 1)
            keep_scores(NG - 2, NG // 2 - 1, 0)
            keep_scores(NG - 1, NG // 2 - 1, 1)
            step.settle()
            pool.sem_inc(s_src_ready, 1)

            pool.wait_ge(h_stored[0], 16 * ((NT + 1) // 2 + 1))
            pool.wait_ge(h_stored[1], 16 * (NT // 2 + 1))
            pool.wait_ge(mix_added, NT + 2)

            def gather_rows(i, par):
                pool.wait_ge(sum_made, 4 * i + 4)
                take_indices(i, par)
                for k in range(G):
                    g.indirect_dma_start(out=ring[:, par, k, :], out_offset=None, in_=h_tab,
                                         in_offset=bass.IndirectOffsetOnAxis(ap=idx_r[:, par, k:k + 1], axis=0)
                                         ).then_inc(rows_in[par], 16)

            with pool.Fori(0, NG // RING) as turn:
                step.enter(turn, RING)
                for n in range(RING):
                    gather_rows(RING * turn + n, n)
                step.leave(NG // RING)
            for i in range(NG // RING * RING, NG):
                gather_rows(i, i % RING)

            s1_u, s2_u = slot_u
            pool.wait_ge(send_ready, 1)
            pool.wait_ge(xs_normed, NT)
            for j in range(NT):
                n = P if j < NT - 1 else LASTN
                g.indirect_dma_start(out=x_rows, out_offset=bass.IndirectOffsetOnAxis(ap=s1_u[0:n, j:j + 1], axis=0),
                                     in_=xs[0:n, j, :], in_offset=None).then_inc(sent, 16)
            pool.wait_ge(send_ready, 2)
            for j in range(NT):
                n = P if j < NT - 1 else LASTN
                g.indirect_dma_start(out=x_rows, out_offset=bass.IndirectOffsetOnAxis(ap=s2_u[0:n, j:j + 1], axis=0),
                                     in_=xs[0:n, j, :], in_offset=None).then_inc(sent, 16)
            pool.wait_ge(out_init, 16 * (4 + X))

            with pool.Fori(0, FT // 2) as turn:
                for par in range(2):
                    pool.wait_ge(tile_done, 2 * turn + par + 5)
                    pool.sem_inc(pool_turn, 1)
                    g.indirect_dma_start(out=out, out_offset=bass.IndirectOffsetOnAxis(ap=tok_u[:, par:par + 1], axis=0),
                                         in_=y_out[:, par], in_offset=None, compute_op=ALU.add).then_inc(y_added[par], 16)
                    pool.wait_ge(y_added[par], 16 * (turn + 1))
                    pool.sem_inc(y_free, 1)


        @block.vector
        def _(dve):
            step = Chain(dve, dve_step)
            v = nc.vector
            dve.sem_inc(stab_copied, 2)
            dve.sem_inc(kv_ready, 1)
            dve.sem_inc(q_read, 1)
            dve.sem_inc(y_free, 2)
            dve.sem_inc(spread_used, 2)
            dve.sem_inc(sum_added, 4)
            dve.sem_inc(mix_added, 2)
            dve.sem_inc(tile_done, 4)

            step(v.memset(e_raw[:, 0, TC - 1, :], NP))
            step(v.memset(e_raw[:, 1, TC - 1, :], 0))
            step(v.memset(e_raw[:, 2, TC - 1, :], 0))
            step(v.memset(x_sb[:, NT - 1, :], 0.0))
            step.settle()
            dve.sem_inc(fill_done, 1)
            step(v.memset(ones[:], 1.0))
            step(v.memset(zrow, 0.0))

            dve.wait_ge(in_att, 16)
            dve.wait_ge(pool_const, 1)
            for c in range(KC):
                for w in range(2):
                    step(v.tensor_scalar(ablock[:, c, w * H:(w + 1) * H], hmask[:, c, :], att_sb[:, c, w:w + 1], None, ALU.mult))
            step.settle()
            dve.sem_inc(dve_to_pe, 1)

            dve.wait_ge(in_edges, 16 * 9)
            step(v.tensor_copy(e_f, e_raw))
            step.settle()
            for b in range(1, NT):
                step(v.tensor_scalar(spread[:, 0:2].rearrange("p c i -> p (c i)")[:, 0:TC * P], e_f[:, 0].rearrange("p c e -> p (c e)"),
                                     float(b * P), 0.0, ALU.is_lt, ALU.add, accum_out=cnt[:, b - 1:b]))
                step.settle()
            dve.sem_inc(dve_to_pe, 1)
            step(v.scalar_tensor_tensor(out=e_f[:, 1], in0=e_f[:, 1], scalar=float(R), in1=e_f[:, 2], op0=ALU.mult, op1=ALU.add))
            step(v.tensor_copy(eye_b[:], ident))
            dve.wait_ge(pe_to_dve, 2)
            fcol, fint = carry[0:NT - 1, 0:1], carry[0:NT - 1, 1:2].bitcast(I32)
            step(v.tensor_copy(fint, psum[0:NT - 1, 0, 0:1]))
            step.settle()
            step(v.tensor_scalar(fint, fint, 7, None, ALU.arith_shift_right))
            step.settle()
            step(v.tensor_copy(fcol, fint))
            step.settle()
            step(v.scalar_tensor_tensor(out=fcol, in0=fcol, scalar=1.0, in1=pcol[0:NT - 1, 0:1], op0=ALU.add, op1=ALU.add))
            step.settle()
            v.tensor_scalar(lt[0:NT - 1, :], t_it[0:NT - 1, :], fcol, None, ALU.is_ge).then_inc(dve_to_pe, 1)
            dve.wait_ge(pe_to_dve, 3)
            step(v.tensor_copy(blk[:], psum[0:1, 1, 0:IT]))
            step(v.tensor_copy(lt, psum[:, 1, 0:IT]))
            step.settle()
            step(v.tensor_tensor(t_it, t_it, lt, ALU.subtract))
            step.settle()
            for c in range(TC):
                step(v.tensor_scalar(spread[:, c], t_it, pcol[:, c:c + 1], None, ALU.is_equal))
            step.settle()
            dve.sem_inc(dve_to_pe, 1)
            def spread_of(mean, dev, out_stats):
                m0, m1, s0, s1 = (out_stats[:, :, c] for c in (1, 4, 2, 5))
                step(v.tensor_tensor(mean, m0, m1, ALU.add))
                step(v.tensor_tensor(stx[:, 3], m0, m1, ALU.subtract))
                step(v.tensor_tensor(dev, s0, s1, ALU.add))
                step.settle()
                step(v.tensor_scalar(mean, mean, 0.5, None, ALU.mult))
                step(v.tensor_tensor(stx[:, 3], stx[:, 3], stx[:, 3], ALU.mult))
                step(v.tensor_scalar(dev, dev, 1.0 / D, LN_EPS, ALU.mult, ALU.add))
                step.settle()
                step(v.scalar_tensor_tensor(out=dev, in0=stx[:, 3], scalar=0.25, in1=dev, op0=ALU.mult, op1=ALU.add))
                step.settle()

            def tile_of(t, j):
                return t[:, bass.ds(j, 1), :].rearrange("p a d -> p (a d)")

            def all_stats(to, t):
                with dve.Fori(0, NT // 5) as turn:
                    step.enter(turn, 5)
                    for n in range(5):
                        step(v.bn_stats(tile_of(to, 5 * turn + n), tile_of(t, 5 * turn + n)))
                    step.leave(NT // 5)
                step.settle()

            dve.wait_ge(in_x, 32)
            all_stats(stats, x_sb)
            spread_of(stx[:, 0], stx[:, 1], stats)
            dve.sem_inc(dve_to_act, 1)
            dve.wait_ge(act_to_dve, 1)
            step(v.reciprocal(stx[:, 2], stx[:, 1]))
            step.settle()

            dve.wait_ge(pe_to_dve, 4)
            step(v.tensor_copy(idx_i[:], psum[:, 3, 0:IT]))
            step(v.scalar_tensor_tensor(out=dl[:], in0=lt, scalar=float(-P), in1=psum[:, 2, 0:IT], op0=ALU.mult, op1=ALU.add))
            step.settle()
            step(v.tensor_scalar(cnt_i, idx_i[:], R - 1, None, ALU.bitwise_and))
            step.settle()
            step(v.tensor_copy(typ, cnt_i))
            for m in range(KC):
                step(v.tensor_copy(wa_sb[:, m].rearrange("p (w r h) -> p w r h", w=2, r=R),
                                   psum[:, 5, m * 2 * R * H:(m + 1) * 2 * R * H].rearrange("p (r w h) -> p w r h", w=2, r=R)))
            step.settle()
            dve.sem_inc(items_ready, 1)
            dve.sem_inc(dve_to_pe, 1)

            def normalise(j, par):
                dve.wait_ge(xt_made, j + 1)
                v.tensor_scalar(xn_ring[:, par], x_sb[:, bass.ds(j, 1), :].rearrange("p a d -> p (a d)"),
                                stx[:, 0, bass.ds(j, 1)], stx[:, 2, bass.ds(j, 1)],
                                ALU.subtract, ALU.mult).then_inc(xn_made, 1)

            def copy_stab(j, par):
                dve.wait_ge(stab_made, j + 3)
                step(v.tensor_copy(s_out[:, bass.ds(j, 1), :].rearrange("p a s -> p (a s)"), psum[:, par, 0:R * H]))
                v.tensor_copy(s_dtab[:, bass.ds(j, 1), :].rearrange("p a s -> p (a s)"),
                              psum[:, par, R * H:2 * R * H]).then_inc(stab_copied, 1)

            normalise(0, 0)
            normalise(1, 1)
            with dve.Fori(0, NT // 2 - 1) as turn:
                step.enter(turn, 2)
                normalise(2 * turn + 2, 0)
                copy_stab(2 * turn, 0)
                normalise(2 * turn + 3, 1)
                copy_stab(2 * turn + 1, 1)
                step.leave(NT // 2 - 1)
            normalise(NT - 1, 0)
            for j in range(NT - 3, NT):
                copy_stab(j, j % 2)
            step.settle()

            dve.wait_ge(in_misc, 16 * 3)
            dve.wait_ge(xt_made, NT + 2)
            step(v.tensor_tensor(x_sb, x_sb, misc[:, 0:D].unsqueeze(1).broadcast_to([P, NT, D]), ALU.add))
            step(v.tensor_copy(bdm.rearrange("p (h d) -> p h d", d=DH), hmask[:, 0, 0:P // DH].unsqueeze(2).broadcast_to([P, P // DH, DH])))
            step.settle()

            def kv_q(j, par):
                dve.wait_ge(kv_made, j + 1)
                step.settle()
                step(v.tensor_scalar(k_low, psum[:, 4, 0:D], 0.0, None, ALU.min))
                dve.wait_ge(q_made, j + 1)
                v.tensor_scalar(q_low, psum[:, 5, 0:D].rearrange("p (a n) -> p a n", a=KC), 0.0, None, ALU.min).then_inc(low_ready, 1)
                dve.wait_ge(ctx_added, j + 1)
                step(v.tensor_copy(kv_sb[:, par, D:2 * D], psum[:, 4, D:2 * D]))
                dve.wait_ge(exp_ready, j + 1)
                step.settle()
                v.scalar_tensor_tensor(out=kv_sb[:, par, 0:D], in0=psum[:, 4, 0:D], scalar=0.0, in1=k_low,
                                       op0=ALU.max, op1=ALU.add).then_inc(kv_ready, 1)
                step(v.scalar_tensor_tensor(out=qT[:, :, bass.ds(j * P, P)], in0=psum[:, 5, 0:D].rearrange("p (a n) -> p a n", a=KC),
                                            scalar=0.0, in1=q_low, op0=ALU.max, op1=ALU.add))
                step.settle()
                dve.sem_inc(q_read, 1)

            with dve.Fori(0, NT // 2) as turn:
                step.enter(turn, 6)
                kv_q(2 * turn, 0)
                kv_q(2 * turn + 1, 1)
                step.leave(NT // 2)
            kv_q(NT - 1, 0)

            dve.wait_ge(ctx_added, NT + 2)
            for a in range(KC):
                step(v.tensor_tensor(ctxT[:, a], psum[:, 6, a * P:(a + 1) * P], bdm, ALU.mult))
                step(v.tensor_scalar(kb_sb[:, a], bdm, psum[:, 6, D + a:D + a + 1], None, ALU.mult))
            step.settle()
            dve.sem_inc(dve_to_pe, 1)
            dve.wait_ge(pe_to_dve, 5)
            step(v.tensor_copy(m_sb, psum[:, 7].rearrange("p (a o) -> p a o", a=KC)))
            step.settle()
            dve.sem_inc(dve_to_pe, 1)

            def divide_q(j, par):
                dve.wait_ge(den_made, j + 1)
                dve.wait_ge(mix_made, j + 1)
                step(v.tensor_scalar(q_inv[:, par], psum[:, 3 * par, 0:D].rearrange("p (a n) -> p a n", a=KC), 1e-6, None, ALU.max))
                step.settle()
                step(v.reciprocal(q_inv[:, par], q_inv[:, par]))
                step.settle()
                v.tensor_tensor(qr[:, par], qT[:, :, bass.ds(j * P, P)], q_inv[:, par], ALU.mult).then_inc(qr_made, 1)

            def add_mix(j, par):
                xj = tile_of(x_sb, j)
                dve.wait_ge(mix_made, j + 3)
                v.tensor_tensor(xj, xj, psum[:, 1 + par, 0:D], ALU.add).then_inc(mix_added, 1)

            divide_q(0, 0)
            with dve.Fori(0, NT // 2) as turn:
                step.enter(turn, 4)
                divide_q(2 * turn + 1, 1)
                add_mix(2 * turn, 0)
                divide_q(2 * turn + 2, 0)
                add_mix(2 * turn + 1, 1)
                step.leave(NT // 2)
            add_mix(NT - 1, 0)

            left = s_dtab
            for n in range(3):
                step(v.tensor_copy(s_parts[:, :, n, :], left))
                step.settle()
                if n < 2:
                    step(v.tensor_tensor(s_rest, left, s_parts[:, :, n, :], ALU.subtract))
                    step.settle()
                left = s_rest
            step(v.tensor_tensor(rmask, typ.unsqueeze(2).broadcast_to([P, IT, R]),
                                 iota_r[:, 0:R].unsqueeze(1).broadcast_to([P, IT, R]), ALU.is_equal))
            step.settle()
            dve.sem_inc(dve_to_pe, 1)


            def one_hot(i, par):
                dve.wait_ge(oha_used, i + 1)
                v.tensor_tensor(oh_a[:, par], dl[:, bass.ds(i * G, G)].unsqueeze(2).broadcast_to([P, G, P]),
                                iota_r[:].unsqueeze(1).broadcast_to([P, G, P]), ALU.is_equal).then_inc(oha_made, 1)

            def pick_relation(i, par):
                dve.wait_ge(spread_made, i + 3)
                step.settle()
                step(v.tensor_tensor(tmp_s.rearrange("p k (r h) -> p k r h", r=R),
                                     psum[:, 4 + 2 * par:6 + 2 * par, :].rearrange("p b (k r h) -> p (b k) r h", r=R, h=H),
                                     rmask[:, bass.ds(i * G, G), :].unsqueeze(3).broadcast_to([P, G, R, H]), ALU.mult))
                step.settle()
                step(v.tensor_reduce(s_dst[:, bass.ds(i * G, G), :], tmp_s.rearrange("p k (r h) -> p k h r", r=R), AX, ALU.add))
                step.settle()
                dve.sem_inc(spread_used, 1)

            one_hot(0, 0)
            one_hot(1, 1)
            with dve.Fori(0, NG // 2 - 1) as turn:
                step.enter(turn, 4)
                one_hot(2 * turn + 2, 0)
                pick_relation(2 * turn, 0)
                one_hot(2 * turn + 3, 1)
                pick_relation(2 * turn + 1, 1)
                step.leave(NG // 2 - 1)
            pick_relation(NG - 2, 0)
            pick_relation(NG - 1, 1)

            dve.wait_ge(s_src_ready, 1)
            step(v.tensor_tensor(s_all.rearrange("p h c j -> p h (c j)"), s_src.rearrange("p i h -> p h i"),
                                 s_dst.rearrange("p i h -> p h i"), ALU.add))
            step.settle()
            step(v.tensor_copy(d_all.rearrange("p h c j -> p h (c j)"), dl[:].unsqueeze(1).broadcast_to([P, H, IT])))
            step.settle()
            dve.sem_inc(dve_to_pe, 1)

            def ask_pe(n):
                step.settle()
                dve.sem_inc(dve_to_pe, 1)
                dve.wait_ge(pe_to_dve, n)

            NB = -(-J // 4)
            dve.wait_ge(tr_copied, NB)
            step(v.scalar_tensor_tensor(out=score, in0=score, scalar=0.2, in1=score, op0=ALU.mult, op1=ALU.max))
            dve.wait_ge(tr_copied, 2 * NB)
            step(v.tensor_tensor(keep[:, 1:L], sc2[:, 1:L], sc2[:, 0:L - 1], ALU.is_equal))
            ask_pe(6)
            step(v.tensor_reduce(carry[:, 0:1], ident.rearrange("p (h c) -> p c h", h=H)[:, 0, :], AX, ALU.add))
            step(v.tensor_tensor(keep[:, 0:1], sc2[:, 0:1], psum[:, 0, 0:1], ALU.is_equal))
            step.settle()
            step(v.tensor_scalar(carry[:, 0:1], carry[:, 0:1], -1.0, 1.0, ALU.mult, ALU.add))
            step.settle()
            step(v.tensor_tensor(keep[:, 0:1], keep[:, 0:1], carry[:, 0:1], ALU.mult))
            ask_pe(7)
            step(v.tensor_copy(keep[:, L:L + 1], psum[:, 1, 0:1]))
            step.settle()
            step(v.tensor_reduce(carry[:, 0:1], keep[:, 1:L], AX, ALU.min))
            step.settle()
            step(v.tensor_tensor(carry[:, 1:2], carry[:, 0:1], keep[:, 0:1], ALU.min))
            step(v.tensor_tensor(carry[:, 2:3], carry[:, 0:1], keep[:, L:L + 1], ALU.min))
            step(v.memset(rows[0:1, 3, :], 0.0))
            ask_pe(8)
            step(v.tensor_copy(rows[0:1, 0:2, 0:P], psum[0:1, 2, 0:2 * P].rearrange("p (a n) -> p a n", a=2)))
            step.settle()

            def scan(out_, data, op, back, answer):
                flip = slice(None, None, -1) if back else slice(None)
                kp = keep[:, 1:L + 1] if back else keep[:, 0:L]
                args = kp[:, flip], data[:, flip]
                step(v.tensor_tensor_scan(out_[:, flip], *args, 0.0, ALU.mult, op))
                step.settle()
                end = 0 if back else L - 1
                step(v.tensor_copy(carry[:, 0:1], out_[:, end:end + 1]))
                ask_pe(answer)
                step(v.tensor_copy(rows[0:1, 2, 0:P], psum[0:1, 3, 0:P]))
                step.settle()
                to = rows[0:1, 3, 0:P] if back else rows[0:1, 3, 1:P + 1]
                edge = rows[0:1, 3, P:P + 1] if back else rows[0:1, 3, 0:1]
                step(v.memset(edge, 0.0))
                step(v.tensor_tensor_scan(to[:, flip], rows[0:1, 1 if back else 0, 0:P][:, flip],
                                          rows[0:1, 2, 0:P][:, flip], 0.0, ALU.mult, op))
                ask_pe(answer + 1)
                step(v.tensor_copy(carry[:, 3:4], psum[:, 4, 0:1]))
                step.settle()
                step(v.tensor_tensor_scan(out_[:, flip], *args, carry[:, 3:4], ALU.mult, op))
                step.settle()

            dve.wait_ge(tr_copied, 2 * NB)
            scan(sc1, score, ALU.max, False, 9)
            scan(sc2, sc1, ALU.max, True, 11)
            step(v.tensor_tensor(score, score, sc2, ALU.subtract))
            step.settle()
            dve.sem_inc(dve_to_act, 1)
            dve.wait_ge(act_to_dve, 2)
            scan(sc1, score, ALU.add, False, 13)
            scan(sc2, sc1, ALU.max, True, 15)
            step(v.tensor_scalar(sc2, sc2, 1e-12, None, ALU.add))
            step.settle()
            step(v.reciprocal(sc2, sc2))
            step.settle()
            step(v.tensor_tensor(score, score, sc2, ALU.mult))
            step.settle()
            dve.sem_inc(dve_to_pe, 1)
            dve.wait_ge(tr_copied, 3 * NB)
            step.settle()
            dve.sem_inc(acc_free, 1)

            def one_hot_b(i, q):
                step(v.tensor_tensor(oh_b[:, 4 * q:4 * q + 4], dl[:, bass.ds(i * G + 4 * q, 4)].unsqueeze(2).broadcast_to([P, 4, P]),
                                     iota_r[:].unsqueeze(1).broadcast_to([P, 4, P]), ALU.is_equal))

            def weigh(i, par, k):
                part = ring[:, par, k:k + 2].rearrange("p k (h d) -> p (k h) d", d=DH)
                wts = w_i.rearrange("p c j h -> p (c j h)")[:, bass.ds((i * G + k) * H, 2 * H)]
                return v.tensor_tensor(part, part, wts.unsqueeze(2).broadcast_to([P, 2 * H, DH]), ALU.mult)

            def add(blocks, k):
                a = tile_of(x_sb, blocks[k])
                return v.tensor_tensor(a, a, psum[:, k // 2, (k % 2) * D:(k % 2 + 1) * D], ALU.add)

            def quarter(i, par, turn, q, blocks):
                dve.wait_ge(sum_made, 4 * i + q + 17)
                if blocks:
                    if not (isinstance(i, int) and i == 1 and q == 0):
                        dve.wait_ge(sum_added, 4 * (i - 1) + q + 4)
                    step(add(blocks, 4 * q))
                one_hot_b(i, q)
                if blocks:
                    step.settle(1)
                    step(add(blocks, 4 * q + 1))
                if q == 0:
                    dve.wait_ge(rows_in[par], 16 * G * (turn + 1))
                step(weigh(i, par, 4 * q))
                if blocks:
                    step.settle(1)
                    step(add(blocks, 4 * q + 2))
                weigh(i, par, 4 * q + 2).then_inc(msg_made, 1)
                if blocks:
                    step.settle()
                    add(blocks, 4 * q + 3).then_inc(sum_added, 1)

            def group(i, par, turn):
                blocks = load_values(ENG.DVE, blk[0:1, bass.ds((i - 1) * G, G)], NT - 1)
                for q in range(4):
                    quarter(i, par, turn, q, blocks)

            for q in range(4):
                quarter(0, 0, 0, q, None)
            with dve.Fori(0, (NG - 1) // RING) as turn:
                step.enter(turn, 20 * RING)
                for n in range(RING):
                    group(RING * turn + n + 1, (n + 1) % RING, turn + (n + 1) // RING)
                step.leave((NG - 1) // RING)
            for i in range((NG - 1) // RING * RING + 1, NG):
                group(i, i % RING, i // RING)
            blocks = load_values(ENG.DVE, blk[0:1, (NG - 1) * G:NG * G], NT - 1)
            for k in range(G):
                if k % 4 == 0:
                    dve.wait_ge(sum_made, 4 * (NG - 1) + k // 4 + 21)
                if k == 0:
                    dve.wait_ge(sum_added, 4 * (NG - 1) + 4)
                step(add(blocks, k))
                step.settle()
            dve.sem_inc(x1_ready, 1)

            all_stats(stats_z, x_sb)

            spread_of(stx[:, 0], stx[:, 1], stats_z)
            dve.sem_inc(dve_to_act, 1)
            dve.wait_ge(act_to_dve, 3)
            step(v.reciprocal(stx[:, 2], stx[:, 1]))
            step.settle()

            def norm_y(j, par):
                dve.wait_ge(yT_made, j + 1)
                dve.wait_ge(xs_copied, j + 1)
                v.tensor_scalar(y_ring[:, par], tile_of(x_sb, j), stx[:, 0, bass.ds(j, 1)], stx[:, 2, bass.ds(j, 1)],
                                ALU.subtract, ALU.mult).then_inc(yr_made, 1)
                dve.wait_ge(yr_made, j + 1)
                step(v.bn_stats(tile_of(stats_z, j), y_ring[:, par]))

            with dve.Fori(0, NT // 2) as turn:
                step.enter(turn, 2)
                norm_y(2 * turn, 0)
                norm_y(2 * turn + 1, 1)
                step.leave(NT // 2)
            norm_y(NT - 1, 0)
            step.settle()
            spread_of(stx[:, 0], stx[:, 1], stats_z)
            dve.sem_inc(dve_to_act, 1)
            dve.wait_ge(act_to_dve, 4)
            step(v.reciprocal(stx[:, 2], stx[:, 1]))
            step.settle()
            dve.wait_ge(xs_copied, NT + 2)
            step(v.scalar_tensor_tensor(out=stx[:, 3], in0=stx[:, 0], scalar=-1.0, in1=stx[:, 2], op0=ALU.mult, op1=ALU.mult))
            step.settle()
            dve.sem_inc(dve_to_act, 1)

            def by_x(t):
                return t.rearrange("p (t x) -> p t x", x=X)

            def over_x(t):
                return t.unsqueeze(2).broadcast_to([P, NT, X])

            def x_row(t):
                return t.unsqueeze(1).broadcast_to([P, NT, X])

            pr, o1, o2, tmp, osum, tot, incl, rank, msk = rt
            mx, sm, p1, p2, w1c, w2c, f1, f2, cx, ntx, cumx = small[:11]
            dve.wait_ge(pe_to_dve, 17)
            step(v.tensor_tensor(by_x(pr), by_x(psum[:, 3, 0:NT * X]), x_row(br_sb), ALU.add))
            step.settle()
            step(v.tensor_reduce(mx, by_x(pr), AX, ALU.max))
            step.settle()
            step(v.tensor_tensor(by_x(pr), by_x(pr), over_x(mx), ALU.subtract))
            step.settle()
            dve.sem_inc(dve_to_act, 1)
            dve.wait_ge(act_to_dve, 5)
            step(v.tensor_reduce(sm, by_x(pr), AX, ALU.add))
            step.settle()
            step(v.reciprocal(sm, sm))
            step(v.tensor_scalar(mx[:, 0:X], iota_r[:, 0:X], -1.0, float(X), ALU.mult, ALU.add))
            step.settle()
            step(v.tensor_tensor(by_x(pr), by_x(pr), over_x(sm), ALU.mult))
            step.settle()

            def top(one_hot_, best):
                step(v.tensor_reduce(best, by_x(pr), AX, ALU.max))
                step.settle()
                step(v.tensor_tensor(by_x(tmp), by_x(pr), over_x(best), ALU.is_equal))
                step.settle()
                step(v.tensor_tensor(by_x(tmp), by_x(tmp), x_row(mx[:, 0:X]), ALU.mult))
                step.settle()
                step(v.tensor_reduce(f1, by_x(tmp), AX, ALU.max))
                step.settle()
                step(v.tensor_tensor(by_x(one_hot_), by_x(tmp), over_x(f1), ALU.is_equal))
                step.settle()

            top(o1, p1)
            step(v.scalar_tensor_tensor(out=pr, in0=o1, scalar=-4.0, in1=pr, op0=ALU.mult, op1=ALU.add))
            step.settle()
            top(o2, p2)
            step(v.tensor_tensor(f1, p1, p2, ALU.add))
            step.settle()
            step(v.reciprocal(f1, f1))
            step.settle()
            step(v.tensor_tensor(w1c, p1, f1, ALU.mult))
            step(v.tensor_tensor(w2c, p2, f1, ALU.mult))
            step(v.tensor_scalar(f2[:, 0:1], pcol[:, 0:1], float(LASTN), None, ALU.is_lt))
            step.settle()
            for o in (o1, o2):
                step(v.tensor_scalar(o[:, (NT - 1) * X:], o[:, (NT - 1) * X:], f2[:, 0:1], None, ALU.mult))
            step.settle()
            by_t = "p (x t) -> p t x"
            step(v.tensor_tensor(osum.rearrange(by_t, x=X), by_x(o1), by_x(o2), ALU.add))
            step(v.tensor_scalar(upper, iota_r[:], pcol[:, 0:1], None, ALU.is_gt))
            step(v.memset(msk, 1.0))
            step.settle()
            step(v.memset(msk.rearrange("p (x t) -> p x t", x=X)[:, :, 0], 0.0))
            ask_pe(18)
            step(v.tensor_copy(tot, psum[:, 5, 0:NT * X]))
            step.settle()
            step(v.tensor_tensor_scan(incl, msk, tot, 0.0, ALU.mult, ALU.add))
            step.settle()
            step(v.tensor_copy(cx[:, 0:X], incl.rearrange("p (x t) -> p x t", x=X)[:, :, NT - 1]))
            step(v.tensor_tensor(rank, incl, tot, ALU.subtract))
            step.settle()
            step(v.tensor_tensor(rank, rank, psum[:, 4, 0:NT * X], ALU.add))
            step.settle()
            step(v.scalar_tensor_tensor(out=rank.rearrange("p (x t) -> p x t", x=X),
                                        in0=iota_r[:, 0:X].unsqueeze(2).broadcast_to([P, X, NT]), scalar=float(XR),
                                        in1=rank.rearrange("p (x t) -> p x t", x=X), op0=ALU.mult, op1=ALU.add))
            step.settle()
            for o, slot in ((o1, slot_u[0]), (o2, slot_u[1])):
                step(v.tensor_tensor(by_x(tmp), by_x(o), rank.rearrange(by_t, x=X), ALU.mult))
                step.settle()
                step(v.tensor_reduce(f1, by_x(tmp), AX, ALU.add))
                step.settle()
                step(v.tensor_copy(slot, f1))
                step.settle()
            step(v.scalar_tensor_tensor(out=f1[:, 0:X], in0=iota_r[:, 0:X], scalar=float(XR), in1=cx[:, 0:X], op0=ALU.mult, op1=ALU.add))
            step.settle()
            step(v.tensor_copy(ftab[:, 2 * FT:2 * FT + X], f1[0:1, 0:X]))
            step(v.memset(xs_pad, 0.0))
            step(v.memset(xs[:, :, D + 2:XW], 0.0))
            step(v.tensor_copy(xs[:, :, D], w1c))
            step(v.tensor_scalar(xs[:, :, D + 1], iota_r[:, 0:NT], float(P), pcol[:, 0:1], ALU.mult, ALU.add))
            step.settle()
            step(v.tensor_scalar(xs_pad[:, D + 1:D + 2], pcol[:, 0:1], float(N), None, ALU.add))
            nti = f2[0:1, 0:X].bitcast(I32)
            step(v.tensor_scalar(ntx[0:1, 0:X], cx[0:1, 0:X], float(P - 1), None, ALU.add))
            step.settle()
            step(v.tensor_copy(nti, ntx[0:1, 0:X]))
            step.settle()
            step(v.tensor_scalar(nti, nti, 7, None, ALU.arith_shift_right))
            step.settle()
            step(v.tensor_copy(ntx[0:1, 0:X], nti))
            step.settle()
            step(v.tensor_tensor_scan(cumx[0:1, 0:X], ones[0:1, 0:X], ntx[0:1, 0:X], 0.0, ALU.mult, ALU.add))
            step.settle()
            step(v.tensor_tensor(ntx[0:1, 0:X], cumx[0:1, 0:X], ntx[0:1, 0:X], ALU.subtract))
            step.settle()
            step(v.tensor_scalar(ntx[0:1, 0:X], ntx[0:1, 0:X], float(-P), None, ALU.mult))
            step.settle()
            step(v.scalar_tensor_tensor(out=ntx[0:1, 0:X], in0=iota_r[0:1, 0:X], scalar=float(XR), in1=ntx[0:1, 0:X], op0=ALU.mult, op1=ALU.add))
            step.settle()
            step(v.tensor_tensor(sm[0:1, 0:X - 1], ntx[0:1, 1:X], ntx[0:1, 0:X - 1], ALU.subtract))
            ge = at(Z1 + 5 * NT * X, FT, X)[0:1]
            step(v.tensor_tensor(ge, iota_r[0:1, 0:FT].unsqueeze(2).broadcast_to([1, FT, X]),
                                 cumx[0:1, 0:X].unsqueeze(1).broadcast_to([1, FT, X]), ALU.is_ge))
            step.settle()
            et, rw = tmp[0:1, 0:FT], tmp[0:1, FT:2 * FT]
            step(v.tensor_reduce(et, ge[:, :, 0:X - 1], AX, ALU.add))
            step(v.tensor_tensor(gt[0:1], ge[:, :, 0:X - 1],
                                 sm[0:1, 0:X - 1].unsqueeze(1).broadcast_to([1, FT, X - 1]), ALU.mult))
            step.settle()
            step(v.tensor_reduce(rw, gt[0:1], AX, ALU.add))
            step.settle()
            step(v.scalar_tensor_tensor(out=rw, in0=iota_r[0:1, 0:FT], scalar=float(P), in1=rw, op0=ALU.mult, op1=ALU.add))
            step.settle()
            step(v.tensor_scalar(rw, rw, ntx[0:1, 0:1], None, ALU.add))
            step.settle()
            step(v.tensor_scalar(gt[0:1, :, 0], rw, -1.0, float(X * XR), ALU.mult, ALU.add))
            step.settle()
            step(v.tensor_tensor(gt[0:1, :, 0], gt[0:1, :, 0], ge[:, :, X - 1], ALU.mult))
            step.settle()
            step(v.tensor_tensor(rw, rw, gt[0:1, :, 0], ALU.add))
            step.settle()
            step(v.tensor_copy(ftab[:, 0:FT], et))
            step(v.tensor_copy(ftab[:, FT:2 * FT], rw))
            step.settle()
            dve.sem_inc(send_ready, 1)
            def add_shift(e):
                dve.wait_ge(w1_used, e + 1)
                dve.wait_ge(b1_in, 16 * (e + 1))
                lo = 0 if e % 2 == 0 else 6
                v.tensor_tensor(b1_row[0:1, :], b1_row[0:1, :], psum[0:1, lo:lo + 2, :].rearrange("p n f -> p (n f)"),
                                ALU.add).then_inc(b1_added, 1)
            for e in range(X - 3):
                add_shift(e)
            dve.wait_ge(sent, 16 * NT)
            step(v.tensor_copy(xs[:, :, D], w2c))
            step.settle()
            dve.sem_inc(send_ready, 1)
            for e in range(X - 3, X):
                add_shift(e)

            def copy_xT(i, par):
                dve.wait_ge(xgT_made, i + 1)
                v.tensor_copy(xgT[:, par], psum[:, 0, 0:D].rearrange("p (a n) -> p a n", a=KC)).then_inc(xgT_copied, 1)

            def add_b1(i, slot, turn):
                dve.wait_ge(xg_in[slot], 48 * (turn + 1))
                for n in range(2):
                    dve.wait_ge(f1_made, 2 * i + n + 1)
                    v.tensor_tensor(h_sb[:, slot % 2, n * 512:(n + 1) * 512], psum[:, 1 + n, :],
                                    bias_r[:, slot, n * 512:(n + 1) * 512], ALU.add).then_inc(h_pre, 1)

            def copy_hT(i, par):
                dve.wait_ge(hT_made, 2 * i + 1)
                v.tensor_copy(hT[:, par, 0:4], psum[:, 3].rearrange("p (c n) -> p c n", c=4)).then_inc(hT_copied, 1)

            def finish(i, slot):
                par = slot % 2
                dve.wait_ge(f2_made, i + 1)
                dve.wait_ge(y_free, i + 1)
                step(v.tensor_tensor(y_b2, psum[:, 5, 0:D], bias_r[:, slot, F:F + D], ALU.add))
                step(v.tensor_copy(tok_u[:, par:par + 1], xg[:, slot, D + 1:D + 2]))
                step.settle()
                v.tensor_scalar(y_out[:, par], y_b2, xg[:, slot, D:D + 1], None, ALU.mult).then_inc(tile_done, 1)
                dve.wait_ge(tile_done, i + 5)

            def turn_of_four(turn, more):
                for n in range(4):
                    copy_hT(4 * turn + n, n % 2)
                    if n < 2 or more:
                        copy_xT(4 * turn + n + 2, n % 2)
                    if n < 3 or more:
                        add_b1(4 * turn + n + 1, (n + 1) % 4, turn + (n + 1) // 4)
                    finish(4 * turn + n, n)

            copy_xT(0, 0)
            copy_xT(1, 1)
            add_b1(0, 0, 0)
            with dve.Fori(0, FT // 4 - 1) as turn:
                step.enter(turn, 8)
                turn_of_four(turn, True)
                step.leave(FT // 4 - 1)
            turn_of_four(FT // 4 - 1, False)

        @block.scalar
        def _(act):
            a_ = nc.scalar
            act.sem_inc(xt_copied, 2)
            act.sem_inc(h_copied, 4)
            for par in range(2):
                act.sem_inc(h_stored[par], 16)
            act.sem_inc(ohT_made, 2)
            act.sem_inc(yT_copied, 2)
            act.sem_inc(xs_copied, 2)

            def root(n):
                act.wait_ge(dve_to_act, n)
                a_.activation(stx[:, 1], stx[:, 1], ACT.Sqrt).then_inc(act_to_dve, 1)

            root(1)

            def copy_xt(j, par):
                act.wait_ge(xt_made, j + 3)
                act.wait_ge(stab_made, j + 1)
                src_ = psum[:, 6 + par, 0:D].rearrange("p (a n) -> p a n", a=KC)
                a_.copy(xs_ring[:, par], src_)
                a_.copy(xnT[:, :, bass.ds(j * P, P)], src_).then_inc(xt_copied, 1)
            pairs(act, NT, copy_xt)

            def copy_xs(j, par):
                act.wait_ge(ctx_added, j + 1)
                a_.copy(xs_ring[:, par], xnT[:, :, bass.ds(j * P, P)]).then_inc(xs_made, 1)

            act.wait_ge(stab_made, NT + 2)
            act.wait_ge(xt_copied, NT + 2)

            def evacuate(j, par, turn, more):
                if more:
                    copy_xs(j + 1, 1 - par)
                act.wait_ge(low_ready, j + 1)
                a_.activation(k_low, k_low, ACT.Exp)
                a_.activation(q_low, q_low, ACT.Exp).then_inc(exp_ready, 1)
                for n in range(4):
                    act.wait_ge(h_made, 4 * j + n + 1)
                    if n == 0:
                        act.wait_ge(h_stored[par], 16 * (turn + 1))
                    a_.copy(h_out[:, par, n * 512:(n + 1) * 512], psum[:, n, :]).then_inc(h_copied, 1)

            copy_xs(0, 0)
            with act.Fori(0, NT // 2) as turn:
                evacuate(2 * turn, 0, turn, True)
                evacuate(2 * turn + 1, 1, turn, True)
            evacuate(NT - 1, 0, NT // 2, False)

            def copy_ohT(i, par):
                act.wait_ge(oha_used, i + 3)
                act.wait_ge(spread_made, i + 1)
                a_.copy(ohT[:, par].rearrange("p k n -> p (k n)"),
                        psum[:, 2 * par:2 * par + 2, :].rearrange("p b n -> p (b n)").bitcast(BF16)).then_inc(ohT_made, 1)
            pairs(act, NG, copy_ohT)

            NB = -(-J // 4)
            n = 0
            for to in (score, sc2):
                for b in range(NB):
                    width = min(4, J - 4 * b) * P
                    act.wait_ge(tr_made, n + 1)
                    a_.copy(to[:, 4 * b * P:4 * b * P + width], psum[:, n % 8, 0:width]).then_inc(tr_copied, 1)
                    n += 1
            act.wait_ge(dve_to_act, 2)
            a_.activation(score, score, ACT.Exp).then_inc(act_to_dve, 1)
            for b in range(NB):
                w = min(4, J - 4 * b)
                act.wait_ge(tr_made, n + 1)
                for k in range(w):
                    ins = a_.copy(w_i[:, :, 4 * b + k, :].rearrange("p c h -> p h c"),
                                  psum[:, b % 8, k * P:(k + 1) * P].rearrange("p (h c) -> p h c", h=H))
                ins.then_inc(tr_copied, 1)
                n += 1

            root(3)

            def copy_y(j, par):
                act.wait_ge(yr_made, j + 1)
                a_.copy(xs[:, bass.ds(j, 1), 0:D].rearrange("p a d -> p (a d)"), y_ring[:, par]).then_inc(xs_copied, 1)
                act.wait_ge(yT_made, j + 3)
                a_.copy(yT[:, par], psum[:, 4 + par, 0:D].rearrange("p (a n) -> p a n", a=KC)).then_inc(yT_copied, 1)
            pairs(act, NT, copy_y)
            root(4)
            act.wait_ge(dve_to_act, 6)
            a_.activation(rt[0], rt[0], ACT.Exp).then_inc(act_to_dve, 1)
            with act.Fori(0, NT // 5) as turn:
                for n in range(5):
                    row = xs[:, bass.ds(5 * turn + n, 1), 0:D].rearrange("p a d -> p (a d)")
                    a_.activation(row, row, ACT.Identity, bias=stx[:, 3, bass.ds(5 * turn + n, 1)],
                                  scale=stx[:, 2, bass.ds(5 * turn + n, 1)]).then_inc(xs_normed, 1)

            act.wait_ge(ln_loaded, 32)
            for e in range(X):
                act.wait_ge(w1_used, e + 1)
                for c in range(KC):
                    a_.mul(w1_sb[:, e, c], w1_sb[:, e, c], ln_cols[:, 0, e, c:c + 1]).then_inc(w1_scaled, 1)

            def gelu(i, par):
                for n in range(2):
                    act.wait_ge(h_pre, 2 * i + n + 1)
                    half = h_sb[:, par, n * 512:(n + 1) * 512]
                    a_.activation(half, half, ACT.Gelu).then_inc(h_act, 1)

            def copy_hT(i, par):
                act.wait_ge(hT_made, 2 * i + 2)
                a_.copy(hT[:, par, 4:8], psum[:, 4].rearrange("p (c n) -> p c n", c=4)).then_inc(hT_copied, 1)

            gelu(0, 0)
            with act.Fori(0, FT // 2 - 1) as turn:
                copy_hT(2 * turn, 0)
                gelu(2 * turn + 1, 1)
                copy_hT(2 * turn + 1, 1)
                gelu(2 * turn + 2, 0)
            copy_hT(FT - 2, 0)
            gelu(FT - 1, 1)
            copy_hT(FT - 1, 1)

        @block.tensor
        def _(pe):
            t_ = nc.tensor
            for s_, n in ((xt_made, 2), (stab_made, 2), (ctx_added, 2), (oha_used, 2), (spread_made, 2),
                          (sum_made, 4 * RING), (mix_made, 2), (yT_made, 2)):
                pe.sem_inc(s_, n)

            def mm(o, lhsT, rhs, first=True, last=True, **kw):
                return t_.matmul(o, lhsT, rhs, start=first, stop=last, **kw)

            pe.wait_ge(dve_to_pe, 1)
            pe.wait_ge(in_wrel, 16)
            for m in range(KC):
                for r in range(R):
                    for c in range(KC):
                        lo = m * 2 * R * H + r * 2 * H
                        last = mm(psum[:, 5, lo:lo + 2 * H], wrel_sb[:, r, c, m * P:(m + 1) * P], ablock[:, c], c == 0, c == KC - 1)
            last.then_inc(pe_to_dve, 1)

            pe.wait_ge(dve_to_pe, 2)
            mm(psum[0:NT - 1, 0, 0:1], cnt[:, 0:NT - 1], ones[:, 0:1]).then_inc(pe_to_dve, 1)
            pe.wait_ge(dve_to_pe, 3)
            mm(psum[:, 1, 0:IT], ones[0:NT - 1, :], lt[0:NT - 1, :]).then_inc(pe_to_dve, 1)
            pe.wait_ge(dve_to_pe, 4)
            for n, bank in ((0, 2), (1, 3)):
                for c in range(TC):
                    last = mm(psum[:, bank, 0:IT], e_f[:, n, c, :], spread[:, c], c == 0, c == TC - 1)
            last.then_inc(pe_to_dve, 1)

            pe.wait_ge(pool_const, 1)
            pe.wait_ge(dve_to_pe, 5)

            def turn_x(j, par):
                pe.wait_ge(xn_made, j + 1)
                pe.wait_ge(xt_copied, j + 1)
                for a in range(KC):
                    last = t_.transpose(psum[:, 6 + par, a * P:(a + 1) * P], xn_ring[:, par, a * P:(a + 1) * P], ident)
                last.then_inc(xt_made, 1)

            def scores(j, par):
                pe.wait_ge(xt_copied, j + 3)
                pe.wait_ge(stab_copied, j + 1)
                for c in range(KC):
                    last = mm(psum[:, par, 0:2 * R * H], xs_ring[:, par, c], wa_sb[:, c], c == 0, c == KC - 1)
                last.then_inc(stab_made, 1)

            turn_x(0, 0)
            with pe.Fori(0, NT // 2) as turn:
                turn_x(2 * turn + 1, 1)
                scores(2 * turn, 0)
                turn_x(2 * turn + 2, 0)
                scores(2 * turn + 1, 1)
            scores(NT - 1, 0)

            pe.wait_ge(stab_copied, NT + 2)
            pe.wait_ge(in_wt, 48)
            mm(psum[:, 6, :], zrow[0:1, 0:P], zrow[0:1, :], skip_group_check=True)

            def node_tile(j, par, rows_=P):
                pe.wait_ge(xs_made, j + 1)
                xt = xs_ring[:, par]
                pe.wait_ge(kv_ready, j + 1)
                pe.wait_ge(q_read, j + 1)
                for c in range(KC):
                    last = mm(psum[:, 4, :], xt[:, c], wmix_sb[:, c, 0:2 * D], c == 0, c == KC - 1)
                last.then_inc(kv_made, 1)
                for a in range(KC):
                    for c in range(KC):
                        last = mm(psum[:, 5, a * P:(a + 1) * P], wmix_sb[:, c, 2 * D + a * P:2 * D + (a + 1) * P], xt[:, c], c == 0, c == KC - 1)
                last.then_inc(q_made, 1)
                for n in range(4):
                    pe.wait_ge(h_copied, 4 * j + n + 1)
                    for c in range(KC):
                        last = mm(psum[:, n, :], xt[:, c], wrt_sb[:, c, n * 512:(n + 1) * 512], c == 0, c == KC - 1)
                    last.then_inc(h_made, 1)
                pe.wait_ge(kv_ready, j + 2)
                for a in range(KC):
                    k_a, v_a = kv_sb[0:rows_, par, a * P:(a + 1) * P], kv_sb[0:rows_, par, D + a * P:D + (a + 1) * P]
                    mm(psum[:, 6, a * P:(a + 1) * P], v_a, k_a, False, False, skip_group_check=True)
                    last = mm(psum[:, 6, D + a:D + a + 1], k_a, ones[0:rows_, 0:1], False, False, skip_group_check=True)
                last.then_inc(ctx_added, 1)

            with pe.Fori(0, NT // 2) as turn:
                node_tile(2 * turn, 0)
                node_tile(2 * turn + 1, 1)
            node_tile(NT - 1, 0, LASTN)

            pe.wait_ge(dve_to_pe, 6)
            for a in range(KC):
                last = mm(psum[:, 7, a * D:(a + 1) * D], ctxT[:, a], wp_sb[:, a])
            last.then_inc(pe_to_dve, 1)

            pe.wait_ge(dve_to_pe, 7)
            pe.wait_ge(h_copied, 4 * NT + 4)

            def denominators(j, par):
                if not (isinstance(j, int) and j < 2):
                    pe.wait_ge(qr_made, j - 1)
                for a in range(KC):
                    last = mm(psum[:, 3 * par, a * P:(a + 1) * P], kb_sb[:, a], qT[:, a, bass.ds(j * P, P)])
                last.then_inc(den_made, 1)

            def mix(j, par):
                pe.wait_ge(qr_made, j + 1)
                pe.wait_ge(mix_added, j + 1)
                for a in range(KC):
                    last = mm(psum[:, 1 + par, 0:D], qr[:, par, a], m_sb[:, a], a == 0, a == KC - 1)
                last.then_inc(mix_made, 1)

            denominators(0, 0)
            denominators(1, 1)
            mix(0, 0)
            with pe.Fori(0, NT // 2 - 1) as turn:
                denominators(2 * turn + 2, 0)
                mix(2 * turn + 1, 1)
                denominators(2 * turn + 3, 1)
                mix(2 * turn + 2, 0)
            denominators(NT - 1, 0)
            mix(NT - 2, 1)
            mix(NT - 1, 0)

            pe.wait_ge(mix_added, NT + 2)
            pe.wait_ge(dve_to_pe, 8)

            def turn_one_hot(i, par):
                pe.wait_ge(oha_made, i + 1)
                pe.wait_ge(ohT_made, i + 1)
                for k in range(G):
                    to = psum[:, 2 * par + k // 8, (k % 8) * 64:(k % 8 + 1) * 64].bitcast(BF16)
                    last = t_.transpose(to, oh_a[:, par, k], eye_b[:])
                last.then_inc(oha_used, 1)

            def spread_scores(i, par):
                blocks = load_values(ENG.PE, blk[0:1, bass.ds(i * G, G)], NT - 1)
                pe.wait_ge(ohT_made, i + 3)
                pe.wait_ge(spread_used, i + 1)
                for k in range(G):
                    for n in range(3):
                        last = mm(psum[:, 4 + 2 * par + k // 8, (k % 8) * 64:(k % 8 + 1) * 64], ohT[:, par, k],
                                  s_parts[:, bass.ds(blocks[k], 1), n, :].rearrange("p a s -> p (a s)"), n == 0, n == 2)
                last.then_inc(spread_made, 1)

            turn_one_hot(0, 0)
            with pe.Fori(0, NG // 2 - 1) as turn:
                turn_one_hot(2 * turn + 1, 1)
                spread_scores(2 * turn, 0)
                turn_one_hot(2 * turn + 2, 0)
                spread_scores(2 * turn + 1, 1)
            turn_one_hot(NG - 1, 1)
            spread_scores(NG - 2, 0)
            spread_scores(NG - 1, 1)

            NB = -(-J // 4)
            pe.wait_ge(dve_to_pe, 9)
            n = 0
            for table in (s_all, d_all):
                for b in range(NB):
                    if n >= 8:
                        pe.wait_ge(tr_copied, n - 7)
                    for k in range(min(4, J - 4 * b)):
                        last = t_.transpose(psum[:, n % 8, k * P:(k + 1) * P], table[:, :, :, 4 * b + k].rearrange("p h c -> p (h c)"), ident)
                    last.then_inc(tr_made, 1)
                    n += 1
            pe.wait_ge(dve_to_pe, 10)
            mm(psum[:, 0, 0:1], shift_up, sc2[:, L - 1:L]).then_inc(pe_to_dve, 1)
            pe.wait_ge(dve_to_pe, 11)
            mm(psum[:, 1, 0:1], shift_down, keep[:, 0:1]).then_inc(pe_to_dve, 1)
            pe.wait_ge(dve_to_pe, 12)
            mm(psum[0:1, 2, 0:P], carry[:, 1:2], ident)
            mm(psum[0:1, 2, P:2 * P], carry[:, 2:3], ident).then_inc(pe_to_dve, 1)
            asked = 12
            for back in (0, 1, 0, 1):
                pe.wait_ge(dve_to_pe, asked + 1)
                mm(psum[0:1, 3, 0:P], carry[:, 0:1], ident).then_inc(pe_to_dve, 1)
                pe.wait_ge(dve_to_pe, asked + 2)
                mm(psum[:, 4, 0:1], rows[0:1, 3, back:back + P], ones[0:1, 0:1]).then_inc(pe_to_dve, 1)
                asked += 2
            pe.wait_ge(dve_to_pe, 21)
            for b in range(NB):
                for k in range(min(4, J - 4 * b)):
                    last = t_.transpose(psum[:, b % 8, k * P:(k + 1) * P], score[:, (4 * b + k) * P:(4 * b + k + 1) * P], ident)
                last.then_inc(tr_made, 1)
            pe.wait_ge(tr_copied, 3 * NB)

            def sum_rows(i, par):
                for q in range(4):
                    pe.wait_ge(msg_made, 4 * i + q + 1)
                    pe.wait_ge(sum_added, 4 * i + q + 1)
                    for k in range(4 * q, 4 * q + 4):
                        last = mm(psum[:, k // 2, (k % 2) * D:(k % 2 + 1) * D], oh_b[:, k], ring[:, par, k])
                    last.then_inc(sum_made, 1)
            with pe.Fori(0, NG // RING) as turn:
                for n in range(RING):
                    sum_rows(RING * turn + n, n)
            for i in range(NG // RING * RING, NG):
                sum_rows(i, i % RING)

            def turn_y(j, par):
                pe.wait_ge(yr_made, j + 1)
                pe.wait_ge(yT_copied, j + 1)
                for a in range(KC):
                    last = t_.transpose(psum[:, 4 + par, a * P:(a + 1) * P], y_ring[:, par, a * P:(a + 1) * P], ident)
                last.then_inc(yT_made, 1)

            def logits(j, par):
                pe.wait_ge(yT_copied, j + 3)
                for c in range(KC):
                    last = mm(psum[:, 3, bass.ds(j * X, X)], yT[:, par, c], wr_sb[:, c], c == 0, c == KC - 1)
                return last

            turn_y(0, 0)
            with pe.Fori(0, NT // 2) as turn:
                turn_y(2 * turn + 1, 1)
                logits(2 * turn, 0)
                turn_y(2 * turn + 2, 0)
                logits(2 * turn + 1, 1)
            logits(NT - 1, 0).then_inc(pe_to_dve, 1)
            pe.wait_ge(dve_to_pe, 22)
            mm(psum[:, 4, 0:NT * X], upper, rt[4])
            mm(psum[:, 5, 0:NT * X], ones[:], rt[4]).then_inc(pe_to_dve, 1)

            pe.wait_ge(w1_loaded, 16 * X)
            pe.wait_ge(ln_loaded, 32)
            for e in range(X):
                lo = 0 if e % 2 == 0 else 6
                if e >= 2:
                    pe.wait_ge(b1_added, e - 1)
                for n in range(2):
                    for c in range(KC):
                        last = mm(psum[0:1, lo + n, :], ln_cols[:, 1, e, c:c + 1], w1_sb[:, e, c, n * 512:(n + 1) * 512], c == 0, c == KC - 1)
                last.then_inc(w1_used, 1)

            pe.wait_ge(w1_scaled, KC * X)
            pe.wait_ge(b1_added, X)
            pe.wait_ge(w2_loaded, 16)

            def turn_rows(i, slot, turn):
                pe.wait_ge(xg_in[slot], 48 * (turn + 1))
                if not isinstance(i, int) or i:
                    pe.wait_ge(xgT_copied, i)
                for a in range(KC):
                    last = t_.transpose(psum[:, 0, a * P:(a + 1) * P], xg[:, slot, a * P:(a + 1) * P], ident)
                last.then_inc(xgT_made, 1)

            def hidden(i, par, e_reg):
                pe.wait_ge(xgT_copied, i + 1)
                if not isinstance(i, int) or i:
                    pe.wait_ge(h_pre, 2 * i)
                for n in range(2):
                    for c in range(KC):
                        last = mm(psum[:, 1 + n, :], xgT[:, par, c],
                                  w1_sb[:, bass.ds(e_reg, 1), c, n * 512:(n + 1) * 512].rearrange("p a f -> p (a f)"), c == 0, c == KC - 1)
                    last.then_inc(f1_made, 1)

            def turn_hidden(i, par):
                for n in range(2):
                    pe.wait_ge(h_act, 2 * i + n + 1)
                    for c in range(4):
                        last = t_.transpose(psum[:, 3 + n, c * P:(c + 1) * P], h_sb[:, par, (4 * n + c) * P:(4 * n + c + 1) * P], ident)
                    last.then_inc(hT_made, 1)

            def project(i, par, e_reg):
                pe.wait_ge(hT_copied, 2 * i + 2)
                pe.wait_ge(tile_done, i + 4)
                for c in range(FC):
                    last = mm(psum[:, 5, 0:D], hT[:, par, c], w2_sb[:, bass.ds(e_reg, 1), c, :].rearrange("p a d -> p (a d)"), c == 0, c == FC - 1)
                last.then_inc(f2_made, 1)

            def turn_of_four(turn, more):
                experts = load_values(ENG.PE, ftab[0:1, bass.ds(4 * turn, 4 + more)], X - 1)
                for n in range(4):
                    turn_hidden(4 * turn + n, n % 2)
                    if n < 2 or more:
                        turn_rows(4 * turn + n + 2, (n + 2) % 4, turn + (n + 2) // 4)
                    if n < 3 or more:
                        hidden(4 * turn + n + 1, (n + 1) % 2, experts[n + 1])
                    project(4 * turn + n, n % 2, experts[n])

            pe.wait_ge(xg_in[0], 48)
            turn_rows(0, 0, 0)
            first = load_values(ENG.PE, ftab[0:1, 0:1], X - 1)
            turn_rows(1, 1, 0)
            hidden(0, 0, first[0])
            with pe.Fori(0, FT // 4 - 1) as turn:
                turn_of_four(turn, True)
            turn_of_four(FT // 4 - 1, False)


def kernel(x, src, dst, edge_type_8, L0_gnn_W, L0_gnn_attn_src, L0_gnn_attn_dst, L0_mix_Wq, L0_mix_Wkv,
           L0_mix_Wproj, L0_mix_bproj, L0_ffn_Wr, L0_ffn_br, L0_ffn_ln_g, L0_ffn_ln_b, L0_ffn_W1,
           L0_ffn_b1, L0_ffn_W2, L0_ffn_b2):
    import concourse.bacc as bacc
    from concourse.bass_utils import run_bass_kernel_spmd

    def chunks(a):
        return a.reshape(-1, P, a.shape[-1]).transpose(1, 0, 2)

    w = np.asarray(L0_gnn_W)
    att = np.stack([np.asarray(L0_gnn_attn_src).reshape(-1), np.asarray(L0_gnn_attn_dst).reshape(-1)], 1)
    wkv, wq = np.asarray(L0_mix_Wkv), np.asarray(L0_mix_Wq)
    arrays = {
        "x": np.asarray(x), "src": np.asarray(src), "dst": np.asarray(dst), "etype": np.asarray(edge_type_8),
        "w_rel": w.reshape(R, KC, P, D).transpose(2, 0, 1, 3),
        "w_rel_t": chunks(w.transpose(2, 0, 1).reshape(D, R * D)),
        "attn": chunks(att),
        "wmix_t": chunks(np.concatenate([wkv, wq], 0).T),
        "wp_t": chunks(np.asarray(L0_mix_Wproj).T),
        "bproj": np.asarray(L0_mix_bproj).reshape(1, D),
        "wr": chunks(np.asarray(L0_ffn_Wr)),
        "br": np.asarray(L0_ffn_br).reshape(1, X),
        "ln_g": np.asarray(L0_ffn_ln_g).reshape(X, KC, P).transpose(2, 0, 1),
        "ln_b": np.asarray(L0_ffn_ln_b).reshape(X, KC, P).transpose(2, 0, 1),
        "w1": np.asarray(L0_ffn_W1).reshape(X, KC, P, F).transpose(0, 2, 1, 3).reshape(X, P, KC * F),
        "b1": np.asarray(L0_ffn_b1),
        "w2": np.asarray(L0_ffn_W2).reshape(X, FC, P, D).transpose(2, 0, 1, 3),
        "b2": np.asarray(L0_ffn_b2),
    }
    arrays = {f"in_{k}": np.ascontiguousarray(a) for k, a in arrays.items()}
    nc = bacc.Bacc("TRN2", target_bir_lowering=False, num_devices=1)
    args = [nc.dram_tensor(k, a.shape, mybir.dt.from_np(a.dtype), kind="ExternalInput").ap() for k, a in arrays.items()]
    args.append(nc.dram_tensor("out", [N + P, D], F32, kind="ExternalOutput").ap())
    gps_layer(nc, *args)
    r = run_bass_kernel_spmd(nc, [arrays], core_ids=[0])
    return r.results[0]["out"][0:N]
```

```python
from contextlib import ExitStack

import numpy as np

import concourse.bass as bass
from concourse import mybir

F32 = mybir.dt.float32
BF16 = mybir.dt.bfloat16
I32 = mybir.dt.int32
U32 = mybir.dt.uint32
ALU = mybir.AluOpType
ACT = mybir.ActivationFunctionType
AX = mybir.AxisListType.X
ENG = mybir.EngineType

P = 128
N, E, D = 3125, 50000, 256
R, H, DH = 8, 8, 32
X, F, TOPK = 8, 1024, 2
KC = D // P
NT = -(-N // P)
NP = NT * P
LASTN = N - (NT - 1) * P
TE = -(-E // P)
LASTE = E - (TE - 1) * P
TC = -(-TE // P)
CH = P // H
G = 16
IT = -(-(TE - 1 + NT) // G) * G
NG = IT // G
RING = 5
J = IT // CH
L = J * P
XR = NP + P
FT = (N * TOPK - X) // P + X
FT += -FT % 4
XW = D + 4
FC = F // P
LN_EPS = 1e-5
assert NG == NT + 1 and IT % CH == 0 and NG % 2 == 0 and NT % 2 == 1 and FT % 4 == 0

WORDS = 51200


class Chain:

    def __init__(self, eng, sem):
        self.eng, self.sem, self.base, self.k, self.per = eng, sem, 0, 0, 0

    def __call__(self, ins):
        self.k += 1
        ins.then_inc(self.sem, 1)
        return ins

    def settle(self, back=0):
        self.eng.wait_ge(self.sem, self.base + self.k - back)

    def enter(self, turn, per):
        if self.k and isinstance(self.base, int) and not self.per:
            self.base, self.k = self.base + self.k, 0
        self.start, self.per = self.base, per
        self.base, self.k = self.start + turn * per, 0

    def leave(self, turns):
        assert self.k == self.per, (self.k, self.per)
        self.base, self.k, self.per = self.start + turns * self.per, 0, 0


def gps_layer(nc, x, src, dst, etype, w_rel, w_rel_t, attn, wmix_t, wp_t, bproj,
              wr, br, ln_g, ln_b, w1, b1, w2, b2, out):
    dl_d = nc.dram_tensor("local_destinations", [IT, P], BF16, kind="Internal").ap()
    s_tab = nc.dram_tensor("source_scores", [NP * R, H], F32, kind="Internal").ap()
    h_tab = nc.dram_tensor("node_rows", [NP * R, D], F32, kind="Internal").ap()
    bias_d = nc.dram_tensor("expert_bias", [X, F], F32, kind="Internal").ap()
    x_rows = nc.dram_tensor("expert_rows", [X * XR + P, XW], F32, kind="Internal").ap()

    ctx = ExitStack()
    with ctx:
        def sb(name, shape, dt=F32):
            return ctx.enter_context(nc.sbuf_tensor(name, shape, dt))

        def sem(name):
            return ctx.enter_context(nc.semaphore(name))

        arena = sb("arena", [P, WORDS])

        def at(lo, *shape, dt=F32):
            n = int(np.prod(shape))
            view = arena[:, lo:lo + (n // 2 if dt == BF16 else n)]
            if dt != F32:
                view = view.bitcast(dt)
            names = "abcd"[:len(shape)]
            if len(shape) > 1:
                view = view.rearrange(f"p ({' '.join(names)}) -> p {' '.join(names)}",
                                      **dict(zip(names[1:], shape[1:])))
            return view

        A0 = NT * D
        ACC = A0 + X * KC * F
        QT = ACC + NT * D
        B0 = QT + KC * NP
        Z0 = ACC + X * FC * D
        x_sb = at(0, NT, D)
        qT = at(QT, KC, NP)
        xnT = at(A0, KC, NP)
        wrt_sb = at(A0 + 6400, KC, R * D)
        wmix_sb = at(A0 + 10496, KC, 3 * D)
        wp_sb = at(A0 + 12032, KC, D)
        ctxT = at(A0 + 12544, KC, P)
        xs_ring = at(A0 + 12800, 2, KC, P)
        s_dtab = at(A0 + 14592, NT, R * H)
        wrel_sb = at(QT, R, KC, D)
        h_out = at(ACC, 2, R * D)
        kv_sb = at(ACC + 4096, 2, 2 * D)
        k_low = at(ACC + 5120, D)
        q_low = at(ACC + 5376, KC, P)
        s_out = at(B0, NT, R * H)
        e_raw = at(B0 + 1600, 3, TC, P, dt=I32)
        e_f = at(B0 + 3136, 3, TC, P)
        before = at(A0, NT - 1, TC, P, dt=BF16)
        block_i = at(B0 + 4672, TC, P, dt=I32)
        block_b = at(B0 + 5184, TC, P, dt=BF16)
        spread = at(B0 + 4672, TC, IT)
        qr = at(B0 + 1600, 2, KC, P)
        q_inv = at(B0 + 2112, 2, KC, P)
        s_parts = at(B0 + 4000, NT, 3, R * H, dt=BF16)
        s_rest = at(B0 + 6400, NT, R * H)
        xn_ring = at(B0 + 6400, 2, D)
        lt = at(B0 + 6912, IT)
        cnt = at(B0 + 7328, NT)
        t_it = at(B0 + 7392, IT)
        typ_i = lt.bitcast(U32)
        stats = at(B0 + 7808, NT, 6)
        dl_b = at(B0 + 6400, 2, G, P, dt=BF16)
        ohT = at(A0 + 2048, 2, G, P, dt=BF16)
        tmp_s = at(A0 + 14592, G, R * H)
        rmask = at(A0 + 7168, IT, R)
        s_dst = at(A0 + 10496, IT, H)
        s_src = at(B0 + 10240, IT, H)
        typ = at(B0 + 13824, IT)
        m_sb = at(B0 + 14784, KC, D)
        kb_sb = at(B0 + 15296, KC, P)
        s_all = at(A0, H, CH, J)
        score = at(A0 + 3328, L)
        keep = at(A0 + 6656, L + 1)
        sc2 = at(A0 + 9992, L)
        sc1 = at(A0, L)
        ring = at(ACC + 384, RING, G, D)
        oh_b = at(B0 + 8192, G, P)
        w_i = at(B0 + 10240, CH, J, H)
        xs = at(Z0, NT, XW)
        xs_pad = at(Z0 + NT * XW, XW)
        y_ring = at(Z0 + 26 * XW, 2, D)
        yT = at(Z0 + 26 * XW + 512, 2, KC, P)
        b1_row = at(0, 4, F)
        Z1 = Z0 + 26 * XW + 1792
        rt = [at(Z1 + n * NT * X, NT * X) for n in range(9)]
        small = [at(Z1 + 9 * NT * X + n * NT, NT) for n in range(14)]
        w1_sb = at(A0, X, KC, F)
        w2_sb = at(ACC, X, FC, D)
        xg = at(Z0, 4, XW)
        xgT = at(Z0 + 1040, 2, KC, P)
        bias_r = at(Z0 + 1552, 4, F + D)
        h_sb = at(Z0 + 6672, 2, F)
        hT = at(Z0 + 8720, 2, FC, P)
        y_out = at(Z0 + 10768, 2, D)
        y_b2 = at(Z0 + 11280, D)
        tok_u = at(Z0 + 11536, 2).bitcast(U32)
        assert Z1 + 9 * NT * X + 14 * NT <= B0 + 14784

        eye = sb("eye", [P, P + 2])
        ident, shift_up, shift_down = eye[:, 1:P + 1], eye[:, 0:P], eye[:, 2:P + 2]
        iota_r = sb("iota_r", [P, P])
        pcol = sb("pcol", [P, TC])
        ones = sb("ones", [P, P])
        idx_i = sb("idx_i", [P, IT], U32)
        idx_r = sb("idx_r", [P, RING, G], U32)
        dl = sb("dl", [P, IT])
        blk = sb("blk", [1, IT], I32)
        hmask = sb("hmask", [P, KC, H])
        wa_sb = at(B0 + 8192, KC, 2 * R * H)
        att_sb = at(B0 + 8448, KC, 2)
        ablock = at(B0 + 8464, KC, 2 * H)
        bproj_b = at(B0 + 8512, D)
        dl_rows = at(B0 + 8768, -(-IT // P), P, dt=BF16)
        ln_cols = at(B0 + 15296, 2, X, KC)
        bdm = at(B0 + 9600, P)
        zrow = at(B0 + 9728, 512)
        wr_sb = at(B0 + 15552, KC, X)
        br_sb = at(B0 + 15568, X)
        stx = sb("stx", [P, 4, NT])
        carry = sb("carry", [P, 4])
        ftab = at(B0 + 15124, 2 * FT + 8, dt=I32)[0:1]
        rows = at(B0 + 8192, 4, P + 1)
        psum = ctx.enter_context(nc.psum_tensor("psum", [P, 8, 512], F32))

        d_all = at(B0 + 10240, H, CH, J)
        slot_u = [m.bitcast(U32) for m in (small[11], small[12])]

        upper = at(Z0 + 26 * XW + 512, P)
        gt = at(Z0 + 26 * XW, FT, X - 1)
        stats_z = at(Z1 + 8 * NT * X, NT, 6)

        fill_done = sem("fill_done")
        in_edges, in_att, in_x, in_wrel, in_wt, in_misc = map(
            sem, ("in_edges", "in_att", "in_x", "in_wrel", "in_wt", "in_misc"))
        pool_const = sem("pool_const")
        dve_step, pool_step = sem("dve_step"), sem("pool_step")
        pool_turn = sem("pool_turn")
        dve_to_pe, pe_to_dve = sem("dve_to_pe"), sem("pe_to_dve")
        dve_to_act, act_to_dve = sem("dve_to_act"), sem("act_to_dve")
        items_ready = sem("items_ready")
        parts_made = sem("parts_made")
        wa_made = sem("wa_made")
        xn_made = sem("xn_made")
        xt_made, xt_copied = sem("xt_made"), sem("xt_copied")
        stab_made, stab_copied = sem("stab_made"), sem("stab_copied")
        stab_stored = sem("stab_stored")
        xs_made = sem("xs_made")
        kv_made, kv_ready, ctx_added = map(sem, ("kv_made", "kv_ready", "ctx_added"))
        q_made, q_read = sem("q_made"), sem("q_read")
        low_ready, exp_ready = sem("low_ready"), sem("exp_ready")
        h_made, h_copied = sem("h_made"), sem("h_copied")
        h_stored = [sem("h_stored0"), sem("h_stored1")]
        b1_in, b1_out = [sem(f"b1_in{n}") for n in range(4)], [sem(f"b1_out{n}") for n in range(4)]
        w1_scaled = sem("w1_scaled")
        w1_used, b1_added = sem("w1_used"), sem("b1_added")
        tr_made, tr_copied = sem("tr_made"), sem("tr_copied")
        shifted = sem("shifted")
        weights_made, idx_taken = sem("weights_made"), sem("idx_taken")
        s_src_in = [sem("s_src_in0"), sem("s_src_in1")]
        dlT_made, dlT_copied, dl_stored = map(sem, ("dlT_made", "dlT_copied", "dl_stored"))
        dl_in = [sem("dl_in0"), sem("dl_in1")]
        ohT_made, spread_made, spread_used = map(sem, ("ohT_made", "spread_made", "spread_used"))
        rows_in = [[sem(f"rows_in{n}_{q}") for q in range(4)] for n in range(RING)]
        msg_made, sum_made, sum_added = map(sem, ("msg_made", "sum_made", "sum_added"))
        w1_loaded, w2_loaded = sem("w1_loaded"), sem("w2_loaded")
        qr_made, mix_made, mix_added, x1_ready, yr_made, yT_made, yT_copied, xs_copied = map(
            sem, ("qr_made", "mix_made", "mix_added", "x1_ready", "yr_made", "yT_made", "yT_copied", "xs_copied"))
        den_made, ln_loaded, xs_normed = sem("den_made"), sem("ln_loaded"), sem("xs_normed")
        out_init = sem("out_init")
        send_ready, sent, tiles_ready = sem("send_ready"), sem("sent"), sem("tiles_ready")
        scans_done = sem("scans_done")
        xg_in = [sem(f"xg_in{n}") for n in range(4)]
        tile_done = sem("tile_done")
        xgT_made, xgT_copied, f1_made, h_pre, h_act, hT_made, hT_copied, f2_made = map(
            sem, ("xgT_made", "xgT_copied", "f1_made", "h_pre", "h_act", "hT_made", "hT_copied", "f2_made"))
        y_free = sem("y_free")
        y_added = [sem("y_added0"), sem("y_added1")]

        def load_values(eng, row, hi):
            return nc.values_load_multi_w_load_instructions(
                row, engines=[eng], min_val=0, max_val=hi,
                skip_runtime_bounds_check_because="the program works these out itself, in range for any input",
            )[1]

        def pairs(eng, n, body):
            with eng.Fori(0, n // 2) as turn:
                body(2 * turn, 0)
                body(2 * turn + 1, 1)
            if n % 2:
                body(n - 1, 0)

        block = ctx.enter_context(nc.Block())

        @block.sync
        def _(sp):
            sp.wait_ge(fill_done, 1)
            full = (TE - 1) // P
            sp.dma_start(att_sb, attn).then_inc(in_att, 16)
            for n, a in enumerate((dst, src, etype)):
                sp.dma_start(e_raw[:, n, 0:full, :], a[0:full * P * P].rearrange("(c t e) -> t c e", t=P, e=P)).then_inc(in_edges, 16)
                rest = TE - 1 - full * P
                sp.dma_start(e_raw[0:rest, n, full, :], a[full * P * P:(TE - 1) * P].rearrange("(t e) -> t e", e=P)).then_inc(in_edges, 16)
                sp.dma_start(e_raw[rest:rest + 1, n, full, 0:LASTE], a[(TE - 1) * P:E].rearrange("(t e) -> t e", t=1)).then_inc(in_edges, 16)
            sp.dma_start(wrel_sb, w_rel).then_inc(in_wrel, 16)
            sp.dma_start(x_sb[:, 0:NT - 1, :], x[0:(NT - 1) * P, :].rearrange("(j p) d -> p j d", p=P)).then_inc(in_x, 16)
            sp.dma_start(x_sb[0:LASTN, NT - 1, :], x[(NT - 1) * P:N, :]).then_inc(in_x, 16)
            sp.dma_start(wrt_sb, w_rel_t).then_inc(in_wt, 16)
            sp.dma_start(wmix_sb, wmix_t).then_inc(in_wt, 16)
            sp.dma_start(wp_sb, wp_t).then_inc(in_wt, 16)
            sp.dma_start(wr_sb, wr).then_inc(in_misc, 16)
            sp.dma_start(br_sb, br.broadcast_to([P, X])).then_inc(in_misc, 16)
            sp.dma_start(bproj_b[:, 0:D], bproj.broadcast_to([P, D])).then_inc(in_misc, 16)
            sp.wait_ge(stab_copied, NT + 2)
            sp.dma_start(s_tab.rearrange("(j p r) h -> p j (r h)", p=P, r=R), s_out).then_inc(stab_stored, 16)

            sp.wait_ge(dlT_copied, 1)
            for c in range(-(-IT // P)):
                n = min(P, IT - c * P)
                sp.dma_start(dl_d[c * P:c * P + n, :], dl_rows[0:n, c, :]).then_inc(dl_stored, 16)

            def load_dl(i, par):
                sp.wait_ge(ohT_made, i + 1)
                sp.dma_start(dl_b[:, par].rearrange("p k n -> p (k n)"),
                             dl_d[bass.ds(i * G, G), :].rearrange("(o k) n -> o (k n)", o=1).broadcast_to([P, G * P])
                             ).then_inc(dl_in[par], 16)

            sp.wait_ge(dl_stored, 16 * -(-IT // P))
            sp.wait_ge(parts_made, 1)
            load_dl(0, 0)
            load_dl(1, 1)

            h_view = h_tab.rearrange("(j p r) d -> j p (r d)", p=P, r=R)

            def store_rows(j, par):
                sp.wait_ge(h_copied, 4 * j + 8)
                sp.dma_start(h_view[bass.ds(j, 1)].rearrange("a p w -> (a p) w"), h_out[:, par]).then_inc(h_stored[par], 16)
            pairs(sp, NT, store_rows)
            with sp.Fori(1, NG // 2) as turn:
                load_dl(2 * turn, 0)
                load_dl(2 * turn + 1, 1)
            sp.wait_ge(mix_added, NT + 2)
            sp.dma_start(ln_cols[:, 0], ln_g).then_inc(ln_loaded, 16)
            sp.dma_start(ln_cols[:, 1], ln_b).then_inc(ln_loaded, 16)
            sp.wait_ge(scans_done, 1)
            for e in range(X):
                sp.dma_start(w1_sb[:, e], w1[e].rearrange("p (c f) -> p c f", c=KC)).then_inc(w1_loaded, 16)
            sp.wait_ge(x1_ready, 1)
            sp.dma_start(out[0:(NT - 1) * P, :].rearrange("(j p) d -> p j d", p=P), x_sb[:, 0:NT - 1, :]).then_inc(out_init, 16)
            sp.dma_start(out[(NT - 1) * P:N, :], x_sb[0:LASTN, NT - 1, :]).then_inc(out_init, 16)
            sp.dma_start(w2_sb, w2).then_inc(w2_loaded, 16)

            def load_b1(e):
                sp.dma_start(b1_row[0:1, e % 4], b1[e:e + 1, :]).then_inc(b1_in[e % 4], 16)
            sp.wait_ge(out_init, 32)
            sp.wait_ge(xs_normed, 1)
            for e in range(4):
                load_b1(e)
            sp.wait_ge(send_ready, 1)
            sp.dma_start(out[N:N + P, :], xs_pad[:, 0:D]).then_inc(out_init, 16)
            sp.dma_start(x_rows[X * XR:X * XR + P, :], xs_pad).then_inc(out_init, 16)
            ends = load_values(ENG.SP, ftab[0:1, 2 * FT:2 * FT + X], X * XR)
            for e in range(X):
                sp.dma_start(x_rows[bass.ds(ends[e], P), :], xs_pad).then_inc(out_init, 16)
            for e in range(X):
                sp.wait_ge(b1_added, e + 1)
                sp.dma_start(bias_d[e:e + 1, :], b1_row[0:1, e % 4]).then_inc(b1_out[e % 4], 16)
                if e + 4 < X:
                    sp.wait_ge(b1_out[e % 4], 16 * (e // 4 + 1))
                    load_b1(e + 4)
            for n in range(4):
                sp.wait_ge(b1_out[n], 16 * X // 4)
            sp.wait_ge(tiles_ready, 1)
            with sp.Fori(0, FT // 4) as turn:
                e_regs = load_values(ENG.SP, ftab[0:1, bass.ds(4 * turn, 4)], X - 1)
                r_regs = load_values(ENG.SP, ftab[0:1, bass.ds(4 * turn + FT, 4)], X * XR)
                sp.wait_ge(sent, 16 * 2 * NT)
                sp.wait_ge(out_init, 16 * (4 + X))
                for n in range(4):
                    sp.wait_ge(tile_done, 4 * turn + n + 1)
                    sp.dma_start(xg[:, n], x_rows[bass.ds(r_regs[n], P), :]).then_inc(xg_in[n], 16)
                    sp.dma_start(bias_r[:, n, 0:F], bias_d[bass.ds(e_regs[n], 1), :].broadcast_to([P, F])).then_inc(xg_in[n], 16)
                    sp.dma_start(bias_r[:, n, F:F + D], b2[bass.ds(e_regs[n], 1), :].broadcast_to([P, D])).then_inc(xg_in[n], 16)

        @block.gpsimd
        def _(pool):
            step = Chain(pool, pool_step)
            g = nc.gpsimd
            step(g.memset(eye[:], 0.0))
            step(g.memset(hmask[:], 1.0))
            step(g.iota(iota_r[:], pattern=[[1, P]], base=0, channel_multiplier=0, allow_small_or_imprecise_dtypes=True))
            step(g.iota(pcol[:], pattern=[[P, TC]], base=0, channel_multiplier=1, allow_small_or_imprecise_dtypes=True))
            step(g.iota(t_it, pattern=[[1, IT]], base=0, channel_multiplier=0, allow_small_or_imprecise_dtypes=True))
            step.settle()
            step(g.affine_select(out=eye[:], in_=eye[:], compare_op=ALU.not_equal, fill=1.0, base=1,
                                 pattern=[[-1, P + 2]], channel_multiplier=1))
            step(g.affine_select(out=hmask[:], in_=hmask[:], compare_op=ALU.is_ge, fill=0.0, base=0,
                                 pattern=[[P, KC], [-DH, H]], channel_multiplier=1))
            step.settle()
            g.affine_select(out=hmask[:], in_=hmask[:], compare_op=ALU.is_ge, fill=0.0, base=DH - 1,
                            pattern=[[-P, KC], [DH, H]], channel_multiplier=-1).then_inc(pool_const, 1)

            pool.wait_ge(items_ready, 1)
            pool.wait_ge(stab_stored, 16)

            for i in range(IT):
                g.indirect_dma_start(out=s_src[:, i, :], out_offset=None, in_=s_tab,
                                     in_offset=bass.IndirectOffsetOnAxis(ap=idx_i[:, i:i + 1], axis=0)
                                     ).then_inc(s_src_in[i % 2], 16)

            pool.wait_ge(h_stored[0], 16 * ((NT + 1) // 2 + 1))
            pool.wait_ge(h_stored[1], 16 * (NT // 2 + 1))
            pool.wait_ge(ctx_added, NT + 2)

            def gather_rows(i, par):
                for k in range(G):
                    if k % 4 == 0:
                        pool.wait_ge(idx_taken, 4 * i + k // 4 + 1)
                        pool.sem_inc(pool_turn, 1)
                    g.indirect_dma_start(out=ring[:, par, k, :], out_offset=None, in_=h_tab,
                                         in_offset=bass.IndirectOffsetOnAxis(ap=idx_r[:, par, k:k + 1], axis=0)
                                         ).then_inc(rows_in[par][k // 4], 16)

            with pool.Fori(0, NG // RING) as turn:
                for n in range(RING):
                    if n == 1:
                        pool.wait_ge(mix_added, NT + 2)
                    if n == 3:
                        pool.wait_ge(spread_made, NG + 2)
                    gather_rows(RING * turn + n, n)
            for i in range(NG // RING * RING, NG):
                gather_rows(i, i % RING)

            s1_u, s2_u = slot_u
            pool.wait_ge(send_ready, 1)
            pool.wait_ge(xs_normed, NT)
            for j in range(NT):
                n = P if j < NT - 1 else LASTN
                g.indirect_dma_start(out=x_rows, out_offset=bass.IndirectOffsetOnAxis(ap=s1_u[0:n, j:j + 1], axis=0),
                                     in_=xs[0:n, j, :], in_offset=None).then_inc(sent, 16)
            pool.wait_ge(send_ready, 2)
            for j in range(NT):
                n = P if j < NT - 1 else LASTN
                g.indirect_dma_start(out=x_rows, out_offset=bass.IndirectOffsetOnAxis(ap=s2_u[0:n, j:j + 1], axis=0),
                                     in_=xs[0:n, j, :], in_offset=None).then_inc(sent, 16)
            pool.wait_ge(out_init, 16 * (4 + X))

            with pool.Fori(0, FT // 2) as turn:
                for par in range(2):
                    pool.wait_ge(tile_done, 2 * turn + par + 5)
                    pool.sem_inc(pool_turn, 1)
                    g.indirect_dma_start(out=out, out_offset=bass.IndirectOffsetOnAxis(ap=tok_u[:, par:par + 1], axis=0),
                                         in_=y_out[:, par], in_offset=None, compute_op=ALU.add).then_inc(y_added[par], 16)
                    pool.wait_ge(y_added[par], 16 * (turn + 1))
                    pool.sem_inc(y_free, 1)


        @block.vector
        def _(dve):
            step = Chain(dve, dve_step)
            v = nc.vector
            dve.sem_inc(stab_copied, 2)
            dve.sem_inc(kv_ready, 1)
            dve.sem_inc(q_read, 1)
            dve.sem_inc(y_free, 2)
            dve.sem_inc(spread_used, 2)
            dve.sem_inc(sum_added, 4)
            dve.sem_inc(mix_added, 2)
            dve.sem_inc(qr_made, 1)
            dve.sem_inc(tile_done, 4)

            step(v.memset(e_raw[:, 0, TC - 1, :], NP))
            step(v.memset(e_raw[:, 1, TC - 1, :], 0))
            step(v.memset(e_raw[:, 2, TC - 1, :], 0))
            step(v.memset(x_sb[:, NT - 1, :], 0.0))
            step.settle()
            dve.sem_inc(fill_done, 1)
            step(v.memset(ones[:], 1.0))
            step(v.memset(zrow, 0.0))

            dve.wait_ge(in_att, 16)
            dve.wait_ge(pool_const, 1)
            for c in range(KC):
                for w in range(2):
                    step(v.tensor_scalar(ablock[:, c, w * H:(w + 1) * H], hmask[:, c, :], att_sb[:, c, w:w + 1], None, ALU.mult))
            step.settle()
            dve.sem_inc(dve_to_pe, 1)

            dve.wait_ge(in_edges, 16 * 9)
            step(v.tensor_scalar(block_i, e_raw[:, 0], 7, None, ALU.arith_shift_right))
            step.settle()
            step(v.tensor_copy(block_b, block_i))
            step.settle()
            for b in range(1, NT):
                step(v.tensor_scalar(before[:, b - 1], block_b, float(b), 0.0, ALU.is_lt, ALU.add, accum_out=cnt[:, b - 1:b]))
            step(v.tensor_copy(e_f, e_raw))
            step.settle()
            dve.sem_inc(dve_to_pe, 1)
            step(v.scalar_tensor_tensor(out=e_f[:, 1], in0=e_f[:, 1], scalar=float(R), in1=e_f[:, 2], op0=ALU.mult, op1=ALU.add))
            dve.wait_ge(pe_to_dve, 2)
            fcol, fint = carry[0:NT - 1, 0:1], carry[0:NT - 1, 1:2].bitcast(I32)
            step(v.tensor_copy(fint, psum[0:NT - 1, 0, 0:1]))
            step.settle()
            step(v.tensor_scalar(fint, fint, 7, None, ALU.arith_shift_right))
            step.settle()
            step(v.tensor_copy(fcol, fint))
            step.settle()
            step(v.scalar_tensor_tensor(out=fcol, in0=fcol, scalar=1.0, in1=pcol[0:NT - 1, 0:1], op0=ALU.add, op1=ALU.add))
            step.settle()
            v.tensor_scalar(lt[0:NT - 1, :], t_it[0:NT - 1, :], fcol, None, ALU.is_ge).then_inc(dve_to_pe, 1)
            dve.wait_ge(pe_to_dve, 3)
            step(v.tensor_copy(blk[:], psum[0:1, 1, 0:IT]))
            step(v.tensor_copy(lt, psum[:, 1, 0:IT]))
            step.settle()
            step(v.tensor_tensor(t_it, t_it, lt, ALU.subtract))
            step.settle()
            for c in range(TC):
                step(v.tensor_scalar(spread[:, c], t_it, pcol[:, c:c + 1], None, ALU.is_equal))
            step.settle()
            dve.sem_inc(dve_to_pe, 1)
            def spread_of(mean, dev, out_stats):
                m0, m1, s0, s1 = (out_stats[:, :, c] for c in (1, 4, 2, 5))
                step(v.tensor_tensor(mean, m0, m1, ALU.add))
                step(v.tensor_tensor(stx[:, 3], m0, m1, ALU.subtract))
                step(v.tensor_tensor(dev, s0, s1, ALU.add))
                step.settle()
                step(v.tensor_scalar(mean, mean, 0.5, None, ALU.mult))
                step(v.tensor_tensor(stx[:, 3], stx[:, 3], stx[:, 3], ALU.mult))
                step(v.tensor_scalar(dev, dev, 1.0 / D, LN_EPS, ALU.mult, ALU.add))
                step.settle()
                step(v.scalar_tensor_tensor(out=dev, in0=stx[:, 3], scalar=0.25, in1=dev, op0=ALU.mult, op1=ALU.add))
                step.settle()

            def tile_of(t, j):
                return t[:, bass.ds(j, 1), :].rearrange("p a d -> p (a d)")

            def all_stats(to, t):
                with dve.Fori(0, NT // 5) as turn:
                    step.enter(turn, 5)
                    for n in range(5):
                        step(v.bn_stats(tile_of(to, 5 * turn + n), tile_of(t, 5 * turn + n)))
                    step.leave(NT // 5)
                step.settle()

            dve.wait_ge(in_x, 32)
            all_stats(stats, x_sb)
            spread_of(stx[:, 0], stx[:, 1], stats)
            dve.sem_inc(dve_to_act, 1)
            dve.wait_ge(act_to_dve, 1)
            step(v.reciprocal(stx[:, 2], stx[:, 1]))
            step.settle()

            dve.wait_ge(pe_to_dve, 4)
            step(v.tensor_copy(idx_i[:], psum[:, 3, 0:IT]))
            step(v.scalar_tensor_tensor(out=dl[:], in0=lt, scalar=float(-P), in1=psum[:, 2, 0:IT], op0=ALU.mult, op1=ALU.add))
            step.settle()
            step(v.tensor_scalar(typ_i, idx_i[:], R - 1, None, ALU.bitwise_and))
            step.settle()
            step(v.tensor_copy(typ, typ_i))
            dve.wait_ge(wa_made, 1)
            for m in range(KC):
                step(v.tensor_copy(wa_sb[:, m].rearrange("p (w r h) -> p w r h", w=2, r=R),
                                   psum[:, 5, m * 2 * R * H:(m + 1) * 2 * R * H].rearrange("p (r w h) -> p w r h", w=2, r=R)))
            step.settle()
            dve.sem_inc(items_ready, 1)
            dve.sem_inc(dve_to_pe, 1)

            def normalise(j, par):
                dve.wait_ge(xt_made, j + 1)
                v.tensor_scalar(xn_ring[:, par], x_sb[:, bass.ds(j, 1), :].rearrange("p a d -> p (a d)"),
                                stx[:, 0, bass.ds(j, 1)], stx[:, 2, bass.ds(j, 1)],
                                ALU.subtract, ALU.mult).then_inc(xn_made, 1)

            def copy_stab(j, par):
                dve.wait_ge(stab_made, j + 3)
                step(v.tensor_copy(s_out[:, bass.ds(j, 1), :].rearrange("p a s -> p (a s)"), psum[:, par, 0:R * H]))
                v.tensor_copy(s_dtab[:, bass.ds(j, 1), :].rearrange("p a s -> p (a s)"),
                              psum[:, par, R * H:2 * R * H]).then_inc(stab_copied, 1)

            normalise(0, 0)
            normalise(1, 1)
            with dve.Fori(0, NT // 2 - 1) as turn:
                step.enter(turn, 2)
                normalise(2 * turn + 2, 0)
                copy_stab(2 * turn, 0)
                normalise(2 * turn + 3, 1)
                copy_stab(2 * turn + 1, 1)
                step.leave(NT // 2 - 1)
            normalise(NT - 1, 0)
            for j in range(NT - 3, NT):
                copy_stab(j, j % 2)
            step.settle()

            dve.wait_ge(in_misc, 16 * 3)
            dve.wait_ge(xt_made, NT + 2)
            step(v.tensor_copy(bdm.rearrange("p (h d) -> p h d", d=DH), hmask[:, 0, 0:P // DH].unsqueeze(2).broadcast_to([P, P // DH, DH])))
            step.settle()

            dve.wait_ge(dlT_made, 1)
            full = IT // P
            step(v.tensor_copy(dl_rows[:, 0:full], psum[:, 2, 0:full * P].rearrange("p (c n) -> p c n", c=full)))
            step(v.tensor_copy(dl_rows[0:IT - full * P, full], psum[0:IT - full * P, 2, full * P:(full + 1) * P]))
            step.settle()
            dve.sem_inc(dlT_copied, 1)

            left = s_dtab
            for n in range(3):
                step(v.tensor_copy(s_parts[:, :, n, :], left))
                step.settle()
                if n < 2:
                    step(v.tensor_tensor(s_rest, left, s_parts[:, :, n, :], ALU.subtract))
                    step.settle()
                left = s_rest

            step.settle()
            dve.sem_inc(parts_made, 1)

            def kv_q(j, par):
                dve.wait_ge(kv_made, j + 1)
                step.settle()
                step(v.tensor_scalar(k_low, psum[:, 4, 0:D], 0.0, None, ALU.min))
                dve.wait_ge(q_made, j + 1)
                v.tensor_scalar(q_low, psum[:, 5, 0:D].rearrange("p (a n) -> p a n", a=KC), 0.0, None, ALU.min).then_inc(low_ready, 1)
                dve.wait_ge(ctx_added, j + 1)
                step(v.tensor_copy(kv_sb[:, par, D:2 * D], psum[:, 4, D:2 * D]))
                dve.wait_ge(exp_ready, j + 1)
                step.settle()
                v.scalar_tensor_tensor(out=kv_sb[:, par, 0:D], in0=psum[:, 4, 0:D], scalar=0.0, in1=k_low,
                                       op0=ALU.max, op1=ALU.add).then_inc(kv_ready, 1)
                step(v.scalar_tensor_tensor(out=qT[:, :, bass.ds(j * P, P)], in0=psum[:, 5, 0:D].rearrange("p (a n) -> p a n", a=KC),
                                            scalar=0.0, in1=q_low, op0=ALU.max, op1=ALU.add))
                step.settle()
                dve.sem_inc(q_read, 1)
                step(v.tensor_tensor(tile_of(x_sb, j), tile_of(x_sb, j), bproj_b[:, 0:D], ALU.add))

            with dve.Fori(0, NT // 2) as turn:
                step.enter(turn, 8)
                kv_q(2 * turn, 0)
                kv_q(2 * turn + 1, 1)
                step.leave(NT // 2)
            kv_q(NT - 1, 0)

            dve.wait_ge(ctx_added, NT + 2)
            for a in range(KC):
                step(v.tensor_tensor(ctxT[:, a], psum[:, 6, a * P:(a + 1) * P], bdm, ALU.mult))
                step(v.tensor_scalar(kb_sb[:, a], bdm, psum[:, 6, D + a:D + a + 1], None, ALU.mult))
            step.settle()
            dve.sem_inc(dve_to_pe, 1)

            def one_hot(i, par, turn):
                dve.wait_ge(dl_in[par], 16 * (turn + 1))
                dve.wait_ge(spread_made, i + 1)
                v.tensor_scalar(ohT[:, par], dl_b[:, par], pcol[:, 0:1], None, ALU.is_equal).then_inc(ohT_made, 1)

            one_hot(0, 0, 0)
            one_hot(1, 1, 0)
            dve.wait_ge(pe_to_dve, 5)
            step(v.tensor_copy(m_sb, psum[:, 7].rearrange("p (a o) -> p a o", a=KC)))
            step.settle()
            dve.sem_inc(dve_to_pe, 1)

            def divide_q(j, par):
                dve.wait_ge(den_made, j + 1)
                dve.wait_ge(mix_made, j + 1)
                step(v.tensor_scalar(q_inv[:, par], psum[:, 2 + par, 0:D].rearrange("p (a n) -> p a n", a=KC), 1e-6, None, ALU.max))
                step.settle()
                step(v.reciprocal(q_inv[:, par], q_inv[:, par]))
                step.settle()
                v.tensor_tensor(qr[:, par], qT[:, :, bass.ds(j * P, P)], q_inv[:, par], ALU.mult).then_inc(qr_made, 1)

            def add_mix(j, par):
                xj = tile_of(x_sb, j)
                dve.wait_ge(mix_made, j + 3)
                v.tensor_tensor(xj, xj, psum[:, par, 0:D], ALU.add).then_inc(mix_added, 1)

            def pick_relation(i, par):
                dve.wait_ge(spread_made, i + 3)
                step.settle()
                step(v.tensor_tensor(tmp_s.rearrange("p k (r h) -> p k r h", r=R),
                                     psum[:, 4 + 2 * par:6 + 2 * par, :].rearrange("p b (k r h) -> p (b k) r h", r=R, h=H),
                                     rmask[:, bass.ds(i * G, G), :].unsqueeze(3).broadcast_to([P, G, R, H]), ALU.mult))
                step.settle()
                step(v.tensor_reduce(s_dst[:, bass.ds(i * G, G), :], tmp_s.rearrange("p k (r h) -> p k h r", r=R), AX, ALU.add))
                step.settle()
                dve.sem_inc(spread_used, 1)

            step(v.tensor_tensor(rmask, typ.unsqueeze(2).broadcast_to([P, IT, R]),
                                 iota_r[:, 0:R].unsqueeze(1).broadcast_to([P, IT, R]), ALU.is_equal))
            divide_q(0, 0)
            with dve.Fori(0, NT // 2) as turn:
                step.enter(turn, 8)
                for par in range(2):
                    divide_q(2 * turn + par + 1, 1 - par)
                    pick_relation(2 * turn + par, par)
                    one_hot(2 * turn + par + 2, par, turn + 1)
                    add_mix(2 * turn + par, par)
                step.leave(NT // 2)
            pick_relation(NG - 2, 0)
            add_mix(NT - 1, 0)
            pick_relation(NG - 1, 1)

            for par in range(2):
                dve.wait_ge(s_src_in[par], 16 * IT // 2)
            step(v.tensor_tensor(s_all.rearrange("p h c j -> p h (c j)"), s_src.rearrange("p i h -> p h i"),
                                 s_dst.rearrange("p i h -> p h i"), ALU.add))
            step.settle()
            dve.sem_inc(dve_to_pe, 1)
            step(v.tensor_copy(d_all.rearrange("p h c j -> p h (c j)"), dl[:].unsqueeze(1).broadcast_to([P, H, IT])))
            step.settle()
            dve.sem_inc(dve_to_pe, 1)

            def ask_pe(n):
                step.settle()
                dve.sem_inc(dve_to_pe, 1)
                dve.wait_ge(pe_to_dve, n)

            NB = -(-J // 4)
            for b in range(NB):
                dve.wait_ge(tr_copied, b + 1)
                part = score[:, 4 * b * P:min(4 * b + 4, J) * P]
                step(v.scalar_tensor_tensor(out=part, in0=part, scalar=0.2, in1=part, op0=ALU.mult, op1=ALU.max))
            for b in range(NB):
                dve.wait_ge(tr_copied, NB + b + 1)
                lo, hi = max(4 * b * P, 1), min(4 * b + 4, J) * P
                step(v.tensor_tensor(keep[:, lo:hi], sc2[:, lo:hi], sc2[:, lo - 1:hi - 1], ALU.is_equal))
            ask_pe(6)
            step(v.tensor_reduce(carry[:, 0:1], ident.rearrange("p (h c) -> p c h", h=H)[:, 0, :], AX, ALU.add))
            step(v.tensor_tensor(keep[:, 0:1], sc2[:, 0:1], psum[:, 0, 0:1], ALU.is_equal))
            step.settle()
            step(v.tensor_scalar(carry[:, 0:1], carry[:, 0:1], -1.0, 1.0, ALU.mult, ALU.add))
            step.settle()
            step(v.tensor_tensor(keep[:, 0:1], keep[:, 0:1], carry[:, 0:1], ALU.mult))
            ask_pe(7)
            step(v.tensor_copy(keep[:, L:L + 1], psum[:, 1, 0:1]))
            step.settle()
            step(v.tensor_reduce(carry[:, 0:1], keep[:, 1:L], AX, ALU.min))
            step.settle()
            step(v.tensor_tensor(carry[:, 1:2], carry[:, 0:1], keep[:, 0:1], ALU.min))
            step(v.tensor_tensor(carry[:, 2:3], carry[:, 0:1], keep[:, L:L + 1], ALU.min))
            step(v.memset(rows[0:1, 3, :], 0.0))
            ask_pe(8)
            step(v.tensor_copy(rows[0:1, 0:2, 0:P], psum[0:1, 2, 0:2 * P].rearrange("p (a n) -> p a n", a=2)))
            step.settle()

            def scan(out_, data, op, back, answer):
                flip = slice(None, None, -1) if back else slice(None)
                kp = keep[:, 1:L + 1] if back else keep[:, 0:L]
                args = kp[:, flip], data[:, flip]
                step(v.tensor_tensor_scan(out_[:, flip], *args, 0.0, ALU.mult, op))
                step.settle()
                end = 0 if back else L - 1
                step(v.tensor_copy(carry[:, 0:1], out_[:, end:end + 1]))
                ask_pe(answer)
                step(v.tensor_copy(rows[0:1, 2, 0:P], psum[0:1, 3, 0:P]))
                step.settle()
                to = rows[0:1, 3, 0:P] if back else rows[0:1, 3, 1:P + 1]
                edge = rows[0:1, 3, P:P + 1] if back else rows[0:1, 3, 0:1]
                step(v.memset(edge, 0.0))
                step(v.tensor_tensor_scan(to[:, flip], rows[0:1, 1 if back else 0, 0:P][:, flip],
                                          rows[0:1, 2, 0:P][:, flip], 0.0, ALU.mult, op))
                ask_pe(answer + 1)
                step(v.tensor_copy(carry[:, 3:4], psum[:, 4, 0:1]))
                step.settle()
                step(v.tensor_tensor_scan(out_[:, flip], *args, carry[:, 3:4], ALU.mult, op))
                step.settle()

            dve.wait_ge(tr_copied, 2 * NB)
            scan(sc1, score, ALU.max, False, 9)
            scan(sc2, sc1, ALU.max, True, 11)
            for b in range(NB):
                part = slice(4 * b * P, min(4 * b + 4, J) * P)
                v.tensor_tensor(score[:, part], score[:, part], sc2[:, part], ALU.subtract).then_inc(shifted, 1)
            dve.wait_ge(act_to_dve, 2)
            scan(sc1, score, ALU.add, False, 13)
            scan(sc2, sc1, ALU.max, True, 15)
            step(v.tensor_scalar(sc2, sc2, 1e-12, None, ALU.add))
            step.settle()
            for b in range(NB):
                part = slice(4 * b * P, min(4 * b + 4, J) * P)
                step(v.reciprocal(sc2[:, part], sc2[:, part]))
                step.settle()
                v.tensor_tensor(score[:, part], score[:, part], sc2[:, part], ALU.mult).then_inc(weights_made, 1)
            dve.wait_ge(tr_copied, 3 * NB)
            step.settle()
            dve.sem_inc(scans_done, 1)

            def one_hot_b(i, q):
                step(v.tensor_tensor(oh_b[:, 4 * q:4 * q + 4], dl[:, bass.ds(i * G + 4 * q, 4)].unsqueeze(2).broadcast_to([P, 4, P]),
                                     iota_r[:].unsqueeze(1).broadcast_to([P, 4, P]), ALU.is_equal))

            def weigh(i, par, k):
                part = ring[:, par, k:k + 2].rearrange("p k (h d) -> p (k h) d", d=DH)
                wts = w_i.rearrange("p c j h -> p (c j h)")[:, bass.ds((i * G + k) * H, 2 * H)]
                return v.tensor_tensor(part, part, wts.unsqueeze(2).broadcast_to([P, 2 * H, DH]), ALU.mult)

            def add(blocks, k):
                a = tile_of(x_sb, blocks[k])
                return v.tensor_tensor(a, a, psum[:, k // 2, (k % 2) * D:(k % 2 + 1) * D], ALU.add)

            def quarter(i, par, turn, q, blocks):
                dve.wait_ge(sum_made, 4 * i + q + 17)
                if blocks:
                    if not (isinstance(i, int) and i == 1 and q == 0):
                        dve.wait_ge(sum_added, 4 * (i - 1) + q + 4)
                    step(add(blocks, 4 * q))
                one_hot_b(i, q)
                if blocks:
                    step.settle(1)
                    step(add(blocks, 4 * q + 1))
                dve.wait_ge(rows_in[par][q], 16 * (G // 4) * (turn + 1))
                step(weigh(i, par, 4 * q))
                if blocks:
                    step.settle(1)
                    step(add(blocks, 4 * q + 2))
                weigh(i, par, 4 * q + 2).then_inc(msg_made, 1)
                if blocks:
                    step.settle()
                    add(blocks, 4 * q + 3).then_inc(sum_added, 1)

            def group(i, par, turn):
                blocks = load_values(ENG.DVE, blk[0:1, bass.ds((i - 1) * G, G)], NT - 1)
                for q in range(4):
                    quarter(i, par, turn, q, blocks)

            for q in range(4):
                quarter(0, 0, 0, q, None)
            with dve.Fori(0, (NG - 1) // RING) as turn:
                step.enter(turn, 20 * RING)
                for n in range(RING):
                    group(RING * turn + n + 1, (n + 1) % RING, turn + (n + 1) // RING)
                step.leave((NG - 1) // RING)
            for i in range((NG - 1) // RING * RING + 1, NG):
                group(i, i % RING, i // RING)
            blocks = load_values(ENG.DVE, blk[0:1, (NG - 1) * G:NG * G], NT - 1)
            dve.wait_ge(sum_added, 4 * (NG - 1) + 4)
            for k in range(G):
                if k % 4 == 0:
                    dve.wait_ge(sum_made, 4 * (NG - 1) + k // 4 + 21)
                for half in range(2):
                    cols = slice(half * P, (half + 1) * P)
                    a = tile_of(x_sb, blocks[k])[:, cols]
                    if k:
                        step.settle(1)
                    step(v.tensor_tensor(a, a, psum[:, k // 2, (k % 2) * D + half * P:(k % 2) * D + (half + 1) * P], ALU.add))
            step.settle()
            dve.sem_inc(x1_ready, 1)

            all_stats(stats_z, x_sb)

            spread_of(stx[:, 0], stx[:, 1], stats_z)
            dve.sem_inc(dve_to_act, 1)
            dve.wait_ge(act_to_dve, 3)
            step(v.reciprocal(stx[:, 2], stx[:, 1]))
            step.settle()

            def norm_y(j, par):
                dve.wait_ge(yT_made, j + 1)
                dve.wait_ge(xs_copied, j + 1)
                step.settle()
                v.tensor_scalar(y_ring[:, par], tile_of(x_sb, j), stx[:, 0, bass.ds(j, 1)], stx[:, 2, bass.ds(j, 1)],
                                ALU.subtract, ALU.mult).then_inc(yr_made, 1)

            def y_stats(j, par):
                dve.wait_ge(yr_made, j + 1)
                step(v.bn_stats(tile_of(stats_z, j), y_ring[:, par]))

            norm_y(0, 0)
            with dve.Fori(0, NT // 2) as turn:
                step.enter(turn, 2)
                norm_y(2 * turn + 1, 1)
                y_stats(2 * turn, 0)
                norm_y(2 * turn + 2, 0)
                y_stats(2 * turn + 1, 1)
                step.leave(NT // 2)
            y_stats(NT - 1, 0)
            step.settle()
            spread_of(stx[:, 0], stx[:, 1], stats_z)
            dve.sem_inc(dve_to_act, 1)
            dve.wait_ge(act_to_dve, 4)
            step(v.reciprocal(stx[:, 2], stx[:, 1]))
            step.settle()
            dve.wait_ge(xs_copied, NT + 2)
            step(v.scalar_tensor_tensor(out=stx[:, 3], in0=stx[:, 0], scalar=-1.0, in1=stx[:, 2], op0=ALU.mult, op1=ALU.mult))
            step.settle()
            dve.sem_inc(dve_to_act, 1)

            def by_x(t):
                return t.rearrange("p (t x) -> p t x", x=X)

            def over_x(t):
                return t.unsqueeze(2).broadcast_to([P, NT, X])

            def x_row(t):
                return t.unsqueeze(1).broadcast_to([P, NT, X])

            pr, o1, o2, tmp, osum, tot, incl, rank, msk = rt
            mx, sm, p1, p2, w1c, w2c, f1, f2, cx, ntx, cumx = small[:11]
            dve.wait_ge(pe_to_dve, 17)
            step(v.tensor_tensor(by_x(pr), by_x(psum[:, 3, 0:NT * X]), x_row(br_sb), ALU.add))
            step.settle()
            step(v.tensor_reduce(mx, by_x(pr), AX, ALU.max))
            step.settle()
            step(v.tensor_tensor(by_x(pr), by_x(pr), over_x(mx), ALU.subtract))
            step.settle()
            dve.sem_inc(dve_to_act, 1)
            dve.wait_ge(act_to_dve, 5)
            step(v.tensor_reduce(sm, by_x(pr), AX, ALU.add))
            step.settle()
            step(v.reciprocal(sm, sm))
            step(v.tensor_scalar(mx[:, 0:X], iota_r[:, 0:X], -1.0, float(X), ALU.mult, ALU.add))
            step.settle()
            step(v.tensor_tensor(by_x(pr), by_x(pr), over_x(sm), ALU.mult))
            step.settle()

            def top(one_hot_, best):
                step(v.tensor_reduce(best, by_x(pr), AX, ALU.max))
                step.settle()
                step(v.tensor_tensor(by_x(tmp), by_x(pr), over_x(best), ALU.is_equal))
                step.settle()
                step(v.tensor_tensor(by_x(tmp), by_x(tmp), x_row(mx[:, 0:X]), ALU.mult))
                step.settle()
                step(v.tensor_reduce(f1, by_x(tmp), AX, ALU.max))
                step.settle()
                step(v.tensor_tensor(by_x(one_hot_), by_x(tmp), over_x(f1), ALU.is_equal))
                step.settle()

            top(o1, p1)
            step(v.scalar_tensor_tensor(out=pr, in0=o1, scalar=-4.0, in1=pr, op0=ALU.mult, op1=ALU.add))
            step.settle()
            top(o2, p2)
            step(v.tensor_tensor(f1, p1, p2, ALU.add))
            step.settle()
            step(v.reciprocal(f1, f1))
            step.settle()
            step(v.tensor_tensor(w1c, p1, f1, ALU.mult))
            step(v.tensor_tensor(w2c, p2, f1, ALU.mult))
            step(v.tensor_scalar(f2[:, 0:1], pcol[:, 0:1], float(LASTN), None, ALU.is_lt))
            step.settle()
            for o in (o1, o2):
                step(v.tensor_scalar(o[:, (NT - 1) * X:], o[:, (NT - 1) * X:], f2[:, 0:1], None, ALU.mult))
            step.settle()
            by_t = "p (x t) -> p t x"
            step(v.tensor_tensor(osum.rearrange(by_t, x=X), by_x(o1), by_x(o2), ALU.add))
            step(v.tensor_scalar(upper, iota_r[:], pcol[:, 0:1], None, ALU.is_gt))
            step(v.memset(msk, 1.0))
            step.settle()
            step(v.memset(msk.rearrange("p (x t) -> p x t", x=X)[:, :, 0], 0.0))
            ask_pe(18)
            step(v.tensor_copy(tot, psum[:, 5, 0:NT * X]))
            step.settle()
            step(v.tensor_tensor_scan(incl, msk, tot, 0.0, ALU.mult, ALU.add))
            step.settle()
            step(v.tensor_copy(cx[:, 0:X], incl.rearrange("p (x t) -> p x t", x=X)[:, :, NT - 1]))
            step(v.tensor_tensor(rank, incl, tot, ALU.subtract))
            step.settle()
            step(v.tensor_tensor(rank, rank, psum[:, 4, 0:NT * X], ALU.add))
            step.settle()
            step(v.scalar_tensor_tensor(out=rank.rearrange("p (x t) -> p x t", x=X),
                                        in0=iota_r[:, 0:X].unsqueeze(2).broadcast_to([P, X, NT]), scalar=float(XR),
                                        in1=rank.rearrange("p (x t) -> p x t", x=X), op0=ALU.mult, op1=ALU.add))
            step.settle()
            for o, slot in ((o1, slot_u[0]), (o2, slot_u[1])):
                step(v.tensor_tensor(by_x(tmp), by_x(o), rank.rearrange(by_t, x=X), ALU.mult))
                step.settle()
                step(v.tensor_reduce(f1, by_x(tmp), AX, ALU.add))
                step.settle()
                step(v.tensor_copy(slot, f1))
                step.settle()
            step(v.scalar_tensor_tensor(out=f1[:, 0:X], in0=iota_r[:, 0:X], scalar=float(XR), in1=cx[:, 0:X], op0=ALU.mult, op1=ALU.add))
            step.settle()
            step(v.tensor_copy(ftab[:, 2 * FT:2 * FT + X], f1[0:1, 0:X]))
            step(v.memset(xs_pad, 0.0))
            step(v.memset(xs[:, :, D + 2:XW], 0.0))
            step(v.tensor_copy(xs[:, :, D], w1c))
            step(v.tensor_scalar(xs[:, :, D + 1], iota_r[:, 0:NT], float(P), pcol[:, 0:1], ALU.mult, ALU.add))
            step.settle()
            step(v.tensor_scalar(xs_pad[:, D + 1:D + 2], pcol[:, 0:1], float(N), None, ALU.add))
            step.settle()
            dve.sem_inc(send_ready, 1)

            nti = f2[0:1, 0:X].bitcast(I32)
            step(v.tensor_scalar(ntx[0:1, 0:X], cx[0:1, 0:X], float(P - 1), None, ALU.add))
            step.settle()
            step(v.tensor_copy(nti, ntx[0:1, 0:X]))
            step.settle()
            step(v.tensor_scalar(nti, nti, 7, None, ALU.arith_shift_right))
            step.settle()
            step(v.tensor_copy(ntx[0:1, 0:X], nti))
            step.settle()
            step(v.tensor_tensor_scan(cumx[0:1, 0:X], ones[0:1, 0:X], ntx[0:1, 0:X], 0.0, ALU.mult, ALU.add))
            step.settle()
            step(v.tensor_tensor(ntx[0:1, 0:X], cumx[0:1, 0:X], ntx[0:1, 0:X], ALU.subtract))
            step.settle()
            step(v.tensor_scalar(ntx[0:1, 0:X], ntx[0:1, 0:X], float(-P), None, ALU.mult))
            step.settle()
            step(v.scalar_tensor_tensor(out=ntx[0:1, 0:X], in0=iota_r[0:1, 0:X], scalar=float(XR), in1=ntx[0:1, 0:X], op0=ALU.mult, op1=ALU.add))
            step.settle()
            step(v.tensor_tensor(sm[0:1, 0:X - 1], ntx[0:1, 1:X], ntx[0:1, 0:X - 1], ALU.subtract))
            ge = at(Z1 + 5 * NT * X, FT, X)[0:1]
            step(v.tensor_tensor(ge, iota_r[0:1, 0:FT].unsqueeze(2).broadcast_to([1, FT, X]),
                                 cumx[0:1, 0:X].unsqueeze(1).broadcast_to([1, FT, X]), ALU.is_ge))
            step.settle()
            et, rw = tmp[0:1, 0:FT], tmp[0:1, FT:2 * FT]
            step(v.tensor_reduce(et, ge[:, :, 0:X - 1], AX, ALU.add))
            step(v.tensor_tensor(gt[0:1], ge[:, :, 0:X - 1],
                                 sm[0:1, 0:X - 1].unsqueeze(1).broadcast_to([1, FT, X - 1]), ALU.mult))
            step.settle()
            step(v.tensor_reduce(rw, gt[0:1], AX, ALU.add))
            step.settle()
            step(v.scalar_tensor_tensor(out=rw, in0=iota_r[0:1, 0:FT], scalar=float(P), in1=rw, op0=ALU.mult, op1=ALU.add))
            step.settle()
            step(v.tensor_scalar(rw, rw, ntx[0:1, 0:1], None, ALU.add))
            step.settle()
            step(v.tensor_scalar(gt[0:1, :, 0], rw, -1.0, float(X * XR), ALU.mult, ALU.add))
            step.settle()
            step(v.tensor_tensor(gt[0:1, :, 0], gt[0:1, :, 0], ge[:, :, X - 1], ALU.mult))
            step.settle()
            step(v.tensor_tensor(rw, rw, gt[0:1, :, 0], ALU.add))
            step.settle()
            step(v.tensor_copy(ftab[:, 0:FT], et))
            step(v.tensor_copy(ftab[:, FT:2 * FT], rw))
            step.settle()
            dve.sem_inc(tiles_ready, 1)
            def add_shift(e):
                dve.wait_ge(w1_used, e + 1)
                dve.wait_ge(b1_in[e % 4], 16 * (e // 4 + 1))
                lo = 0 if e % 2 == 0 else 6
                v.tensor_tensor(b1_row[0:1, e % 4], b1_row[0:1, e % 4], psum[0:1, lo:lo + 2, :].rearrange("p n f -> p (n f)"),
                                ALU.add).then_inc(b1_added, 1)
            for e in range(X - 2):
                add_shift(e)
            dve.wait_ge(sent, 16 * NT)
            step(v.tensor_copy(xs[:, :, D], w2c))
            step.settle()
            dve.sem_inc(send_ready, 1)
            for e in range(X - 2, X):
                add_shift(e)

            def copy_xT(i, par):
                dve.wait_ge(xgT_made, i + 1)
                v.tensor_copy(xgT[:, par], psum[:, 0, 0:D].rearrange("p (a n) -> p a n", a=KC)).then_inc(xgT_copied, 1)

            def add_b1(i, slot, turn):
                dve.wait_ge(xg_in[slot], 48 * (turn + 1))
                for n in range(2):
                    dve.wait_ge(f1_made, 2 * i + n + 1)
                    v.tensor_tensor(h_sb[:, slot % 2, n * 512:(n + 1) * 512], psum[:, 1 + n, :],
                                    bias_r[:, slot, n * 512:(n + 1) * 512], ALU.add).then_inc(h_pre, 1)

            def copy_hT(i, par):
                dve.wait_ge(hT_made, 2 * i + 1)
                v.tensor_copy(hT[:, par, 0:4], psum[:, 3].rearrange("p (c n) -> p c n", c=4)).then_inc(hT_copied, 1)

            def finish(i, slot):
                par = slot % 2
                dve.wait_ge(f2_made, i + 1)
                dve.wait_ge(y_free, i + 1)
                step(v.tensor_tensor(y_b2, psum[:, 5, 0:D], bias_r[:, slot, F:F + D], ALU.add))
                step(v.tensor_copy(tok_u[:, par:par + 1], xg[:, slot, D + 1:D + 2]))
                step.settle()
                v.tensor_scalar(y_out[:, par], y_b2, xg[:, slot, D:D + 1], None, ALU.mult).then_inc(tile_done, 1)
                dve.wait_ge(tile_done, i + 5)

            def turn_of_four(turn, more):
                for n in range(4):
                    copy_hT(4 * turn + n, n % 2)
                    if n < 2 or more:
                        copy_xT(4 * turn + n + 2, n % 2)
                    if n < 3 or more:
                        add_b1(4 * turn + n + 1, (n + 1) % 4, turn + (n + 1) // 4)
                    finish(4 * turn + n, n)

            copy_xT(0, 0)
            copy_xT(1, 1)
            add_b1(0, 0, 0)
            with dve.Fori(0, FT // 4 - 1) as turn:
                step.enter(turn, 8)
                turn_of_four(turn, True)
                step.leave(FT // 4 - 1)
            turn_of_four(FT // 4 - 1, False)

        @block.scalar
        def _(act):
            a_ = nc.scalar
            act.sem_inc(xt_copied, 2)
            act.sem_inc(h_copied, 4)
            for par in range(2):
                act.sem_inc(h_stored[par], 16)
            act.sem_inc(ohT_made, 2)
            act.sem_inc(yT_copied, 2)
            act.sem_inc(xs_copied, 2)

            def root(n):
                act.wait_ge(dve_to_act, n)
                a_.activation(stx[:, 1], stx[:, 1], ACT.Sqrt).then_inc(act_to_dve, 1)

            root(1)

            def copy_xt(j, par):
                act.wait_ge(xt_made, j + 3)
                act.wait_ge(stab_made, j + 1)
                src_ = psum[:, 6 + par, 0:D].rearrange("p (a n) -> p a n", a=KC)
                a_.copy(xs_ring[:, par], src_)
                a_.copy(xnT[:, :, bass.ds(j * P, P)], src_).then_inc(xt_copied, 1)
            pairs(act, NT, copy_xt)

            def copy_xs(j, par):
                act.wait_ge(ctx_added, j + 1)
                a_.copy(xs_ring[:, par], xnT[:, :, bass.ds(j * P, P)]).then_inc(xs_made, 1)

            act.wait_ge(stab_made, NT + 2)
            act.wait_ge(xt_copied, NT + 2)

            def evacuate(j, par, turn, more):
                if more:
                    copy_xs(j + 1, 1 - par)
                act.wait_ge(low_ready, j + 1)
                a_.activation(k_low, k_low, ACT.Exp)
                a_.activation(q_low, q_low, ACT.Exp).then_inc(exp_ready, 1)
                for n in range(4):
                    act.wait_ge(h_made, 4 * j + n + 1)
                    if n == 0:
                        act.wait_ge(h_stored[par], 16 * (turn + 1))
                    a_.copy(h_out[:, par, n * 512:(n + 1) * 512], psum[:, n, :]).then_inc(h_copied, 1)

            copy_xs(0, 0)
            with act.Fori(0, NT // 2) as turn:
                evacuate(2 * turn, 0, turn, True)
                evacuate(2 * turn + 1, 1, turn, True)
            evacuate(NT - 1, 0, NT // 2, False)

            def take_indices(i, par):
                for q in range(4):
                    act.wait_ge(sum_made, 4 * i + q + 1)
                    a_.copy(idx_r[:, par, 4 * q:4 * q + 4], idx_i[:, bass.ds(i * G + 4 * q, 4)]).then_inc(idx_taken, 1)

            for i in range(RING):
                take_indices(i, i)

            NB = -(-J // 4)
            n = 0
            for to in (score, sc2):
                for b in range(NB):
                    width = min(4, J - 4 * b) * P
                    act.wait_ge(tr_made, n + 1)
                    a_.copy(to[:, 4 * b * P:4 * b * P + width], psum[:, n % 8, 0:width]).then_inc(tr_copied, 1)
                    n += 1
            for b in range(NB):
                act.wait_ge(shifted, b + 1)
                part = score[:, 4 * b * P:min(4 * b + 4, J) * P]
                last = a_.activation(part, part, ACT.Exp)
            last.then_inc(act_to_dve, 1)
            for b in range(NB):
                w = min(4, J - 4 * b)
                act.wait_ge(tr_made, n + 1)
                for k in range(w):
                    ins = a_.copy(w_i[:, :, 4 * b + k, :].rearrange("p c h -> p h c"),
                                  psum[:, b % 8, k * P:(k + 1) * P].rearrange("p (h c) -> p h c", h=H))
                ins.then_inc(tr_copied, 1)
                n += 1

            with act.Fori(1, NG // RING) as turn:
                for n in range(RING):
                    take_indices(RING * turn + n, n)
            for i in range(NG // RING * RING, NG):
                take_indices(i, i % RING)

            root(2)

            def copy_y(j, par):
                act.wait_ge(yr_made, j + 1)
                a_.copy(xs[:, bass.ds(j, 1), 0:D].rearrange("p a d -> p (a d)"), y_ring[:, par]).then_inc(xs_copied, 1)
                act.wait_ge(yT_made, j + 3)
                a_.copy(yT[:, par], psum[:, 4 + par, 0:D].rearrange("p (a n) -> p a n", a=KC)).then_inc(yT_copied, 1)
            pairs(act, NT, copy_y)
            root(3)
            act.wait_ge(dve_to_act, 5)
            a_.activation(rt[0], rt[0], ACT.Exp).then_inc(act_to_dve, 1)
            with act.Fori(0, NT // 5) as turn:
                for n in range(5):
                    row = xs[:, bass.ds(5 * turn + n, 1), 0:D].rearrange("p a d -> p (a d)")
                    a_.activation(row, row, ACT.Identity, bias=stx[:, 3, bass.ds(5 * turn + n, 1)],
                                  scale=stx[:, 2, bass.ds(5 * turn + n, 1)]).then_inc(xs_normed, 1)

            act.wait_ge(ln_loaded, 32)
            for e in range(X):
                act.wait_ge(w1_used, e + 1)
                for c in range(KC):
                    a_.mul(w1_sb[:, e, c], w1_sb[:, e, c], ln_cols[:, 0, e, c:c + 1]).then_inc(w1_scaled, 1)

            def gelu(i, par):
                for n in range(2):
                    act.wait_ge(h_pre, 2 * i + n + 1)
                    half = h_sb[:, par, n * 512:(n + 1) * 512]
                    a_.activation(half, half, ACT.Gelu).then_inc(h_act, 1)

            def copy_hT(i, par):
                act.wait_ge(hT_made, 2 * i + 2)
                a_.copy(hT[:, par, 4:8], psum[:, 4].rearrange("p (c n) -> p c n", c=4)).then_inc(hT_copied, 1)

            gelu(0, 0)
            with act.Fori(0, FT // 2 - 1) as turn:
                copy_hT(2 * turn, 0)
                gelu(2 * turn + 1, 1)
                copy_hT(2 * turn + 1, 1)
                gelu(2 * turn + 2, 0)
            copy_hT(FT - 2, 0)
            gelu(FT - 1, 1)
            copy_hT(FT - 1, 1)

        @block.tensor
        def _(pe):
            t_ = nc.tensor
            for s_, n in ((xt_made, 2), (stab_made, 2), (ctx_added, 2), (spread_made, 2),
                          (sum_made, 4 * RING), (mix_made, 2), (yT_made, 2)):
                pe.sem_inc(s_, n)

            def mm(o, lhsT, rhs, first=True, last=True, **kw):
                return t_.matmul(o, lhsT, rhs, start=first, stop=last, **kw)

            pe.wait_ge(dve_to_pe, 1)
            pe.wait_ge(in_wrel, 16)

            def through_weights(m):
                for r in range(R):
                    for c in range(KC):
                        lo = m * 2 * R * H + r * 2 * H
                        last = mm(psum[:, 5, lo:lo + 2 * H], wrel_sb[:, r, c, m * P:(m + 1) * P], ablock[:, c], c == 0, c == KC - 1)
                return last
            through_weights(0).then_inc(pe_to_dve, 1)

            pe.wait_ge(dve_to_pe, 2)
            mm(psum[0:NT - 1, 0, 0:1], cnt[:, 0:NT - 1], ones[:, 0:1]).then_inc(pe_to_dve, 1)
            pe.wait_ge(dve_to_pe, 3)
            mm(psum[:, 1, 0:IT], ones[0:NT - 1, :], lt[0:NT - 1, :]).then_inc(pe_to_dve, 1)
            pe.wait_ge(dve_to_pe, 4)
            for n, bank in ((0, 2), (1, 3)):
                for c in range(TC):
                    last = mm(psum[:, bank, 0:IT], e_f[:, n, c, :], spread[:, c], c == 0, c == TC - 1)
            last.then_inc(pe_to_dve, 1)

            through_weights(1).then_inc(wa_made, 1)

            pe.wait_ge(pool_const, 1)
            pe.wait_ge(dve_to_pe, 5)

            def turn_x(j, par):
                pe.wait_ge(xn_made, j + 1)
                pe.wait_ge(xt_copied, j + 1)
                for a in range(KC):
                    last = t_.transpose(psum[:, 6 + par, a * P:(a + 1) * P], xn_ring[:, par, a * P:(a + 1) * P], ident)
                last.then_inc(xt_made, 1)

            def scores(j, par):
                pe.wait_ge(xt_copied, j + 3)
                pe.wait_ge(stab_copied, j + 1)
                for c in range(KC):
                    last = mm(psum[:, par, 0:2 * R * H], xs_ring[:, par, c], wa_sb[:, c], c == 0, c == KC - 1)
                last.then_inc(stab_made, 1)

            turn_x(0, 0)
            with pe.Fori(0, NT // 2) as turn:
                turn_x(2 * turn + 1, 1)
                scores(2 * turn, 0)
                turn_x(2 * turn + 2, 0)
                scores(2 * turn + 1, 1)
            scores(NT - 1, 0)

            for c in range(-(-IT // P)):
                n = min(P, IT - c * P)
                last = t_.transpose(psum[0:n, 2, c * P:(c + 1) * P], dl[:, c * P:c * P + n], ident)
            last.then_inc(dlT_made, 1)

            pe.wait_ge(dlT_copied, 1)
            pe.wait_ge(stab_copied, NT + 2)
            pe.wait_ge(in_wt, 48)
            mm(psum[:, 6, :], zrow[0:1, 0:P], zrow[0:1, :], skip_group_check=True)

            def node_tile(j, par, rows_=P):
                pe.wait_ge(xs_made, j + 1)
                xt = xs_ring[:, par]
                pe.wait_ge(kv_ready, j + 1)
                pe.wait_ge(q_read, j + 1)
                for c in range(KC):
                    last = mm(psum[:, 4, :], xt[:, c], wmix_sb[:, c, 0:2 * D], c == 0, c == KC - 1)
                last.then_inc(kv_made, 1)
                for a in range(KC):
                    for c in range(KC):
                        last = mm(psum[:, 5, a * P:(a + 1) * P], wmix_sb[:, c, 2 * D + a * P:2 * D + (a + 1) * P], xt[:, c], c == 0, c == KC - 1)
                last.then_inc(q_made, 1)
                for n in range(4):
                    pe.wait_ge(h_copied, 4 * j + n + 1)
                    for c in range(KC):
                        last = mm(psum[:, n, :], xt[:, c], wrt_sb[:, c, n * 512:(n + 1) * 512], c == 0, c == KC - 1)
                    last.then_inc(h_made, 1)
                pe.wait_ge(kv_ready, j + 2)
                for a in range(KC):
                    k_a, v_a = kv_sb[0:rows_, par, a * P:(a + 1) * P], kv_sb[0:rows_, par, D + a * P:D + (a + 1) * P]
                    mm(psum[:, 6, a * P:(a + 1) * P], v_a, k_a, False, False, skip_group_check=True)
                    last = mm(psum[:, 6, D + a:D + a + 1], k_a, ones[0:rows_, 0:1], False, False, skip_group_check=True)
                last.then_inc(ctx_added, 1)

            with pe.Fori(0, NT // 2) as turn:
                node_tile(2 * turn, 0)
                node_tile(2 * turn + 1, 1)
            node_tile(NT - 1, 0, LASTN)

            pe.wait_ge(dve_to_pe, 6)
            for a in range(KC):
                last = mm(psum[:, 7, a * D:(a + 1) * D], ctxT[:, a], wp_sb[:, a])
            last.then_inc(pe_to_dve, 1)

            pe.wait_ge(dve_to_pe, 7)
            pe.wait_ge(h_copied, 4 * NT + 4)

            def denominators(j, par):
                if not isinstance(j, int):
                    pe.wait_ge(qr_made, j)
                for a in range(KC):
                    last = mm(psum[:, 2 + par, a * P:(a + 1) * P], kb_sb[:, a], qT[:, a, bass.ds(j * P, P)])
                last.then_inc(den_made, 1)

            def mix(j, par):
                pe.wait_ge(qr_made, j + 2)
                pe.wait_ge(mix_added, j + 1)
                for a in range(KC):
                    last = mm(psum[:, par, 0:D], qr[:, par, a], m_sb[:, a], a == 0, a == KC - 1)
                last.then_inc(mix_made, 1)

            def spread_scores(i, par, blocks):
                pe.wait_ge(ohT_made, i + 3)
                pe.wait_ge(spread_used, i + 1)
                for k in range(G):
                    for n in range(3):
                        last = mm(psum[:, 4 + 2 * par + k // 8, (k % 8) * 64:(k % 8 + 1) * 64], ohT[:, par, k],
                                  s_parts[:, bass.ds(blocks[k], 1), n, :].rearrange("p a s -> p (a s)"), n == 0, n == 2)
                last.then_inc(spread_made, 1)

            denominators(0, 0)
            with pe.Fori(0, NT // 2) as turn:
                blocks = load_values(ENG.PE, blk[0:1, bass.ds(2 * turn * G, 2 * G)], NT - 1)
                for par in range(2):
                    denominators(2 * turn + par + 1, 1 - par)
                    spread_scores(2 * turn + par, par, blocks[par * G:(par + 1) * G])
                    mix(2 * turn + par, par)
            blocks = load_values(ENG.PE, blk[0:1, (NG - 2) * G:NG * G], NT - 1)
            spread_scores(NG - 2, 0, blocks[0:G])
            mix(NT - 1, 0)
            spread_scores(NG - 1, 1, blocks[G:2 * G])

            NB = -(-J // 4)
            pe.wait_ge(dve_to_pe, 8)
            n = 0
            for table in (s_all, d_all):
                if n:
                    pe.wait_ge(dve_to_pe, 9)
                for b in range(NB):
                    if n >= 8:
                        pe.wait_ge(tr_copied, n - 7)
                    for k in range(min(4, J - 4 * b)):
                        last = t_.transpose(psum[:, n % 8, k * P:(k + 1) * P], table[:, :, :, 4 * b + k].rearrange("p h c -> p (h c)"), ident)
                    last.then_inc(tr_made, 1)
                    n += 1
            pe.wait_ge(dve_to_pe, 10)
            mm(psum[:, 0, 0:1], shift_up, sc2[:, L - 1:L]).then_inc(pe_to_dve, 1)
            pe.wait_ge(dve_to_pe, 11)
            mm(psum[:, 1, 0:1], shift_down, keep[:, 0:1]).then_inc(pe_to_dve, 1)
            pe.wait_ge(dve_to_pe, 12)
            mm(psum[0:1, 2, 0:P], carry[:, 1:2], ident)
            mm(psum[0:1, 2, P:2 * P], carry[:, 2:3], ident).then_inc(pe_to_dve, 1)
            asked = 12
            for back in (0, 1, 0, 1):
                pe.wait_ge(dve_to_pe, asked + 1)
                mm(psum[0:1, 3, 0:P], carry[:, 0:1], ident).then_inc(pe_to_dve, 1)
                pe.wait_ge(dve_to_pe, asked + 2)
                mm(psum[:, 4, 0:1], rows[0:1, 3, back:back + P], ones[0:1, 0:1]).then_inc(pe_to_dve, 1)
                asked += 2
            for b in range(NB):
                pe.wait_ge(weights_made, b + 1)
                for k in range(min(4, J - 4 * b)):
                    last = t_.transpose(psum[:, b % 8, k * P:(k + 1) * P], score[:, (4 * b + k) * P:(4 * b + k + 1) * P], ident)
                last.then_inc(tr_made, 1)
            pe.wait_ge(tr_copied, 3 * NB)

            def sum_rows(i, par):
                for q in range(4):
                    pe.wait_ge(msg_made, 4 * i + q + 1)
                    pe.wait_ge(sum_added, 4 * i + q + 1)
                    for k in range(4 * q, 4 * q + 4):
                        last = mm(psum[:, k // 2, (k % 2) * D:(k % 2 + 1) * D], oh_b[:, k], ring[:, par, k])
                    last.then_inc(sum_made, 1)
            with pe.Fori(0, NG // RING) as turn:
                for n in range(RING):
                    sum_rows(RING * turn + n, n)
            for i in range(NG // RING * RING, NG):
                sum_rows(i, i % RING)

            def turn_y(j, par):
                pe.wait_ge(yr_made, j + 1)
                pe.wait_ge(yT_copied, j + 1)
                for a in range(KC):
                    last = t_.transpose(psum[:, 4 + par, a * P:(a + 1) * P], y_ring[:, par, a * P:(a + 1) * P], ident)
                last.then_inc(yT_made, 1)

            def logits(j, par):
                pe.wait_ge(yT_copied, j + 3)
                for c in range(KC):
                    last = mm(psum[:, 3, bass.ds(j * X, X)], yT[:, par, c], wr_sb[:, c], c == 0, c == KC - 1)
                return last

            turn_y(0, 0)
            with pe.Fori(0, NT // 2) as turn:
                turn_y(2 * turn + 1, 1)
                logits(2 * turn, 0)
                turn_y(2 * turn + 2, 0)
                logits(2 * turn + 1, 1)
            logits(NT - 1, 0).then_inc(pe_to_dve, 1)
            pe.wait_ge(dve_to_pe, 21)
            mm(psum[:, 4, 0:NT * X], upper, rt[4])
            mm(psum[:, 5, 0:NT * X], ones[:], rt[4]).then_inc(pe_to_dve, 1)

            pe.wait_ge(w1_loaded, 16 * X)
            pe.wait_ge(ln_loaded, 32)
            for e in range(X):
                lo = 0 if e % 2 == 0 else 6
                if e >= 2:
                    pe.wait_ge(b1_added, e - 1)
                for n in range(2):
                    for c in range(KC):
                        last = mm(psum[0:1, lo + n, :], ln_cols[:, 1, e, c:c + 1], w1_sb[:, e, c, n * 512:(n + 1) * 512], c == 0, c == KC - 1)
                last.then_inc(w1_used, 1)

            pe.wait_ge(w1_scaled, KC * X)
            pe.wait_ge(b1_added, X)
            pe.wait_ge(w2_loaded, 16)

            def turn_rows(i, slot, turn):
                pe.wait_ge(xg_in[slot], 48 * (turn + 1))
                if not isinstance(i, int) or i:
                    pe.wait_ge(xgT_copied, i)
                for a in range(KC):
                    last = t_.transpose(psum[:, 0, a * P:(a + 1) * P], xg[:, slot, a * P:(a + 1) * P], ident)
                last.then_inc(xgT_made, 1)

            def hidden(i, par, e_reg):
                pe.wait_ge(xgT_copied, i + 1)
                if not isinstance(i, int) or i:
                    pe.wait_ge(h_pre, 2 * i)
                for n in range(2):
                    for c in range(KC):
                        last = mm(psum[:, 1 + n, :], xgT[:, par, c],
                                  w1_sb[:, bass.ds(e_reg, 1), c, n * 512:(n + 1) * 512].rearrange("p a f -> p (a f)"), c == 0, c == KC - 1)
                    last.then_inc(f1_made, 1)

            def turn_hidden(i, par):
                for n in range(2):
                    pe.wait_ge(h_act, 2 * i + n + 1)
                    for c in range(4):
                        last = t_.transpose(psum[:, 3 + n, c * P:(c + 1) * P], h_sb[:, par, (4 * n + c) * P:(4 * n + c + 1) * P], ident)
                    last.then_inc(hT_made, 1)

            def project(i, par, e_reg):
                pe.wait_ge(hT_copied, 2 * i + 2)
                pe.wait_ge(tile_done, i + 4)
                for c in range(FC):
                    last = mm(psum[:, 5, 0:D], hT[:, par, c], w2_sb[:, bass.ds(e_reg, 1), c, :].rearrange("p a d -> p (a d)"), c == 0, c == FC - 1)
                last.then_inc(f2_made, 1)

            def turn_of_four(turn, more):
                experts = load_values(ENG.PE, ftab[0:1, bass.ds(4 * turn, 4 + more)], X - 1)
                for n in range(4):
                    turn_hidden(4 * turn + n, n % 2)
                    if n < 2 or more:
                        turn_rows(4 * turn + n + 2, (n + 2) % 4, turn + (n + 2) // 4)
                    if n < 3 or more:
                        hidden(4 * turn + n + 1, (n + 1) % 2, experts[n + 1])
                    project(4 * turn + n, n % 2, experts[n])

            pe.wait_ge(tiles_ready, 1)
            first = load_values(ENG.PE, ftab[0:1, 0:1], X - 1)
            turn_rows(0, 0, 0)
            turn_rows(1, 1, 0)
            hidden(0, 0, first[0])
            with pe.Fori(0, FT // 4 - 1) as turn:
                turn_of_four(turn, True)
            turn_of_four(FT // 4 - 1, False)


def kernel(x, src, dst, edge_type_8, L0_gnn_W, L0_gnn_attn_src, L0_gnn_attn_dst, L0_mix_Wq, L0_mix_Wkv,
           L0_mix_Wproj, L0_mix_bproj, L0_ffn_Wr, L0_ffn_br, L0_ffn_ln_g, L0_ffn_ln_b, L0_ffn_W1,
           L0_ffn_b1, L0_ffn_W2, L0_ffn_b2):
    import concourse.bacc as bacc
    from concourse.bass_utils import run_bass_kernel_spmd

    def chunks(a):
        return a.reshape(-1, P, a.shape[-1]).transpose(1, 0, 2)

    w = np.asarray(L0_gnn_W)
    att = np.stack([np.asarray(L0_gnn_attn_src).reshape(-1), np.asarray(L0_gnn_attn_dst).reshape(-1)], 1)
    wkv, wq = np.asarray(L0_mix_Wkv), np.asarray(L0_mix_Wq)
    arrays = {
        "x": np.asarray(x), "src": np.asarray(src), "dst": np.asarray(dst), "etype": np.asarray(edge_type_8),
        "w_rel": w.reshape(R, KC, P, D).transpose(2, 0, 1, 3),
        "w_rel_t": chunks(w.transpose(2, 0, 1).reshape(D, R * D)),
        "attn": chunks(att),
        "wmix_t": chunks(np.concatenate([wkv, wq], 0).T),
        "wp_t": chunks(np.asarray(L0_mix_Wproj).T),
        "bproj": np.asarray(L0_mix_bproj).reshape(1, D),
        "wr": chunks(np.asarray(L0_ffn_Wr)),
        "br": np.asarray(L0_ffn_br).reshape(1, X),
        "ln_g": np.asarray(L0_ffn_ln_g).reshape(X, KC, P).transpose(2, 0, 1),
        "ln_b": np.asarray(L0_ffn_ln_b).reshape(X, KC, P).transpose(2, 0, 1),
        "w1": np.asarray(L0_ffn_W1).reshape(X, KC, P, F).transpose(0, 2, 1, 3).reshape(X, P, KC * F),
        "b1": np.asarray(L0_ffn_b1),
        "w2": np.asarray(L0_ffn_W2).reshape(X, FC, P, D).transpose(2, 0, 1, 3),
        "b2": np.asarray(L0_ffn_b2),
    }
    arrays = {f"in_{k}": np.ascontiguousarray(a) for k, a in arrays.items()}
    nc = bacc.Bacc("TRN2", target_bir_lowering=False, num_devices=1)
    args = [nc.dram_tensor(k, a.shape, mybir.dt.from_np(a.dtype), kind="ExternalInput").ap() for k, a in arrays.items()]
    args.append(nc.dram_tensor("out", [N + P, D], F32, kind="ExternalOutput").ap())
    gps_layer(nc, *args)
    r = run_bass_kernel_spmd(nc, [arrays], core_ids=[0])
    return r.results[0]["out"][0:N]
```
